# Optimizing a Trainium2 kernel written in Bass

```python
import numpy as np
import jax
import jax.numpy as jnp

def _softmax(x, axis=-1):
    return jax.nn.softmax(x, axis=axis)

def _gelu(x):
    return jax.nn.gelu(x, approximate=True)

def _silu(x):
    return jax.nn.silu(x)

def _sigmoid(x):
    return jax.nn.sigmoid(x)

def _layernorm(x, axis=-1, eps=1e-05):
    m = jnp.mean(x, axis=axis, keepdims=True)
    v = jnp.var(x, axis=axis, keepdims=True)
    return (x - m) / jnp.sqrt(v + eps)

def _scatter_add(tgt, idx, src, axis=0):
    return tgt.at[idx].add(src)

def _segment_sum(src, seg, n):
    return jax.ops.segment_sum(src, seg, n)
kernel_name = 'mk_adaln_d2_jaxref_r8_90db15'

def setup_inputs(seed: int=0):
    np.random.seed(seed)
    _w = jnp.asarray

    def _L0_attn_setup():
        import jax, jax.numpy as jnp
        import numpy as np
        import math
        B, T, DIM, NH = (2, 256, 256, 16)
        HD = DIM // NH

        def rotate_half(x):
            h = x.shape[-1] // 2
            return jnp.concatenate([-x[..., h:], x[..., :h]], axis=-1)

        def rope_tables(t_len, rot_dim, base=10000.0, dtype=jnp.float32):
            inv_freq = 1.0 / base ** (jnp.arange(0, rot_dim, 2, dtype=dtype) / rot_dim)
            t = jnp.arange(t_len, dtype=dtype)
            ang = jnp.einsum('i,j->ij', t, inv_freq)
            return (jnp.sin(ang), jnp.cos(ang))

        def apply_rope(q, k, sin, cos):
            h = q.shape[-1] // 2
            q1, q2 = (q[..., :h], q[..., h:])
            k1, k2 = (k[..., :h], k[..., h:])
            sin = sin[None, None]
            cos = cos[None, None]
            q1r = q1 * cos + rotate_half(q1) * sin
            k1r = k1 * cos + rotate_half(k1) * sin
            return (jnp.concatenate([q1r, q2], axis=-1), jnp.concatenate([k1r, k2], axis=-1))
        key = jax.random.key(seed)
        ks = jax.random.split(key, 5)
        s = 1.0 / math.sqrt(DIM)
        return {'x': jax.random.normal(ks[0], (B, T, DIM), jnp.float32), 'wq': jax.random.normal(ks[1], (DIM, DIM), jnp.float32) * s, 'wk': jax.random.normal(ks[2], (DIM, DIM), jnp.float32) * s, 'wv': jax.random.normal(ks[3], (DIM, DIM), jnp.float32) * s, 'wo': jax.random.normal(ks[4], (DIM, DIM), jnp.float32) * s}
    _L0_attn_in = _L0_attn_setup()

    def _L0_ffn_setup():
        import jax, jax.numpy as jnp
        import numpy as np
        B, S, D = (2, 256, 256)
        MOE_D = 176
        E = 16
        K = 6
        ALPHA = 0.001

        def _moe_forward(x, gate_w, w_gate, w_up, w_down):
            b, s, d = x.shape
            T = b * s
            h = x.reshape(T, d)
            logits = h @ gate_w.T
            scores = jax.nn.softmax(logits.astype(jnp.float32), axis=-1)
            topk_w, topk_idx = jax.lax.top_k(scores, K)
            cw = jnp.zeros((T, E), jnp.float32)
            cw = cw.at[jnp.arange(T)[:, None], topk_idx].add(topk_w)
            y = jnp.zeros((T, d), x.dtype)
            for e in range(E):
                g = h @ w_gate[e].T
                u = h @ w_up[e].T
                out = jax.nn.silu(g) * u @ w_down[e].T
                y = y + cw[:, e:e + 1].astype(x.dtype) * out
            counts = jnp.sum(jax.nn.one_hot(topk_idx.reshape(b, s * K), E, dtype=jnp.float32), axis=1)
            ce = counts * (E / (s * K))
            scores_bse = scores.reshape(b, s, E)
            aux = jnp.mean(jnp.sum(ce * scores_bse.mean(axis=1), axis=1)) * ALPHA
            return (y.reshape(b, s, d), aux)
        key = jax.random.key(seed)
        ks = jax.random.split(key, 5)
        sd = 1.0 / np.sqrt(D)
        sm = 1.0 / np.sqrt(MOE_D)
        return {'x': jax.random.normal(ks[0], (B, S, D), jnp.float32), 'gate_w': jax.random.normal(ks[1], (E, D), jnp.float32) * sd, 'w_gate': jax.random.normal(ks[2], (E, MOE_D, D), jnp.float32) * sd, 'w_up': jax.random.normal(ks[3], (E, MOE_D, D), jnp.float32) * sd, 'w_down': jax.random.normal(ks[4], (E, D, MOE_D), jnp.float32) * sm}
    _L0_ffn_in = _L0_ffn_setup()
    _L0_c = _w((lambda *s: np.random.randn(*s).astype(np.float32) * 0.05)(8, 256))
    _L0_wmod = _w((lambda *s: np.random.randn(*s).astype(np.float32) * 0.05)(256, 6 * 256) * 256 ** (-0.5))

    def _L1_attn_setup():
        import jax, jax.numpy as jnp
        import numpy as np
        import math
        D = 256
        H = 16
        KV = 4
        DH = D // H
        REP = H // KV
        LAMBDA_INIT = 0.8 - 0.6 * math.exp(-0.3 * 0)
        ROPE_BASE = 10000.0
        EPS = 1e-05

        def _rope(x, cos, sin):
            x1, x2 = (x[..., ::2], x[..., 1::2])
            c = cos[None, None]
            s = sin[None, None]
            o1 = x1 * c - x2 * s
            o2 = x1 * s + x2 * c
            return jnp.stack([o1, o2], axis=-1).reshape(x.shape)

        def _forward(x, Wq, Wk, Wv, Wo, lambda_q1, lambda_k1, lambda_q2, lambda_k2, gn_w, gn_b):
            B, T, _ = x.shape
            q = (x @ Wq).reshape(B, T, H, 2 * DH).transpose(0, 2, 1, 3)
            k = (x @ Wk).reshape(B, T, KV, 2 * DH).transpose(0, 2, 1, 3)
            v = (x @ Wv).reshape(B, T, KV, 2 * DH).transpose(0, 2, 1, 3)
            q1, q2 = (q[..., :DH], q[..., DH:])
            k1, k2 = (k[..., :DH], k[..., DH:])
            inv = 1.0 / ROPE_BASE ** (jnp.arange(0, DH, 2, dtype=jnp.float32) / DH)
            freqs = jnp.arange(T, dtype=jnp.float32)[:, None] * inv[None, :]
            cos, sin = (jnp.cos(freqs), jnp.sin(freqs))
            q1, q2 = (_rope(q1, cos, sin), _rope(q2, cos, sin))
            k1, k2 = (_rope(k1, cos, sin), _rope(k2, cos, sin))
            k1 = jnp.repeat(k1, REP, axis=1)
            k2 = jnp.repeat(k2, REP, axis=1)
            v = jnp.repeat(v, REP, axis=1)
            mask = jnp.triu(jnp.full((T, T), -jnp.inf, dtype=x.dtype), k=1)[None, None]
            scale = 1.0 / math.sqrt(DH)
            s1 = jnp.einsum('bhtd,bhsd->bhts', q1, k1) * scale + mask
            s2 = jnp.einsum('bhtd,bhsd->bhts', q2, k2) * scale + mask
            a1 = jax.nn.softmax(s1, axis=-1)
            a2 = jax.nn.softmax(s2, axis=-1)
            lam = jnp.exp(jnp.sum(lambda_q1 * lambda_k1)) - jnp.exp(jnp.sum(lambda_q2 * lambda_k2)) + LAMBDA_INIT
            diff = a1 - lam * a2
            out = jnp.einsum('bhts,bhsd->bhtd', diff, v)
            out = out.transpose(0, 2, 1, 3)
            mean = jnp.mean(out, axis=(1, 3), keepdims=True)
            var = jnp.var(out, axis=(1, 3), keepdims=True)
            out = (out - mean) * jax.lax.rsqrt(var + EPS)
            out = out * gn_w.reshape(1, 1, H, 2 * DH) + gn_b.reshape(1, 1, H, 2 * DH)
            out = out.reshape(B, T, 2 * H * DH) * (1.0 - LAMBDA_INIT)
            return out @ Wo
        key = jax.random.key(seed)
        ks = jax.random.split(key, 12)
        B, T = (1, 256)
        s = 0.02
        return {'x': jax.random.normal(ks[0], (B, T, D), jnp.float32), 'Wq': jax.random.normal(ks[1], (D, 2 * H * DH), jnp.float32) * s, 'Wk': jax.random.normal(ks[2], (D, 2 * KV * DH), jnp.float32) * s, 'Wv': jax.random.normal(ks[3], (D, 2 * KV * DH), jnp.float32) * s, 'Wo': jax.random.normal(ks[4], (2 * H * DH, D), jnp.float32) * s, 'lambda_q1': jax.random.normal(ks[5], (DH,), jnp.float32) * 0.1, 'lambda_k1': jax.random.normal(ks[6], (DH,), jnp.float32) * 0.1, 'lambda_q2': jax.random.normal(ks[7], (DH,), jnp.float32) * 0.1, 'lambda_k2': jax.random.normal(ks[8], (DH,), jnp.float32) * 0.1, 'gn_w': jnp.ones((2 * H * DH,), jnp.float32), 'gn_b': jnp.zeros((2 * H * DH,), jnp.float32)}
    _L1_attn_in = _L1_attn_setup()

    def _L1_ffn_setup():
        import jax, jax.numpy as jnp
        import numpy as np
        HIDDEN = 256
        INTER = 1024
        BATCH, LOCAL_SEQ = (2, 512)
        key = jax.random.key(seed)
        k1, k2, k3 = jax.random.split(key, 3)
        h_shard = jax.random.normal(k1, (BATCH, LOCAL_SEQ, HIDDEN), dtype=jnp.float32)
        w_gate_up = jax.random.normal(k2, (2 * INTER, HIDDEN), dtype=jnp.float32) * 0.02
        w_down = jax.random.normal(k3, (HIDDEN, INTER), dtype=jnp.float32) * 0.02
        return {'h_shard': h_shard, 'w_gate_up': w_gate_up, 'w_down': w_down}
    _L1_ffn_in = _L1_ffn_setup()
    _L1_c = _w((lambda *s: np.random.randn(*s).astype(np.float32) * 0.05)(8, 256))
    _L1_wmod = _w((lambda *s: np.random.randn(*s).astype(np.float32) * 0.05)(256, 6 * 256) * 256 ** (-0.5))
    _d = {'L0_attn_x': _L0_attn_in['x'], 'L0_attn_wq': _L0_attn_in['wq'], 'L0_attn_wk': _L0_attn_in['wk'], 'L0_attn_wv': _L0_attn_in['wv'], 'L0_attn_wo': _L0_attn_in['wo'], 'L0_ffn_gate_w': _L0_ffn_in['gate_w'], 'L0_ffn_w_gate': _L0_ffn_in['w_gate'], 'L0_ffn_w_up': _L0_ffn_in['w_up'], 'L0_ffn_w_down': _L0_ffn_in['w_down'], 'L0_c': _L0_c, 'L0_wmod': _L0_wmod, 'L1_attn_Wq': _L1_attn_in['Wq'], 'L1_attn_Wk': _L1_attn_in['Wk'], 'L1_attn_Wv': _L1_attn_in['Wv'], 'L1_attn_Wo': _L1_attn_in['Wo'], 'L1_attn_lambda_q1': _L1_attn_in['lambda_q1'], 'L1_attn_lambda_k1': _L1_attn_in['lambda_k1'], 'L1_attn_lambda_q2': _L1_attn_in['lambda_q2'], 'L1_attn_lambda_k2': _L1_attn_in['lambda_k2'], 'L1_attn_gn_w': _L1_attn_in['gn_w'], 'L1_attn_gn_b': _L1_attn_in['gn_b'], 'L1_ffn_w_gate_up': _L1_ffn_in['w_gate_up'], 'L1_ffn_w_down': _L1_ffn_in['w_down'], 'L1_c': _L1_c, 'L1_wmod': _L1_wmod}
    _x0 = _d['L0_attn_x']
    _d['L0_attn_x'] = jax.random.normal(jax.random.fold_in(jax.random.key(seed), 1), (8, 256, 256), dtype=_x0.dtype)
    del _x0
    return _d

def reference(L0_attn_x, L0_attn_wq, L0_attn_wk, L0_attn_wv, L0_attn_wo, L0_ffn_gate_w, L0_ffn_w_gate, L0_ffn_w_up, L0_ffn_w_down, L0_c, L0_wmod, L1_attn_Wq, L1_attn_Wk, L1_attn_Wv, L1_attn_Wo, L1_attn_lambda_q1, L1_attn_lambda_k1, L1_attn_lambda_q2, L1_attn_lambda_k2, L1_attn_gn_w, L1_attn_gn_b, L1_ffn_w_gate_up, L1_ffn_w_down, L1_c, L1_wmod):

    def _L0_attn_ref(x, wq, wk, wv, wo):
        import jax, jax.numpy as jnp
        import numpy as np
        import math
        B, T, DIM, NH = (2, 256, 256, 16)
        HD = DIM // NH

        def rotate_half(x):
            h = x.shape[-1] // 2
            return jnp.concatenate([-x[..., h:], x[..., :h]], axis=-1)

        def rope_tables(t_len, rot_dim, base=10000.0, dtype=jnp.float32):
            inv_freq = 1.0 / base ** (jnp.arange(0, rot_dim, 2, dtype=dtype) / rot_dim)
            t = jnp.arange(t_len, dtype=dtype)
            ang = jnp.einsum('i,j->ij', t, inv_freq)
            return (jnp.sin(ang), jnp.cos(ang))

        def apply_rope(q, k, sin, cos):
            h = q.shape[-1] // 2
            q1, q2 = (q[..., :h], q[..., h:])
            k1, k2 = (k[..., :h], k[..., h:])
            sin = sin[None, None]
            cos = cos[None, None]
            q1r = q1 * cos + rotate_half(q1) * sin
            k1r = k1 * cos + rotate_half(k1) * sin
            return (jnp.concatenate([q1r, q2], axis=-1), jnp.concatenate([k1r, k2], axis=-1))
        b, t, c = x.shape

        def proj(w):
            return (x @ w.T).reshape(b, t, NH, HD).transpose(0, 2, 1, 3)
        q, k, v = (proj(wq), proj(wk), proj(wv))
        sin, cos = rope_tables(t, HD, dtype=x.dtype)
        q, k = apply_rope(q, k, sin, cos)
        att = jnp.einsum('bhqd,bhkd->bhqk', q, k) * (1.0 / math.sqrt(HD))
        att = jax.nn.softmax(att, axis=-1)
        y = jnp.einsum('bhqk,bhkd->bhqd', att, v)
        y = y.transpose(0, 2, 1, 3).reshape(b, t, c)
        return y @ wo.T

    def _L0_ffn_ref(x, gate_w, w_gate, w_up, w_down):
        import jax, jax.numpy as jnp
        import numpy as np
        B, S, D = (2, 256, 256)
        MOE_D = 176
        E = 16
        K = 6
        ALPHA = 0.001

        def _moe_forward(x, gate_w, w_gate, w_up, w_down):
            b, s, d = x.shape
            T = b * s
            h = x.reshape(T, d)
            logits = h @ gate_w.T
            scores = jax.nn.softmax(logits.astype(jnp.float32), axis=-1)
            topk_w, topk_idx = jax.lax.top_k(scores, K)
            cw = jnp.zeros((T, E), jnp.float32)
            cw = cw.at[jnp.arange(T)[:, None], topk_idx].add(topk_w)
            y = jnp.zeros((T, d), x.dtype)
            for e in range(E):
                g = h @ w_gate[e].T
                u = h @ w_up[e].T
                out = jax.nn.silu(g) * u @ w_down[e].T
                y = y + cw[:, e:e + 1].astype(x.dtype) * out
            counts = jnp.sum(jax.nn.one_hot(topk_idx.reshape(b, s * K), E, dtype=jnp.float32), axis=1)
            ce = counts * (E / (s * K))
            scores_bse = scores.reshape(b, s, E)
            aux = jnp.mean(jnp.sum(ce * scores_bse.mean(axis=1), axis=1)) * ALPHA
            return (y.reshape(b, s, d), aux)
        y, _aux = _moe_forward(x, gate_w, w_gate, w_up, w_down)
        return y

    def _L1_attn_ref(x, Wq, Wk, Wv, Wo, lambda_q1, lambda_k1, lambda_q2, lambda_k2, gn_w, gn_b):
        import jax, jax.numpy as jnp
        import numpy as np
        import math
        D = 256
        H = 16
        KV = 4
        DH = D // H
        REP = H // KV
        LAMBDA_INIT = 0.8 - 0.6 * math.exp(-0.3 * 0)
        ROPE_BASE = 10000.0
        EPS = 1e-05

        def _rope(x, cos, sin):
            x1, x2 = (x[..., ::2], x[..., 1::2])
            c = cos[None, None]
            s = sin[None, None]
            o1 = x1 * c - x2 * s
            o2 = x1 * s + x2 * c
            return jnp.stack([o1, o2], axis=-1).reshape(x.shape)

        def _forward(x, Wq, Wk, Wv, Wo, lambda_q1, lambda_k1, lambda_q2, lambda_k2, gn_w, gn_b):
            B, T, _ = x.shape
            q = (x @ Wq).reshape(B, T, H, 2 * DH).transpose(0, 2, 1, 3)
            k = (x @ Wk).reshape(B, T, KV, 2 * DH).transpose(0, 2, 1, 3)
            v = (x @ Wv).reshape(B, T, KV, 2 * DH).transpose(0, 2, 1, 3)
            q1, q2 = (q[..., :DH], q[..., DH:])
            k1, k2 = (k[..., :DH], k[..., DH:])
            inv = 1.0 / ROPE_BASE ** (jnp.arange(0, DH, 2, dtype=jnp.float32) / DH)
            freqs = jnp.arange(T, dtype=jnp.float32)[:, None] * inv[None, :]
            cos, sin = (jnp.cos(freqs), jnp.sin(freqs))
            q1, q2 = (_rope(q1, cos, sin), _rope(q2, cos, sin))
            k1, k2 = (_rope(k1, cos, sin), _rope(k2, cos, sin))
            k1 = jnp.repeat(k1, REP, axis=1)
            k2 = jnp.repeat(k2, REP, axis=1)
            v = jnp.repeat(v, REP, axis=1)
            mask = jnp.triu(jnp.full((T, T), -jnp.inf, dtype=x.dtype), k=1)[None, None]
            scale = 1.0 / math.sqrt(DH)
            s1 = jnp.einsum('bhtd,bhsd->bhts', q1, k1) * scale + mask
            s2 = jnp.einsum('bhtd,bhsd->bhts', q2, k2) * scale + mask
            a1 = jax.nn.softmax(s1, axis=-1)
            a2 = jax.nn.softmax(s2, axis=-1)
            lam = jnp.exp(jnp.sum(lambda_q1 * lambda_k1)) - jnp.exp(jnp.sum(lambda_q2 * lambda_k2)) + LAMBDA_INIT
            diff = a1 - lam * a2
            out = jnp.einsum('bhts,bhsd->bhtd', diff, v)
            out = out.transpose(0, 2, 1, 3)
            mean = jnp.mean(out, axis=(1, 3), keepdims=True)
            var = jnp.var(out, axis=(1, 3), keepdims=True)
            out = (out - mean) * jax.lax.rsqrt(var + EPS)
            out = out * gn_w.reshape(1, 1, H, 2 * DH) + gn_b.reshape(1, 1, H, 2 * DH)
            out = out.reshape(B, T, 2 * H * DH) * (1.0 - LAMBDA_INIT)
            return out @ Wo
        return _forward(x, Wq, Wk, Wv, Wo, lambda_q1, lambda_k1, lambda_q2, lambda_k2, gn_w, gn_b)

    def _L1_ffn_ref(h_shard, w_gate_up, w_down):
        import jax, jax.numpy as jnp
        import numpy as np
        HIDDEN = 256
        INTER = 1024
        BATCH, LOCAL_SEQ = (2, 512)
        batch, local_seq, hidden = h_shard.shape
        gate_up = jnp.einsum('bsh,oh->bso', h_shard, w_gate_up)
        gate, up = jnp.split(gate_up, 2, axis=-1)
        h = jax.nn.silu(gate) * up
        out = jnp.einsum('bsi,hi->bsh', h, w_down)
        return out
    x = L0_attn_x
    mod = (_silu(L0_c) @ L0_wmod).reshape(L0_c.shape[0], 6, 1, -1)
    sa, ca, ga, sb, cb, gb = (mod[:, 0], mod[:, 1], mod[:, 2], mod[:, 3], mod[:, 4], mod[:, 5])
    ga = (2 * (ga >= 0) - 1) * jnp.maximum(jnp.abs(ga), 0.25)
    gb = (2 * (gb >= 0) - 1) * jnp.maximum(jnp.abs(gb), 0.25)
    h = _layernorm(x, axis=-1) * (1 + ca) + sa
    x = x + ga * _L0_attn_ref(h, L0_attn_wq, L0_attn_wk, L0_attn_wv, L0_attn_wo)
    h = _layernorm(x, axis=-1) * (1 + cb) + sb
    x = x + gb * _L0_ffn_ref(h, L0_ffn_gate_w, L0_ffn_w_gate, L0_ffn_w_up, L0_ffn_w_down)
    mod = (_silu(L1_c) @ L1_wmod).reshape(L1_c.shape[0], 6, 1, -1)
    sa, ca, ga, sb, cb, gb = (mod[:, 0], mod[:, 1], mod[:, 2], mod[:, 3], mod[:, 4], mod[:, 5])
    ga = (2 * (ga >= 0) - 1) * jnp.maximum(jnp.abs(ga), 0.25)
    gb = (2 * (gb >= 0) - 1) * jnp.maximum(jnp.abs(gb), 0.25)
    h = _layernorm(x, axis=-1) * (1 + ca) + sa
    x = x + ga * _L1_attn_ref(h, L1_attn_Wq, L1_attn_Wk, L1_attn_Wv, L1_attn_Wo, L1_attn_lambda_q1, L1_attn_lambda_k1, L1_attn_lambda_q2, L1_attn_lambda_k2, L1_attn_gn_w, L1_attn_gn_b)
    h = _layernorm(x, axis=-1) * (1 + cb) + sb
    x = x + gb * _L1_ffn_ref(h, L1_ffn_w_gate_up, L1_ffn_w_down)
    return x

_drawn_inputs = setup_inputs


def setup_inputs(seed=0):
    import zlib

    import numpy as np

    out = dict(_drawn_inputs(seed))
    spreads = {'L1_attn_gn_w': (1.0, 0.6), 'L1_attn_gn_b': (0.0, 0.8)}
    factors = {'L1_attn_Wq': 5.079,
     'L1_attn_Wk': 5.136,
     'L1_attn_lambda_q1': 8.0,
     'L1_attn_lambda_k1': 8.0,
     'L1_attn_lambda_q2': 200.0,
     'L1_attn_lambda_k2': 8.0,
     'L1_ffn_w_gate_up': 5.894,
     'L1_ffn_w_down': 5.303}
    for name, (base, spread) in spreads.items():
        noise = np.random.default_rng([zlib.crc32(name.encode()), seed]).standard_normal(out[name].shape)
        drawn = base * np.exp(spread * noise) if base else spread * noise
        out[name] = jnp.asarray(drawn.astype(out[name].dtype))
    for name, factor in factors.items():
        out[name] = (out[name] * factor).astype(out[name].dtype)
    return out
```

```python
from contextlib import ExitStack

import numpy as np

import concourse.bass as bass
from concourse import mybir

F32 = mybir.dt.float32
F32R = mybir.dt.float32r
BF16 = mybir.dt.bfloat16
ALU = mybir.AluOpType
ACT = mybir.ActivationFunctionType
AX = mybir.AxisListType

P = 128
B, T, D = 8, 256, 256
TOKENS = B * T
TILES = TOKENS // P
BT = T // P
KD = D // P
PAIRS = B // 2
PT_ = 2 * BT
NP = 2 * T
HW = 16
ROWS = 3 * HW
HEADS = 16
E, MOE_D, TOPK = 16, 176, 6
MOE_TILES = E * MOE_D // P
INTER = 1024
FFN_TILES = INTER // P
WT = 2 * KD * P + D
LN_EPS = 1e-5
GN_EPS = 1e-5
LAMBDA_INIT = 0.2
SCALE = 0.25
MASKED = -1e30
SHIFT_A, SCALE_A, GATE_A, SHIFT_B, SCALE_B, GATE_B = range(6)

C_ID = 0
C_MASK = C_ID + P
C_COS0 = C_MASK + 2 * P
C_SIN0A = C_COS0 + BT * 8
C_SIN0B = C_SIN0A + BT * 4
C_COS1 = C_SIN0B + BT * 4
C_SIN1A = C_COS1 + BT * 16
C_SIN1B = C_SIN1A + BT * 8
C_END = C_SIN1B + BT * 8


class Parts:
    pass


def new_semaphore(nc, c, stack, name):
    made = stack.enter_context(nc.semaphore(name))
    c.used.append(made)
    return made


def flat(ap):
    return ap.rearrange("p a b -> p (a b)")


def split_heads(ap, heads, width):
    return ap.rearrange("p (h w) -> p h w", h=heads, w=width)


def ln_vector(v, s, i):
    for t in range(PT_):
        v.bn_stats(s.stats[:, t, :], flat(s.x[:, bass.ds(PT_ * i + t, 1), :])).then_inc(s.ln_stats, 1)
    v.wait_ge(s.ln_stats, PT_ * i + PT_)
    v.sem_inc(s.passed)
    for t in range(PT_):
        v.bn_aggr(s.moments[:, t, :], s.stats[:, t, :]).then_inc(s.ln_moments, 1)
    v.wait_ge(s.ln_moments, PT_ * i + PT_)
    v.tensor_scalar(s.var[:], s.moments[:, :, 1], LN_EPS, None, ALU.add).then_inc(s.ln_var, 1)
    v.wait_ge(s.ln_rstd, i + 1)
    for t in range(PT_):
        v.tensor_scalar(s.xn[:, t, :], flat(s.x[:, bass.ds(PT_ * i + t, 1), :]), s.moments[:, t, 0:1],
                        s.rstd[:, t:t + 1], ALU.subtract, ALU.mult).then_inc(s.ln_xn, 1)


def ln_gpsimd_rstd(g, s, i):
    g.wait_ge(s.ln_var, i + 1)
    g.tensor_tensor(s.rstd[:], s.var[:], s.minus_half[:, 0:PT_], ALU.pow).then_inc(s.ln_rstd, 1)


def ln_tensor(t_, s, i):
    t_.wait_ge(s.ln_xn, PT_ * i + PT_)
    for half in range(KD):
        for t in range(PT_):
            mm = t_.transpose(s.ps[:, half, t * P:(t + 1) * P], s.xn[:, t, half * P:(half + 1) * P], s.ident)
    mm.then_inc(s.ln_turned, 1)


def ln_scalar(a, s, i):
    a.wait_ge(s.ln_turned, i + 1)
    for half in range(KD):
        for b in range(2):
            a.activation(s.h[:, half, b * T:(b + 1) * T], s.ps[:, half, b * T:(b + 1) * T], ACT.Identity,
                         scale=s.mod[:, KD * s.scale + half, bass.ds(2 * i + b, 1)],
                         bias=s.mod[:, KD * s.shift + half, bass.ds(2 * i + b, 1)]).then_inc(s.ln_h, 1)


def ln_gpsimd_split(g, s, i, h_hi, h_lo):
    for half in range(KD):
        g.wait_ge(s.ln_h, 2 * KD * i + 2 * half + 2)
        g.sem_inc(s.passed)
        g.tensor_copy(h_hi(half), s.h[:, half, :]).then_inc(s.ln_hi, 1)
        g.wait_ge(s.ln_hi, KD * i + half + 1)
        g.tensor_tensor(h_lo(half), s.h[:, half, :], h_hi(half).bitcast(F32), ALU.subtract).then_inc(s.ln_lo, 1)


def ln_buffers(sb, sem, c, mod, shift, scale):
    s = Parts()
    s.x = c.x
    s.ps = c.ps
    s.ident = c.ident
    s.minus_half = c.minus_half
    s.mod = mod
    s.shift = shift
    s.scale = scale
    s.stats = sb("ln_stats_t", [P, PT_, 6], F32)
    s.moments = sb("ln_moments_t", [P, PT_, 2], F32)
    s.var = sb("ln_var_t", [P, PT_], F32)
    s.rstd = sb("ln_rstd_t", [P, PT_], F32)
    s.xn = sb("ln_xn_t", [P, PT_, D], F32)
    s.h = sb("ln_h_t", [P, KD, NP], F32)
    s.ln_stats = sem("ln_stats")
    s.ln_moments = sem("ln_moments")
    s.ln_var = sem("ln_var")
    s.ln_rstd = sem("ln_rstd")
    s.ln_xn = sem("ln_xn")
    s.ln_turned = sem("ln_turned")
    s.ln_h = sem("ln_h")
    s.ln_hi = sem("ln_hi")
    s.ln_lo = sem("ln_lo")
    s.passed = sem("passed")
    return s


def qkv_buffers(sb, sem, n_q, n_k, n_v, v_width):
    s = Parts()
    s.n_q = n_q
    s.n_k = n_k
    s.n_v = n_v
    s.v_width = v_width
    s.n_qk = n_q + n_k
    s.h_hi = sb("h_hi", [P, KD, NP], F32R)
    s.h_lo = sb("h_lo", [P, KD, NP], F32R)
    s.cosine = sb("rope_cos_part", [P, 2, s.n_qk * HW], F32)
    s.sine = sb("rope_sin_part", [P, 2, s.n_qk * HW], F32)
    s.roped = sb("roped", [P, 2, s.n_qk * HW], F32)
    s.q_stack = [sb(f"q_stack{j}", [P, n_q * 64], F32) for j in range(2)]
    s.k_stack = [sb(f"k_stack{j}", [P, n_k * 64], F32) for j in range(2)]
    s.q_rows = sb("q_rows", [P, 2, n_q // 2, T], F32R)
    s.k_rows = sb("k_rows", [P, 2, n_k // 2, T], F32R)
    s.v = sb("v_ones", [P, PT_, n_v, v_width + 1], F32)
    s.qkv_done = sem("qkv_done")
    s.v_copied = sem("v_copied")
    s.plain_copied = sem("plain_copied")
    s.rope_parts = sem("rope_parts")
    s.roped_ready = sem("roped_ready")
    s.stack_hi = sem("stack_hi")
    s.stack_lo = sem("stack_lo")
    s.rows_turned = sem("rows_turned")
    s.q_rows_ready = sem("q_rows_ready")
    s.k_rows_ready = sem("k_rows_ready")
    s.stacks_set = sem("stacks_set")
    s.q_rounds, s.k_rounds = n_q // 8, n_k // 8
    s.rounds = s.q_rounds + s.k_rounds
    return s


def stack_view(stack, heads):
    return stack[:, :].rearrange("p (h s w) -> p h s w", h=heads, s=4, w=HW)


def qkv_gpsimd_prepare(g, q):
    for j in range(2):
        g.memset(q.q_stack[j][:], 0.0).then_inc(q.stacks_set, 1)
        g.memset(q.k_stack[j][:], -1.0).then_inc(q.stacks_set, 1)
    g.memset(q.v[:], 1.0).then_inc(q.stacks_set, 1)


def qkv_tensor(t_, s, q, w_hi, w_lo, i):
    def project(t):
        if t == 0:
            t_.wait_ge(s.ln_lo, KD * i + KD)
        else:
            if t >= 2:
                t_.wait_ge(q.v_copied, PT_ * i + t - 1)
                t_.wait_ge(q.rope_parts, 3 * (PT_ * i + t - 1))
        b0 = 2 + 2 * (t % 2)
        tok = slice(t * P, (t + 1) * P)
        terms = [(h, w, k) for k in range(KD) for h, w in ((q.h_hi, w_hi), (q.h_hi, w_lo), (q.h_lo, w_hi))]
        for n, (h, w, k) in enumerate(terms):
            for bank, lo, hi in ((b0, 0, 512), (b0 + 1, 512, 768)):
                mm = t_.matmul(s.ps[:, bank, 0:hi - lo], h[:, k, tok], w[:, k, lo:hi],
                               start=(n == 0), stop=(n == len(terms) - 1))
        mm.then_inc(q.qkv_done, 1)

    def turn(t):
        t_.wait_ge(q.stack_lo, 2 * (PT_ * i + t + 1))
        for r in range(q.rounds):
            done = q.rounds * t + r
            if done >= 4:
                last = done - 4
                lt, lr = last // q.rounds, last % q.rounds
                if lr < q.q_rounds:
                    t_.wait_ge(q.q_rows_ready, q.q_rounds * (PT_ * i + lt) + lr + 1)
                else:
                    t_.wait_ge(q.k_rows_ready, q.k_rounds * (PT_ * i + lt) + lr - q.q_rounds + 1)
            bank = (6, 7, 0, 1)[done % 4]
            src, at = (q.q_stack, r) if r < q.q_rounds else (q.k_stack, r - q.q_rounds)
            for c in range(4):
                mm = t_.transpose(s.ps[:, bank, c * P:(c + 1) * P],
                                  src[t % 2][:, (4 * at + c) * P:(4 * at + c + 1) * P], s.ident)
            mm.then_inc(q.rows_turned, 1)

    for t in range(PT_):
        project(t)
        if t >= 1:
            turn(t - 1)
    turn(PT_ - 1)


def qkv_scalar(a, s, q, i, plain):
    def rows(t):
        for r in range(q.q_rounds):
            done = q.rounds * t + r
            bank = (6, 7, 0, 1)[done % 4]
            a.wait_ge(q.rows_turned, q.rounds * (PT_ * i + t) + r + 1)
            a.activation(q.q_rows[:, t // BT, 4 * r:4 * r + 4, (t % BT) * P:(t % BT + 1) * P],
                         s.ps[:, bank, :].rearrange("p (c n) -> p c n", c=4), ACT.Copy).then_inc(q.q_rows_ready, 1)

    for t in range(PT_):
        b0 = 2 + 2 * (t % 2)
        a.wait_ge(q.qkv_done, PT_ * i + t + 1)
        v_from = q.n_qk * HW - 512
        a.activation(q.v[:, t, :, 0:q.v_width],
                     split_heads(s.ps[:, b0 + 1, v_from:v_from + q.n_v * q.v_width], q.n_v, q.v_width),
                     ACT.Copy).then_inc(q.v_copied, 1)
        if plain:
            if t >= 2:
                a.wait_ge(q.stack_lo, 2 * (PT_ * i + t - 1))
            a.activation(split_heads(q.roped[:, t % 2, :], q.n_qk, HW)[:, :, 8:16],
                         split_heads(s.ps[:, b0, :], q.n_qk, HW)[:, :, 8:16], ACT.Copy).then_inc(q.plain_copied, 1)
        if t >= 1:
            rows(t - 1)
    rows(PT_ - 1)


def qkv_gpsimd(g, s, q, i, plain):
    for t in range(PT_):
        g.wait_ge(q.roped_ready, 2 * (PT_ * i + t + 1))
        if plain:
            g.wait_ge(q.plain_copied, PT_ * i + t + 1)
        if t >= 2:
            g.wait_ge(q.rows_turned, q.rounds * (PT_ * i + t - 1))
        g.sem_inc(s.passed)
        roped = split_heads(q.roped[:, t % 2, :], q.n_qk, HW)
        qs = stack_view(q.q_stack[t % 2], q.n_q).bitcast(F32R)
        ks = stack_view(q.k_stack[t % 2], q.n_k).bitcast(F32R)
        g.tensor_copy(qs[:, :, 0:3:2, :], roped[:, 0:q.n_q, :].unsqueeze(2).to_broadcast([P, q.n_q, 2, HW]))\
            .then_inc(q.stack_hi, 1)
        g.tensor_copy(ks[:, :, 0:2, :], roped[:, q.n_q:q.n_qk, :].unsqueeze(2).to_broadcast([P, q.n_k, 2, HW]))\
            .then_inc(q.stack_hi, 1)


def qkv_vector(v, s, q, i, rope, plain):
    def rotate(t):
        b0 = 2 + 2 * (t % 2)
        v.wait_ge(q.plain_copied if plain else q.v_copied, PT_ * i + t + 1)
        x = split_heads(s.psflat[:, b0 * 512:b0 * 512 + q.n_qk * HW], q.n_qk, HW)
        cp = split_heads(q.cosine[:, t % 2, :], q.n_qk, HW)
        sp = split_heads(q.sine[:, t % 2, :], q.n_qk, HW)
        out = split_heads(q.roped[:, t % 2, :], q.n_qk, HW)
        w, half = rope.width, rope.width // 2
        cos = rope.cos[:, t % BT, :].unsqueeze(1).to_broadcast([P, q.n_qk, w])
        sin_a = rope.sin_a[:, t % BT, :].unsqueeze(1).to_broadcast([P, q.n_qk, half])
        sin_b = rope.sin_b[:, t % BT, :].unsqueeze(1).to_broadcast([P, q.n_qk, half])
        v.tensor_tensor(cp[:, :, 0:w], x[:, :, 0:w], cos, ALU.mult).then_inc(q.rope_parts, 1)
        v.tensor_tensor(rope.first(sp), rope.second(x), sin_a, ALU.mult).then_inc(q.rope_parts, 1)
        v.tensor_tensor(rope.second(sp), rope.first(x), sin_b, ALU.mult).then_inc(q.rope_parts, 1)
        v.wait_ge(q.rope_parts, 3 * (PT_ * i + t + 1))
        v.tensor_tensor(out[:, :, 0:w], cp[:, :, 0:w], sp[:, :, 0:w], ALU.add).then_inc(q.roped_ready, 2)

    def low(t):
        v.wait_ge(q.stack_hi, 2 * (PT_ * i + t + 1))
        roped = split_heads(q.roped[:, t % 2, :], q.n_qk, HW)
        qs, ks = stack_view(q.q_stack[t % 2], q.n_q), stack_view(q.k_stack[t % 2], q.n_k)
        v.tensor_tensor(qs[:, :, 1, :].bitcast(F32R), roped[:, 0:q.n_q, :], qs[:, :, 0, :], ALU.subtract)\
            .then_inc(q.stack_lo, 1)
        v.tensor_tensor(ks[:, :, 2, :].bitcast(F32R), roped[:, q.n_q:q.n_qk, :], ks[:, :, 0, :], ALU.subtract)\
            .then_inc(q.stack_lo, 1)

    def rows(t):
        for r in range(q.k_rounds):
            n = q.q_rounds + r
            bank = (6, 7, 0, 1)[(q.rounds * t + n) % 4]
            v.wait_ge(q.rows_turned, q.rounds * (PT_ * i + t) + n + 1)
            v.tensor_copy(q.k_rows[:, t // BT, 4 * r:4 * r + 4, (t % BT) * P:(t % BT + 1) * P],
                          s.ps[:, bank, :].rearrange("p (c n) -> p c n", c=4)).then_inc(q.k_rows_ready, 1)

    for t in range(PT_):
        rotate(t)
        if t >= 1:
            low(t - 1)
            rows(t - 1)
    low(PT_ - 1)
    rows(PT_ - 1)


def weights_hi_lo(a, g, raw_ready, count, raw, hi, lo, done_hi, done_lo, engine):
    if engine == "scalar":
        a.wait_ge(raw_ready, count)
        a.activation(hi, raw, ACT.Copy).then_inc(done_hi, 1)
    else:
        g.tensor_tensor(lo, raw, hi.bitcast(F32), ALU.subtract).then_inc(done_lo, 1)


def setup(nc, c, args):
    with ExitStack() as stack:
        def sb(name, shape, dt):
            return stack.enter_context(nc.sbuf_tensor(name, shape, dt))

        def sem(name):
            return new_semaphore(nc, c, stack, name)

        cond = [sb(f"cond{n}", [P, KD, B], F32) for n in range(2)]
        cond_silu = [sb(f"cond_silu{n}", [P, KD, B], F32) for n in range(2)]
        wmod = [sb(f"wmod{n}", [P, KD, 6 * D], F32) for n in range(2)]
        gate_sign = sb("gate_sign", [P, 2, 2 * KD * B], F32)
        gate_size = sb("gate_size", [P, 2, 2 * KD * B], F32)
        lam_in = sb("lam_in", [P, 4, HW], F32)
        lam_prod = sb("lam_prod", [P, 2, HW], F32)
        lam_sum = sb("lam_sum", [P, 2], F32)
        lam_exp = sb("lam_exp", [P, 2], F32)

        consts_in, x_in, cond_in, wmod_in, attn_in, lam_loaded, gn_in = (
            sem(n) for n in ("consts_in", "x_in", "cond_in", "wmod_in", "attn_in", "lam_loaded", "gn_in"))
        silu_done, mod_done, mod_read, sign_done, size_done, gates_done = (
            sem(n) for n in ("silu_done", "mod_done", "mod_read", "sign_done", "size_done", "gates_done"))
        lam_mul, lam_added, lam_exped, lam_done = (sem(n) for n in ("lam_mul", "lam_added", "lam_exped", "lam_done"))
        whi_done, wlo_done, fills = (sem(n) for n in ("whi_done", "wlo_done", "fills"))
        block = stack.enter_context(nc.Block())

        @block.sync
        def _(sp):
            sp.dma_start(cond[0][:], args.c0).then_inc(cond_in, 16)
            sp.dma_start(cond[1][:], args.c1).then_inc(cond_in, 16)
            for n, w in enumerate((args.wmod0, args.wmod1)):
                sp.dma_start(wmod[n][:], w).then_inc(wmod_in, 16)
            sp.dma_start(c.consts[:], args.consts).then_inc(consts_in, 16)
            sp.dma_start(c.x[:], args.x).then_inc(x_in, 16)
            sp.wait_ge(consts_in, 16)
            sp.wait_ge(x_in, 16)

        @block.scalar
        def _(a):
            a.dma_start(c.w0[:], args.w0).then_inc(attn_in, 16)
            a.dma_start(lam_in[:], args.lam).then_inc(lam_loaded, 16)
            a.dma_start(c.gn[:], args.gn).then_inc(gn_in, 16)
            a.wait_ge(cond_in, 32)
            for n in range(2):
                a.activation(flat(cond_silu[n][:]), flat(cond[n][:]), ACT.Silu).then_inc(silu_done, 1)
            a.wait_ge(lam_added, 1)
            a.activation(lam_exp[:], lam_sum[:], ACT.Exp).then_inc(lam_exped, 1)
            a.wait_ge(attn_in, 16)
            a.activation(flat(c.w0_hi[:]), flat(c.w0[:]), ACT.Copy).then_inc(whi_done, 1)

        @block.gpsimd
        def _(g):
            g.memset(c.minus_half[:], -0.5).then_inc(fills, 1)
            g.memset(c.mean_of[:], 1.0 / (T * 2 * HW)).then_inc(fills, 1)
            g.wait_ge(consts_in, 16)
            g.tensor_copy(c.ident_bf[:], c.consts[:, C_ID:C_ID + P]).then_inc(fills, 1)
            g.tensor_copy(c.mask_bf[:], c.consts[:, C_MASK:C_MASK + 2 * P]).then_inc(fills, 1)
            g.wait_ge(whi_done, 1)
            g.tensor_tensor(flat(c.w0_lo[:]), flat(c.w0[:]), flat(c.w0_hi[:]).bitcast(F32), ALU.subtract)\
                .then_inc(wlo_done, 1)

        @block.tensor
        def _(t_):
            for n in range(2):
                t_.wait_ge(silu_done, n + 1)
                t_.wait_ge(wmod_in, 32)
                for col in range(6 * KD):
                    for k in range(KD):
                        mm = t_.matmul(c.ps[:, n, col * B:(col + 1) * B], wmod[n][:, k, col * P:(col + 1) * P],
                                       cond_silu[n][:, k, :], start=(k == 0), stop=(k == KD - 1))
                mm.then_inc(mod_done, 1)

        @block.vector
        def _(v):
            v.wait_ge(lam_loaded, 16)
            v.tensor_tensor(lam_prod[:], lam_in[:, 0:4:2, :], lam_in[:, 1:4:2, :], ALU.mult).then_inc(lam_mul, 1)
            v.wait_ge(lam_mul, 1)
            v.tensor_reduce(lam_sum[:], lam_prod[:], AX.X, ALU.add).then_inc(lam_added, 1)
            for n in range(2):
                mod = flat(c.mod[n][:])
                v.wait_ge(mod_done, n + 1)
                v.tensor_copy(mod, c.ps[:, n, 0:6 * KD * B]).then_inc(mod_read, 1)
                v.wait_ge(mod_read, 3 * n + 1)
                for part in (SCALE_A, SCALE_B):
                    at = c.mod[n][:, KD * part:KD * part + KD, :]
                    v.tensor_scalar(at, at, 1.0, None, ALU.add).then_inc(mod_read, 1)
                for j, part in enumerate((GATE_A, GATE_B)):
                    g = flat(c.mod[n][:, KD * part:KD * part + KD, :])
                    at = slice(j * KD * B, (j + 1) * KD * B)
                    v.tensor_scalar(gate_sign[:, n, at], g, 0.0, 2.0, ALU.is_ge, ALU.mult).then_inc(sign_done, 1)
                    v.tensor_scalar(gate_size[:, n, at], g, -1.0, None, ALU.mult).then_inc(sign_done, 1)
                v.wait_ge(sign_done, 4 * n + 4)
                for j, part in enumerate((GATE_A, GATE_B)):
                    g = flat(c.mod[n][:, KD * part:KD * part + KD, :])
                    at = slice(j * KD * B, (j + 1) * KD * B)
                    v.scalar_tensor_tensor(gate_size[:, n, at], gate_size[:, n, at], 0.25, g, ALU.max, ALU.max)\
                        .then_inc(size_done, 1)
                v.wait_ge(size_done, 2 * n + 2)
                for j, part in enumerate((GATE_A, GATE_B)):
                    g = flat(c.mod[n][:, KD * part:KD * part + KD, :])
                    at = slice(j * KD * B, (j + 1) * KD * B)
                    v.scalar_tensor_tensor(g, gate_sign[:, n, at], -1.0, gate_size[:, n, at], ALU.add, ALU.mult)\
                        .then_inc(gates_done, 1)
            v.wait_ge(lam_exped, 1)
            v.scalar_tensor_tensor(c.neg_lam[:], lam_exp[:, 1:2], -LAMBDA_INIT, lam_exp[:, 0:1],
                                   ALU.add, ALU.subtract).then_inc(lam_done, 1)
            v.wait_ge(gn_in, 16)
            v.tensor_scalar(c.gn[:], c.gn[:], 1.0 - LAMBDA_INIT, None, ALU.mult).then_inc(lam_done, 1)


def out_project(c, s, o, f_tiles):
    def tensor(t_, i, b, turned_from):
        n = 2 * i + b
        t_.wait_ge(o.o_lo_done, n + 1)
        for dh in range(KD):
            terms = [(w, x, f) for f in range(f_tiles)
                     for w, x in ((o.wo_hi, o.o_hi), (o.wo_hi, o.o_lo), (o.wo_lo, o.o_hi))]
            for m, (w, x, f) in enumerate(terms):
                mm = t_.matmul(c.ps[:, 1 if turned_from == 1 else 1, dh * T:(dh + 1) * T],
                               w[:, f, dh * P:(dh + 1) * P], x[:, f, :],
                               start=(m == 0), stop=(m == len(terms) - 1))
        mm.then_inc(o.y_done, 1)

    def tensor_back(t_, i, b):
        n = 2 * i + b
        t_.wait_ge(o.y_gated, KD * (n + 1))
        for q in range(BT):
            for dh in range(KD):
                mm = t_.transpose(c.ps[:, 0, q * D + dh * P:q * D + (dh + 1) * P],
                                  o.y[:, dh, q * P:(q + 1) * P], c.ident)
        mm.then_inc(o.y_turned, 1)

    def scalar_gate(a, i, b):
        n = 2 * i + b
        a.wait_ge(o.y_done, n + 1)
        for dh in range(KD):
            a.activation(o.y[:, dh, :], c.ps[:, 1, dh * T:(dh + 1) * T], ACT.Copy,
                         scale=o.mod[:, KD * GATE_A + dh, bass.ds(2 * i + b, 1)]).then_inc(o.y_gated, 1)

    def vector_add(v, i, b):
        n = 2 * i + b
        v.wait_ge(o.y_turned, n + 1)
        x = flat(c.x[:, bass.ds(PT_ * i + BT * b, BT), :])
        v.tensor_tensor(x, x, c.ps[:, 0, :], ALU.add).then_inc(o.x_added, 1)

    made = Parts()
    made.tensor = tensor
    made.tensor_back = tensor_back
    made.scalar_gate = scalar_gate
    made.vector_add = vector_add
    return made


def attention0(nc, c):
    with ExitStack() as stack:
        def sb(name, shape, dt):
            return stack.enter_context(nc.sbuf_tensor("a0_" + name, shape, dt))

        def sem(name):
            return new_semaphore(nc, c, stack, "a0_" + name)

        s = ln_buffers(sb, sem, c, c.mod[0], SHIFT_A, SCALE_A)
        s.psflat = c.psflat
        q = qkv_buffers(sb, sem, HEADS, HEADS, HEADS, HW)
        w_hi, w_lo = c.w0_hi[:, :, 0:768], c.w0_lo[:, :, 0:768]
        maxima = sb("maxima", [P, 2, BT, HEADS], F32)
        max_rows = sb("max_rows", [HEADS, 2, T], F32R)
        probs = sb("probs", [P, 2, 2, BT * T], F32)
        denom = sb("denom", [P, BT, HEADS], F32)
        heads_out = sb("heads_out", [P, BT, D], F32)
        o = Parts()
        o.wo_hi = c.w0_hi[:, :, 768:1024]
        o.wo_lo = c.w0_lo[:, :, 768:1024]
        o.mod = c.mod[0]
        o.o_hi = sb("o_hi", [P, KD, T], F32R)
        o.o_lo = sb("o_lo", [P, KD, T], F32R)
        o.y = sb("y", [P, KD, T], F32)
        o.o_hi_done = sem("o_hi_done")
        o.o_lo_done = sem("o_lo_done")
        o.y_done = sem("y_done")
        o.y_gated = sem("y_gated")
        o.y_turned = sem("y_turned")
        o.x_added = sem("x_added")
        scores_done, max_done, max_turned, max_rows_ready, max_in = (
            sem(n) for n in ("scores_done", "max_done", "max_turned", "max_rows_ready", "max_in"))
        keyed_done, exp_done, pv_done, denom_done, out_scaled, out_turned = (
            sem(n) for n in ("keyed_done", "exp_done", "pv_done", "denom_done", "out_scaled", "out_turned"))
        proj = out_project(c, s, o, KD)
        rope = Parts()
        rope.width = 8
        rope.first = lambda a: a[:, :, 0:4]
        rope.second = lambda a: a[:, :, 4:8]
        rope.cos = c.table(C_COS0, 8)
        rope.sin_a = c.table(C_SIN0A, 4)
        rope.sin_b = c.table(C_SIN0B, 4)
        GROUPS = HEADS // 2
        ps = c.ps
        ones_col = HW + 1
        pv_view = ps[:, 6:8, 0:HEADS * ones_col].rearrange("p q (h w) -> p q h w", h=HEADS, w=ones_col)
        block = stack.enter_context(nc.Block())

        @block.tensor
        def _(t_):
            t_.wait_ge(q.stacks_set, 5)

            def row_scores(i, b, h):
                n = HEADS * (2 * i + b) + h
                if h >= 2:
                    t_.wait_ge(max_done, n - 1)
                if b == 1 and h == 0:
                    t_.wait_ge(max_rows_ready, 2 * i + 1)
                base, pair = 64 * (h % 2), h // 2
                for qt in range(BT):
                    mm = t_.matmul(ps[:, h % 2, qt * T:(qt + 1) * T],
                                   q.q_rows[base:base + ROWS, b, pair, qt * P:(qt + 1) * P],
                                   q.k_rows[base:base + ROWS, b, pair, :], start=(qt == 0), stop=(qt == BT - 1),
                                   skip_group_check=True)
                mm.then_inc(scores_done, 1)

            def turn_maxima(i, b):
                t_.wait_ge(max_done, HEADS * (2 * i + b + 1))
                for qt in range(BT):
                    mm = t_.transpose(ps[0:HEADS, 0, qt * P:(qt + 1) * P], maxima[:, b, qt, :], c.ident)
                mm.then_inc(max_turned, 1)

            def key_scores(i, b, g):
                n = GROUPS * (2 * i + b) + g
                if g == 0:
                    t_.wait_ge(max_in, 32 * (2 * i + b + 1))
                if g >= 2 or b == 1:
                    t_.wait_ge(exp_done, n - 1)
                for hh in range(2):
                    base = 64 * hh
                    for kt in range(BT):
                        mm = t_.matmul(ps[:, 2 + 2 * (g % 2) + hh, kt * T:(kt + 1) * T],
                                       q.k_rows[base:base + ROWS + 1, b, g, kt * P:(kt + 1) * P],
                                       q.q_rows[base:base + ROWS + 1, b, g, :], start=(kt == 0), stop=(kt == BT - 1),
                                       skip_group_check=True)
                mm.then_inc(keyed_done, 1)

            def weigh(i, b, g):
                n = GROUPS * (2 * i + b) + g
                t_.wait_ge(exp_done, n + 1)
                if g == 0 and b == 1:
                    t_.wait_ge(out_scaled, 2 * i + 1)
                for hh in range(2):
                    h = 2 * g + hh
                    for qt in range(BT):
                        for kt in range(BT):
                            mm = t_.matmul(ps[:, 6 + qt, h * ones_col:(h + 1) * ones_col],
                                           probs[:, g % 2, hh, kt * T + qt * P:kt * T + (qt + 1) * P],
                                           q.v[:, BT * b + kt, h, :], start=(kt == 0), stop=(kt == BT - 1))
                mm.then_inc(pv_done, 1)

            def turn_out(i, b):
                t_.wait_ge(out_scaled, 2 * i + b + 1)
                for f in range(KD):
                    for qt in range(BT):
                        mm = t_.transpose(ps[:, 0, f * T + qt * P:f * T + (qt + 1) * P],
                                          heads_out[:, qt, f * P:(f + 1) * P], c.ident)
                mm.then_inc(out_turned, 1)

            with t_.Fori(0, PAIRS) as i:
                ln_tensor(t_, s, i)
                qkv_tensor(t_, s, q, w_hi, w_lo, i)
                t_.wait_ge(q.q_rows_ready, q.q_rounds * (PT_ * i + PT_))
                t_.wait_ge(q.k_rows_ready, q.k_rounds * (PT_ * i + PT_))
                for h in range(HEADS):
                    row_scores(i, 0, h)
                turn_maxima(i, 0)
                for g in range(GROUPS + 1):
                    if g < GROUPS:
                        row_scores(i, 1, 2 * g)
                        row_scores(i, 1, 2 * g + 1)
                        key_scores(i, 0, g)
                    if g >= 1:
                        weigh(i, 0, g - 1)
                turn_maxima(i, 1)
                for g in range(GROUPS + 1):
                    if g < GROUPS:
                        key_scores(i, 1, g)
                    if g == 1:
                        t_.wait_ge(max_rows_ready, 2 * i + 2)
                        turn_out(i, 0)
                    if g == 3:
                        proj.tensor(t_, i, 0, 0)
                    if g == 5:
                        proj.tensor_back(t_, i, 0)
                    if g >= 1:
                        weigh(i, 1, g - 1)
                t_.wait_ge(o.x_added, 2 * i + 1)
                turn_out(i, 1)
                proj.tensor(t_, i, 1, 0)
                proj.tensor_back(t_, i, 1)

        @block.scalar
        def _(a):
            def exps(i, b, g):
                n = GROUPS * (2 * i + b) + g
                a.wait_ge(keyed_done, n + 1)
                if g >= 2 or b == 1:
                    a.wait_ge(pv_done, n - 1)
                a.activation(probs[:, g % 2, :, :], ps[:, 2 + 2 * (g % 2):4 + 2 * (g % 2), :], ACT.Exp,
                             scale=SCALE).then_inc(exp_done, 1)

            def max_out(i, b):
                a.wait_ge(max_turned, 2 * i + b + 1)
                a.activation(max_rows[:, b, :], ps[0:HEADS, 0, 0:T], ACT.Copy).then_inc(max_rows_ready, 1)

            def out_hi(i, b):
                a.wait_ge(out_turned, 2 * i + b + 1)
                a.activation(o.o_hi[:], ps[:, 0, :].rearrange("p (f n) -> p f n", f=KD), ACT.Copy)\
                    .then_inc(o.o_hi_done, 1)

            a.wait_ge(q.stacks_set, 5)
            with a.Fori(0, PAIRS) as i:
                ln_scalar(a, s, i)
                qkv_scalar(a, s, q, i, plain=True)
                max_out(i, 0)
                for g in range(GROUPS):
                    exps(i, 0, g)
                max_out(i, 1)
                for g in range(GROUPS):
                    exps(i, 1, g)
                    if g == 1:
                        out_hi(i, 0)
                    if g == 3:
                        proj.scalar_gate(a, i, 0)
                out_hi(i, 1)
                proj.scalar_gate(a, i, 1)

        @block.vector
        def _(v):
            def max_of(i, b, h):
                v.wait_ge(scores_done, HEADS * (2 * i + b) + h + 1)
                col = GROUPS * (h % 2) + h // 2
                v.tensor_reduce(maxima[:, b, :, col:col + 1],
                                ps[:, h % 2, :].rearrange("p (q k) -> p q k", q=BT), AX.X, ALU.max)\
                    .then_inc(max_done, 1)

            def scale_out(i, b):
                n = 2 * i + b
                v.wait_ge(pv_done, GROUPS * (n + 1))
                v.reciprocal(denom[:], pv_view[:, :, :, HW]).then_inc(denom_done, 1)
                v.wait_ge(denom_done, n + 1)
                if b == 1:
                    v.wait_ge(out_turned, 2 * i + 1)
                v.tensor_tensor(heads_out[:].rearrange("p q (h w) -> p q h w", h=HEADS, w=HW),
                                pv_view[:, :, :, 0:HW],
                                denom[:].unsqueeze(3).to_broadcast([P, BT, HEADS, HW]), ALU.mult)\
                    .then_inc(out_scaled, 1)

            def out_lo(i, b):
                v.wait_ge(o.o_hi_done, 2 * i + b + 1)
                v.tensor_tensor(o.o_lo[:], ps[:, 0, :].rearrange("p (f n) -> p f n", f=KD),
                                o.o_hi[:].bitcast(F32), ALU.subtract).then_inc(o.o_lo_done, 1)

            v.wait_ge(q.stacks_set, 5)
            with v.Fori(0, PAIRS) as i:
                ln_vector(v, s, i)
                qkv_vector(v, s, q, i, rope, plain=True)
                for b in range(2):
                    for h in range(HEADS):
                        max_of(i, b, h)
                scale_out(i, 0)
                out_lo(i, 0)
                proj.vector_add(v, i, 0)
                scale_out(i, 1)
                out_lo(i, 1)
                proj.vector_add(v, i, 1)

        @block.gpsimd
        def _(g):
            qkv_gpsimd_prepare(g, q)
            g.wait_ge(q.stacks_set, 5)
            with g.Fori(0, PAIRS) as i:
                ln_gpsimd_rstd(g, s, i)
                ln_gpsimd_split(g, s, i, lambda half: q.h_hi[:, half, :], lambda half: q.h_lo[:, half, :])
                qkv_gpsimd(g, s, q, i, plain=True)

        @block.sync
        def _(sp):
            with sp.Fori(0, PAIRS) as i:
                for b in range(2):
                    sp.wait_ge(max_rows_ready, 2 * i + b + 1)
                    for hh in range(2):
                        row = 64 * hh + ROWS
                        sp.dma_start(q.q_rows[row:row + 1, b, :, :].bitcast(F32),
                                     max_rows[GROUPS * hh:GROUPS * (hh + 1), b, :].bitcast(F32))\
                            .then_inc(max_in, 16)
            sp.wait_ge(max_in, 32 * B)


def mlp_buffers(sb, sem, slots):
    m = Parts()
    m.w_hi = [sb(f"w_hi{j}", [P, WT], F32R) for j in range(slots)]
    m.w_lo = [sb(f"w_lo{j}", [P, WT], F32R) for j in range(slots)]
    m.silu = sb("silu", [P, 2, NP], F32)
    m.act = sb("act", [P, 2, NP], F32)
    m.act_hi = sb("act_hi", [P, 4, NP], F32R)
    m.act_lo = sb("act_lo", [P, 4, NP], F32R)
    m.up_done = sem("up_done")
    m.silu_done = sem("silu_done")
    m.act_done = sem("act_done")
    m.weighted = sem("weighted")
    m.act_hi_done = sem("act_hi_done")
    m.act_lo_done = sem("act_lo_done")
    m.down_done = sem("down_done")
    m.y_added = sem("y_added")
    m.w_hi_done = sem("w_hi_done")
    m.w_lo_done = sem("w_lo_done")
    m.raw_in = [sem(f"raw_in{j}") for j in range(2)]
    return m


def mlp_up(t_, c, m, n, j, slot, tb, first, expert_of=None, cw_rows=None):
    if not first:
        t_.wait_ge(m.act_done, n - 1)
        if expert_of is not None:
            t_.wait_ge(m.weighted, n - 1)
    tok = slice(tb * NP, (tb + 1) * NP)
    for bank, at in ((0, 0), (2, KD * P)):
        terms = [(w, h, k) for k in range(KD)
                 for w, h in ((m.w_hi[slot], c.h_hi), (m.w_hi[slot], c.h_lo), (m.w_lo[slot], c.h_hi))]
        for e, (w, h, k) in enumerate(terms):
            mm = t_.matmul(c.ps[:, bank + j % 2, :], w[:, at + k * P:at + (k + 1) * P], h[:, k, tok],
                           start=(e == 0), stop=(e == len(terms) - 1))
    if expert_of is not None:
        mm = t_.matmul(c.ps[:, 4 + j % 2, :], expert_of[:, :], cw_rows[:, tok], start=True, stop=True)
    mm.then_inc(m.up_done, 1)


def mlp_down(t_, c, m, n, j, slot, first, last):
    t_.wait_ge(m.act_lo_done, n + 1)
    at = 2 * KD * P
    for dh in range(KD):
        terms = ((m.w_hi[slot], m.act_hi), (m.w_hi[slot], m.act_lo), (m.w_lo[slot], m.act_hi))
        for e, (w, a) in enumerate(terms):
            mm = t_.matmul(c.ps[:, 6 + dh, :], w[:, at + dh * P:at + (dh + 1) * P], a[:, j % 4, :],
                           start=(first and e == 0), stop=(last and e == 2))
    mm.then_inc(m.down_done, 1)


def mlp_silu(a, c, m, n, j, first):
    a.wait_ge(m.up_done, n + 1)
    if not first:
        a.wait_ge(m.act_done, n - 1)
    a.activation(m.silu[:, j % 2, :], c.ps[:, j % 2, :], ACT.Silu).then_inc(m.silu_done, 1)


def mlp_hi(a, m, n, j, ready, first):
    a.wait_ge(ready, n + 1)
    if not first:
        a.wait_ge(m.down_done, n - 3)
    a.activation(m.act_hi[:, j % 4, :], m.act[:, j % 2, :], ACT.Copy).then_inc(m.act_hi_done, 1)


def mlp_lo(g, m, n, j):
    g.wait_ge(m.act_hi_done, n + 1)
    g.tensor_tensor(m.act_lo[:, j % 4, :], m.act[:, j % 2, :], m.act_hi[:, j % 4, :].bitcast(F32), ALU.subtract)\
        .then_inc(m.act_lo_done, 1)


def mlp_act(v, c, m, n, j, first, weigh):
    v.wait_ge(m.silu_done, n + 1)
    if not first:
        v.wait_ge(m.act_lo_done, n - 1)
    v.tensor_tensor(m.act[:, j % 2, :], m.silu[:, j % 2, :], c.ps[:, 2 + j % 2, :], ALU.mult).then_inc(m.act_done, 1)
    if weigh:
        v.wait_ge(m.act_done, n + 1)
        v.tensor_tensor(m.act[:, j % 2, :], m.act[:, j % 2, :], c.ps[:, 4 + j % 2, :], ALU.mult)\
            .then_inc(m.weighted, 1)


def add_back_phase(nc, c, mod, name):
    with ExitStack() as stack:
        def sem(n):
            return new_semaphore(nc, c, stack, name + n)

        gated, turned, added = sem("gated"), sem("turned"), sem("added")
        block = stack.enter_context(nc.Block())

        @block.scalar
        def _(a):
            with a.Fori(0, B) as b:
                for dh in range(KD):
                    y = c.yT[:, dh, bass.ds(b * T, T)]
                    a.activation(y, y, ACT.Copy, scale=mod[:, KD * GATE_B + dh, bass.ds(b, 1)]).then_inc(gated, 1)

        @block.tensor
        def _(t_):
            for b in range(B):
                t_.wait_ge(gated, KD * (b + 1))
                if b >= 4:
                    t_.wait_ge(added, b - 3)
                for q in range(BT):
                    for dh in range(KD):
                        at = b * T + q * P
                        mm = t_.transpose(c.ps[:, b % 4, q * D + dh * P:q * D + (dh + 1) * P],
                                          c.yT[:, dh, at:at + P], c.ident)
                mm.then_inc(turned, 1)

        @block.vector
        def _(v):
            for b in range(B):
                v.wait_ge(turned, b + 1)
                x = flat(c.x[:, BT * b:BT * b + BT, :])
                v.tensor_tensor(x, x, c.ps[:, b % 4, :], ALU.add).then_inc(added, 1)


def route(nc, c, args):
    with ExitStack() as stack:
        def sb(name, shape, dt):
            return stack.enter_context(nc.sbuf_tensor("r_" + name, shape, dt))

        def sem(name):
            return new_semaphore(nc, c, stack, "r_" + name)

        s = ln_buffers(sb, sem, c, c.mod[0], SHIFT_B, SCALE_B)
        gate_w = sb("gate_w", [P, KD, E], F32)
        e_raw = sb("e_raw", [P, PT_, E], F32)
        top = sb("top", [P, PT_, 8], F32)
        neg_top = sb("neg_top", [P, PT_], F32)
        picked = sb("picked", [P, PT_, E], F32)
        total = sb("total", [P, PT_], F32)
        inv_total = sb("inv_total", [P, PT_], F32)
        share = sb("share", [P, PT_, E], F32)
        kept = sb("kept", [P, PT_, E], F32)
        cw = sb("cw", [P, PT_, 2 * E], F32)
        names = ("gate_in", "logits_done", "top_logit", "neg_done", "exped", "totaled", "inverted", "shared", "topped",
                 "cut", "matched", "masked", "cw_full", "cw_hi", "cw_lo", "cw_turned", "cw_out")
        (gate_in, logits_done, top_logit, neg_done, exped, totaled, inverted, shared, topped, cut, matched, masked,
         cw_full, cw_hi, cw_lo, cw_turned, cw_out) = (sem(n) for n in names)
        block = stack.enter_context(nc.Block())

        @block.sync
        def _(sp):
            sp.dma_start(gate_w[:], args.gate_w).then_inc(gate_in, 16)

        @block.tensor
        def _(t_):
            t_.wait_ge(gate_in, 16)
            with t_.Fori(0, PAIRS) as i:
                ln_tensor(t_, s, i)
                t_.wait_ge(s.ln_h, 2 * KD * (i + 1))
                for t in range(PT_):
                    for k in range(KD):
                        mm = t_.matmul(c.ps[:, 2, t * E:(t + 1) * E], s.h[:, k, t * P:(t + 1) * P], gate_w[:, k, :],
                                       start=(k == 0), stop=(k == KD - 1))
                mm.then_inc(logits_done, 1)
                t_.wait_ge(cw_lo, i + 1)
                for t in range(PT_):
                    mm = t_.transpose(c.ps[0:2 * E, 3, t * P:(t + 1) * P], cw[:, t, :], c.ident)
                mm.then_inc(cw_turned, 1)

        @block.scalar
        def _(a):
            with a.Fori(0, PAIRS) as i:
                ln_scalar(a, s, i)
                a.wait_ge(neg_done, i + 1)
                for t in range(PT_):
                    a.activation(e_raw[:, t, :], c.ps[:, 2, t * E:(t + 1) * E], ACT.Exp,
                                 bias=neg_top[:, t:t + 1]).then_inc(exped, 1)
                a.wait_ge(cw_turned, i + 1)
                a.activation(c.cw_rows[:, bass.ds(i * NP, NP)], c.ps[0:2 * E, 3, :], ACT.Copy).then_inc(cw_out, 1)

        @block.gpsimd
        def _(g):
            with g.Fori(0, PAIRS) as i:
                ln_gpsimd_rstd(g, s, i)
                ln_gpsimd_split(g, s, i, lambda half: c.h_hi[:, half, bass.ds(i * NP, NP)],
                                lambda half: c.h_lo[:, half, bass.ds(i * NP, NP)])

        @block.vector
        def _(v):
            with v.Fori(0, PAIRS) as i:
                ln_vector(v, s, i)
                v.wait_ge(logits_done, i + 1)
                v.tensor_reduce(neg_top[:], c.ps[:, 2, 0:PT_ * E].rearrange("p (t e) -> p t e", e=E), AX.X, ALU.max)\
                    .then_inc(top_logit, 1)
                v.wait_ge(top_logit, i + 1)
                v.tensor_scalar(neg_top[:], neg_top[:], -1.0, None, ALU.mult).then_inc(neg_done, 1)
                v.wait_ge(exped, PT_ * (i + 1))
                v.tensor_reduce(total[:], e_raw[:], AX.X, ALU.add).then_inc(totaled, 1)
                v.wait_ge(totaled, i + 1)
                v.reciprocal(inv_total[:], total[:]).then_inc(inverted, 1)
                v.wait_ge(inverted, i + 1)
                v.tensor_tensor(share[:], e_raw[:], inv_total[:].unsqueeze(2).to_broadcast([P, PT_, E]), ALU.mult)\
                    .then_inc(shared, 1)
                v.wait_ge(shared, i + 1)
                v.sem_inc(s.passed)
                for t in range(PT_):
                    v.max(top[:, t, :], share[:, t, :]).then_inc(topped, 1)
                v.wait_ge(topped, PT_ * (i + 1))
                v.memset(top[:, :, TOPK:8], -2.0).then_inc(cut, 1)
                v.wait_ge(cut, i + 1)
                v.sem_inc(s.passed)
                for t in range(PT_):
                    v.match_replace(picked[:, t, :], top[:, t, :], share[:, t, :], -1.0).then_inc(matched, 1)
                v.wait_ge(matched, PT_ * (i + 1))
                v.tensor_scalar(kept[:], picked[:], 0.0, None, ALU.is_lt).then_inc(masked, 1)
                v.wait_ge(masked, i + 1)
                v.tensor_tensor(kept[:], kept[:], share[:], ALU.mult).then_inc(cw_full, 1)
                v.wait_ge(cw_full, i + 1)
                v.tensor_copy(cw[:, :, 0:E].bitcast(F32R), kept[:]).then_inc(cw_hi, 1)
                v.wait_ge(cw_hi, i + 1)
                v.tensor_tensor(cw[:, :, E:2 * E].bitcast(F32R), kept[:], cw[:, :, 0:E], ALU.subtract)\
                    .then_inc(cw_lo, 1)


def experts(nc, c, args):
    TB = TOKENS // NP
    STEPS = 2 * TB
    CHUNKS = MOE_TILES // 2
    LOOP = CHUNKS // 2
    with ExitStack() as stack:
        def sb(name, shape, dt):
            return stack.enter_context(nc.sbuf_tensor("m_" + name, shape, dt))

        def sem(name):
            return new_semaphore(nc, c, stack, "m_" + name)

        m = mlp_buffers(sb, sem, 4)
        raw = sb("raw", [P, 4, WT], F32)
        which = [sb(f"which{j}", [2 * E, P], F32R) for j in range(4)]
        which_raw = sb("which_raw", [2 * E, MOE_TILES * P], F32)
        which_in, which_done, y_cleared = sem("which_in"), sem("which_done"), sem("y_cleared")
        block = stack.enter_context(nc.Block())

        def slot_of(j):
            return 2 * (j // STEPS % 2) + j % 2

        @block.sync
        def _(sp):
            def load(chunk, par):
                sp.dma_start(raw[:, 2 * par:2 * par + 2, :],
                             args.moe_w[bass.ds(2 * chunk, 2), :, :].rearrange("t p w -> p t w"))\
                    .then_inc(m.raw_in[par], 16)

            sp.dma_start(which_raw[:], args.expert_of).then_inc(which_in, 16)
            load(0, 0)
            load(1, 1)
            with sp.Fori(0, LOOP - 1) as i:
                for par in range(2):
                    sp.wait_ge(m.w_lo_done, 2 * (2 * i + par + 1))
                    load(2 * i + par + 2, par)
            sp.wait_ge(m.w_lo_done, 2 * (2 * LOOP - 1))
            load(2 * LOOP, 0)

        @block.tensor
        def _(t_):
            def step_up(i, j, first=False):
                n = 2 * STEPS * i + j
                jj = j % (2 * STEPS)
                if jj % STEPS < 2:
                    tile = 4 * i + 2 * (j // STEPS) + jj % 2
                    t_.wait_ge(m.w_lo_done, tile + 1)
                    t_.wait_ge(which_done, tile + 1)
                mlp_up(t_, c, m, n, j, slot_of(jj), jj % STEPS // 2, first, which[slot_of(jj)], c.cw_rows)

            step_up(0, 0, first=True)
            step_up(0, 1, first=True)
            t_.wait_ge(y_cleared, 1)
            t_.sem_inc(m.y_added, 1)
            with t_.Fori(0, LOOP) as i:
                for j in range(2 * STEPS):
                    n = 2 * STEPS * i + j
                    if j % 2 == 0:
                        t_.wait_ge(m.y_added, STEPS * i + j // 2 + 1)
                    mlp_down(t_, c, m, n, j, slot_of(j), j % 2 == 0, j % 2 == 1)
                    step_up(i, j + 2)
            for j in range(STEPS):
                if j % 2 == 0:
                    t_.wait_ge(m.y_added, STEPS * LOOP + j // 2 + 1)
                mlp_down(t_, c, m, 2 * STEPS * LOOP + j, j, slot_of(j), j % 2 == 0, j % 2 == 1)
                if j + 2 < STEPS:
                    step_up(LOOP, j + 2)

        @block.scalar
        def _(a):
            def split(k, par, first):
                chunk = 2 * k + par
                a.wait_ge(m.raw_in[par], 16 * (k + 1))
                if not first:
                    a.wait_ge(m.down_done, STEPS * (chunk - 1))
                for t in range(2):
                    a.activation(m.w_hi[2 * par + t][:], raw[:, 2 * par + t, :], ACT.Copy).then_inc(m.w_hi_done, 1)
                for t in range(2):
                    col = (2 * chunk + t) * P
                    a.activation(which[2 * par + t][:, :], which_raw[:, bass.ds(col, P)], ACT.Copy)\
                        .then_inc(which_done, 1)

            def step(i, j, first0=False, first1=False):
                n = 2 * STEPS * i + j
                mlp_silu(a, c, m, n, j, first0)
                mlp_hi(a, m, n, j, m.weighted, first1)

            a.wait_ge(which_in, 16)
            split(0, 0, True)
            split(0, 1, True)
            for j in range(4):
                step(0, j, first0=j < 2, first1=True)
            for j in range(4, 2 * STEPS):
                step(0, j)
                if j == STEPS + 3:
                    split(1, 0, False)
            with a.Fori(1, LOOP) as i:
                for j in range(2 * STEPS):
                    step(i, j)
                    if j == 3:
                        split(i, 1, False)
                    if j == STEPS + 3:
                        split(i + 1, 0, False)
            for j in range(STEPS):
                step(LOOP, j)

        @block.gpsimd
        def _(g):
            def split(k, par):
                chunk = 2 * k + par
                for t in range(2):
                    g.wait_ge(m.w_hi_done, 2 * chunk + t + 1)
                    g.tensor_tensor(m.w_lo[2 * par + t][:], raw[:, 2 * par + t, :],
                                    m.w_hi[2 * par + t][:].bitcast(F32), ALU.subtract).then_inc(m.w_lo_done, 1)

            split(0, 0)
            split(0, 1)
            for j in range(2 * STEPS):
                mlp_lo(g, m, j, j)
                if j == STEPS + 3:
                    split(1, 0)
            with g.Fori(1, LOOP) as i:
                for j in range(2 * STEPS):
                    mlp_lo(g, m, 2 * STEPS * i + j, j)
                    if j == 3:
                        split(i, 1)
                    if j == STEPS + 3:
                        split(i + 1, 0)
            for j in range(STEPS):
                mlp_lo(g, m, 2 * STEPS * LOOP + j, j)

        @block.vector
        def _(v):
            def add_y(n, tb):
                v.wait_ge(m.down_done, n + 1)
                y = c.yT[:, :, tb * NP:(tb + 1) * NP]
                v.tensor_tensor(y, y, c.ps[:, 6:8, :], ALU.add).then_inc(m.y_added, 1)

            def step(i, j, first=False, first_y=False):
                n = 2 * STEPS * i + j
                mlp_act(v, c, m, n, j, first, weigh=True)
                if j % 2 == 0 and not first_y:
                    add_y(n - 1, (j // 2 - 1) % TB)

            v.memset(c.yT[:], 0.0).then_inc(y_cleared, 1)
            v.wait_ge(y_cleared, 1)
            for j in range(2 * STEPS):
                step(0, j, first=j < 2, first_y=j == 0)
            with v.Fori(1, LOOP) as i:
                for j in range(2 * STEPS):
                    step(i, j)
            for j in range(STEPS):
                step(LOOP, j)
            add_y(2 * STEPS * LOOP + STEPS - 1, TB - 1)


def attention1(nc, c, args):
    with ExitStack() as stack:
        def sb(name, shape, dt):
            return stack.enter_context(nc.sbuf_tensor("a1_" + name, shape, dt))

        def sem(name):
            return new_semaphore(nc, c, stack, "a1_" + name)

        KV = 4
        VW = 2 * HW
        FT = HEADS * VW // P
        VC = VW + 1
        NB = 3
        s = ln_buffers(sb, sem, c, c.mod[1], SHIFT_A, SCALE_A)
        s.psflat = c.psflat
        q = qkv_buffers(sb, sem, 2 * HEADS, 2 * KV, KV, VW)
        raw = sb("w_raw", [P, KD * 768 + FT * D], F32)
        w_hi_all = sb("w_hi", [P, KD * 768 + FT * D], F32R)
        w_lo_all = sb("w_lo", [P, KD * 768 + FT * D], F32R)

        def qkv_w(w):
            return w[:, 0:KD * 768].rearrange("p (k n) -> p k n", k=KD)

        def wo_w(w):
            return w[:, KD * 768:].rearrange("p (f n) -> p f n", f=FT)

        block_max = sb("block_max", [P, 2 * HEADS, NB], F32)
        maxima = sb("maxima", [P, BT, 2 * HEADS], F32)
        max_rows = sb("max_rows", [2 * HEADS, T], F32R)
        probs = sb("probs", [P, 3, 2, NB * P], F32)
        denom = sb("denom", [P, 2, BT * 2 * 2], F32)
        parts = sb("parts", [P, 2, BT * 2, 2, VW], F32)
        heads_out = [sb(f"heads_out{b}", [P, BT, HEADS, VW], F32) for b in range(2)]
        squares = sb("squares", [P, BT, HEADS, VW], F32)
        sums = sb("sums", [P, HEADS], F32)
        sq_sums = sb("sq_sums", [P, HEADS], F32)
        var = sb("var", [P, HEADS], F32)
        rstd = sb("rstd", [P, HEADS], F32)
        o_full = sb("o_full", [P, FT, T], F32)
        o = Parts()
        o.wo_hi = wo_w(w_hi_all)
        o.wo_lo = wo_w(w_lo_all)
        o.mod = c.mod[1]
        o.o_hi = sb("o_hi", [P, FT, T], F32R)
        o.o_lo = sb("o_lo", [P, FT, T], F32R)
        o.y = sb("y", [P, KD, T], F32)
        o.o_hi_done = sem("o_hi_done")
        o.o_lo_done = sem("o_lo_done")
        o.y_done = sem("y_done")
        o.y_gated = sem("y_gated")
        o.y_turned = sem("y_turned")
        o.x_added = sem("x_added")
        w_in, w_hi_done, w_lo_done = sem("w_in"), sem("w_hi_done"), sem("w_lo_done")
        scores_done, max_done, max_joined, max_turned, max_rows_ready, max_in = (
            sem(n) for n in ("scores_done", "max_done", "max_joined", "max_turned", "max_rows_ready", "max_in"))
        keyed_done, exp_done, cut_done, pv_done, denom_done, parted, out_ready = (
            sem(n) for n in ("keyed_done", "exp_done", "cut_done", "pv_done", "denom_done", "parted", "out_ready"))
        summed, mean_done, centred, squared, sq_summed, var_done, var_eps, rstd_done, normed, out_turned, o_affine = (
            sem(n) for n in ("summed", "mean_done", "centred", "squared", "sq_summed", "var_done", "var_eps",
                             "rstd_done", "normed", "out_turned", "o_affine"))
        proj = out_project(c, s, o, FT)
        rope = Parts()
        rope.width = 16
        rope.first = lambda a: a[:, :, 0:16:2]
        rope.second = lambda a: a[:, :, 1:16:2]
        rope.cos = c.table(C_COS1, 16)
        rope.sin_a = c.table(C_SIN1A, 8)
        rope.sin_b = c.table(C_SIN1B, 8)
        ps = c.ps
        PVG = HEADS // 2
        block = stack.enter_context(nc.Block())

        def pv_bank(grp):
            return ps[:, 6 + grp % 2, 0:BT * 4 * VC].rearrange("p (m w) -> p m w", w=VC)

        @block.tensor
        def _(t_):
            t_.wait_ge(q.stacks_set, 5)
            t_.wait_ge(w_lo_done, 1)

            def row_scores(i, b, h):
                for half in range(2):
                    n = 2 * HEADS * (2 * i + b) + 2 * h + half
                    if h >= 1:
                        t_.wait_ge(max_done, n - 1)
                    if h == 0 and half == 0 and b == 1:
                        t_.wait_ge(max_rows_ready, 2 * i + 1)
                    base = 64 * half
                    qr, kr = q.q_rows[base:base + ROWS, b, h, :], q.k_rows[base:base + ROWS, b, h // KV, :]
                    t_.matmul(ps[:, half, 0:T], qr[:, P:T], kr[:, 0:T], start=True, stop=False, skip_group_check=True)
                    t_.matmul(ps[:, half, T:T + P], qr[:, 0:P], kr[:, 0:P], start=False, stop=False,
                              skip_group_check=True)
                    t_.matmul(ps[:, half, P:P + T], c.ident_bf[:, :], c.mask_bf[:, :], start=False, stop=True,
                              skip_group_check=True).then_inc(scores_done, 1)

            def turn_maxima(i, b):
                t_.wait_ge(max_joined, 2 * (2 * i + b + 1))
                for qt in range(BT):
                    mm = t_.transpose(ps[0:2 * HEADS, 0, qt * P:(qt + 1) * P], maxima[:, qt, :], c.ident)
                mm.then_inc(max_turned, 1)

            def key_scores(i, b, h):
                n = HEADS * (2 * i + b) + h
                if h == 0:
                    t_.wait_ge(max_in, 32 * (2 * i + b + 1))
                if h >= 2 or b == 1:
                    t_.wait_ge(exp_done, n - 1)
                for half in range(2):
                    base, bank = 64 * half, 2 + 2 * (h % 2) + half
                    qr, kr = q.q_rows[base:base + ROWS + 1, b, h, :], q.k_rows[base:base + ROWS + 1, b, h // KV, :]
                    t_.matmul(ps[:, bank, 0:T], kr[:, 0:P], qr[:, 0:T], start=True, stop=False, skip_group_check=True)
                    mm = t_.matmul(ps[:, bank, T:T + P], kr[:, P:T], qr[:, P:T], start=False, stop=True,
                                   skip_group_check=True)
                mm.then_inc(keyed_done, 1)

            def weigh(i, b, h, slot):
                n = HEADS * (2 * i + b) + h
                t_.wait_ge(cut_done, n + 1)
                grp = h // 2
                if h % 2 == 0 and (grp >= 2 or b == 1):
                    t_.wait_ge(parted, 2 * (PVG * (2 * i + b) + grp - 1))
                out = pv_bank(grp)
                for half in range(2):
                    for qt in range(BT):
                        at = (h % 2) * BT * 2 + qt * 2 + half
                        for kt in range(qt + 1):
                            blk = (0, 1)[qt] if kt == 0 else 2
                            mm = t_.matmul(out[:, at, :], probs[:, slot, half, blk * P:(blk + 1) * P],
                                           q.v[:, BT * b + kt, h // KV, :], start=(kt == 0), stop=(kt == qt))
                mm.then_inc(pv_done, 1)

            def group_mean(i, b, bank, of, ready, done, wait_to):
                t_.wait_ge(ready, wait_to)
                t_.matmul(ps[:, bank, 0:HEADS], c.mean_of[:, :], of[:, :], start=True, stop=True).then_inc(done, 1)

            def turn_out(i, b):
                t_.wait_ge(normed, 2 * i + b + 1)
                for f in range(FT):
                    for qt in range(BT):
                        at = (f % 2) * T + qt * P
                        mm = t_.transpose(ps[:, f // 2, at:at + P],
                                          heads_out[b][:, qt, 4 * f:4 * f + 4, :].rearrange("p h w -> p (h w)"), c.ident)
                mm.then_inc(out_turned, 1)

            def tail(i, b, stage):
                if stage == 0:
                    group_mean(i, b, 0, sums, summed, mean_done, 2 * i + b + 1)
                if stage == 1:
                    group_mean(i, b, 1, sq_sums, sq_summed, var_done, 2 * i + b + 1)
                if stage == 2:
                    turn_out(i, b)
                if stage == 3:
                    proj.tensor(t_, i, b, 1)
                if stage == 4:
                    proj.tensor_back(t_, i, b)

            with t_.Fori(0, PAIRS) as i:
                ln_tensor(t_, s, i)
                qkv_tensor(t_, s, q, qkv_w(w_hi_all), qkv_w(w_lo_all), i)
                t_.wait_ge(q.q_rows_ready, q.q_rounds * (PT_ * i + PT_))
                t_.wait_ge(q.k_rows_ready, q.k_rounds * (PT_ * i + PT_))
                for h in range(HEADS):
                    row_scores(i, 0, h)
                turn_maxima(i, 0)
                for h in range(HEADS + 2):
                    if h < HEADS:
                        row_scores(i, 1, h)
                        key_scores(i, 0, h)
                    if h >= 2:
                        weigh(i, 0, h - 2, (h - 2) % 3)
                turn_maxima(i, 1)
                for h in range(HEADS + 2):
                    if h < HEADS:
                        key_scores(i, 1, h)
                    if h == 2:
                        t_.wait_ge(max_rows_ready, 2 * i + 2)
                        tail(i, 0, 0)
                    if h in (6, 9, 12, 15):
                        tail(i, 0, (6, 9, 12, 15).index(h) + 1)
                    if h >= 2:
                        weigh(i, 1, h - 2, (HEADS + h - 2) % 3)
                t_.wait_ge(o.x_added, 2 * i + 1)
                for stage in range(5):
                    tail(i, 1, stage)

        @block.scalar
        def _(a):
            a.wait_ge(w_in, 16)
            a.activation(w_hi_all[:], raw[:], ACT.Copy).then_inc(w_hi_done, 1)

            def exps(i, b, h, slot):
                n = HEADS * (2 * i + b) + h
                a.wait_ge(keyed_done, n + 1)
                if h >= 3 or b == 1:
                    a.wait_ge(pv_done, n - 2)
                a.activation(probs[:, slot, :, :], ps[:, 2 + 2 * (h % 2):4 + 2 * (h % 2), 0:NB * P], ACT.Exp,
                             scale=SCALE).then_inc(exp_done, 1)

            def max_out(i, b):
                a.wait_ge(max_turned, 2 * i + b + 1)
                if b == 1:
                    a.wait_ge(max_in, 32 * (2 * i + 1))
                a.activation(max_rows[:, :], ps[0:2 * HEADS, 0, 0:T], ACT.Copy).then_inc(max_rows_ready, 1)

            def square(i, b):
                a.wait_ge(centred, 2 * i + b + 1)
                a.activation(squares[:].rearrange("p q h w -> p (q h w)"),
                             heads_out[b][:].rearrange("p q h w -> p (q h w)"), ACT.Square).then_inc(squared, 1)

            def affine(i, b):
                a.wait_ge(out_turned, 2 * i + b + 1)
                for f in range(FT):
                    a.activation(o_full[:, f, :], ps[:, f // 2, (f % 2) * T:(f % 2 + 1) * T], ACT.Identity,
                                 scale=c.gn[:, f:f + 1], bias=c.gn[:, FT + f:FT + f + 1]).then_inc(o_affine, 1)

            a.wait_ge(q.stacks_set, 5)
            with a.Fori(0, PAIRS) as i:
                ln_scalar(a, s, i)
                qkv_scalar(a, s, q, i, plain=False)
                max_out(i, 0)
                for h in range(HEADS):
                    exps(i, 0, h, h % 3)
                max_out(i, 1)
                for h in range(HEADS):
                    exps(i, 1, h, (HEADS + h) % 3)
                    if h == 3:
                        square(i, 0)
                    if h == 10:
                        affine(i, 0)
                    if h == 13:
                        proj.scalar_gate(a, i, 0)
                square(i, 1)
                affine(i, 1)
                proj.scalar_gate(a, i, 1)

        @block.vector
        def _(v):
            def max_of(i, b, n):
                v.wait_ge(scores_done, 2 * HEADS * (2 * i + b) + n + 1)
                col = HEADS * (n % 2) + n // 2
                v.tensor_reduce(block_max[:, col, :], ps[:, n % 2, 0:NB * P].rearrange("p (c k) -> p c k", c=NB),
                                AX.X, ALU.max).then_inc(max_done, 1)

            def join(i, b):
                v.wait_ge(max_done, 2 * HEADS * (2 * i + b + 1))
                if b == 1:
                    v.wait_ge(max_turned, 2 * i + 1)
                v.tensor_tensor(maxima[:, 1, :], block_max[:, :, 0], block_max[:, :, 1], ALU.max)\
                    .then_inc(max_joined, 1)
                v.tensor_copy(maxima[:, 0, :], block_max[:, :, 2]).then_inc(max_joined, 1)

            def combine(i, b, grp):
                n = PVG * (2 * i + b) + grp
                v.wait_ge(pv_done, 2 * (n + 1))
                src = pv_bank(grp)
                v.reciprocal(denom[:, grp % 2, :], src[:, :, VW]).then_inc(denom_done, 1)
                v.wait_ge(denom_done, n + 1)
                v.tensor_tensor(parts[:, grp % 2, :, :, :].rearrange("p a b w -> p (a b) w"), src[:, :, 0:VW],
                                denom[:, grp % 2, :].unsqueeze(2).to_broadcast([P, 4 * BT, VW]), ALU.mult)\
                    .then_inc(parted, 2)
                v.wait_ge(parted, 2 * (n + 1))
                for hh in range(2):
                    at = parts[:, grp % 2, BT * hh:BT * hh + BT, :, :]
                    v.scalar_tensor_tensor(heads_out[b][:, :, 2 * grp + hh, :], at[:, :, 1, :], c.neg_lam[:, 0:1],
                                           at[:, :, 0, :], ALU.mult, ALU.add).then_inc(out_ready, 1)

            def per_head(ap):
                return ap[:].rearrange("p q h w -> p h q w")

            def each(ap):
                return ap.unsqueeze(1).unsqueeze(3).to_broadcast([P, BT, HEADS, VW])

            def norm_a(i, b):
                n = 2 * i + b
                v.wait_ge(out_ready, HEADS * (n + 1))
                v.tensor_reduce(sums[:], per_head(heads_out[b]), AX.XY, ALU.add).then_inc(summed, 1)

            def norm_b(i, b):
                n = 2 * i + b
                v.wait_ge(mean_done, n + 1)
                v.tensor_tensor(heads_out[b][:], heads_out[b][:], each(ps[:, 0, 0:HEADS]), ALU.subtract)\
                    .then_inc(centred, 1)

            def norm_c(i, b):
                n = 2 * i + b
                v.wait_ge(squared, n + 1)
                v.tensor_reduce(sq_sums[:], per_head(squares), AX.XY, ALU.add).then_inc(sq_summed, 1)

            def norm_d(i, b):
                n = 2 * i + b
                v.wait_ge(var_done, n + 1)
                v.tensor_scalar(var[:], ps[:, 1, 0:HEADS], GN_EPS, None, ALU.add).then_inc(var_eps, 1)
                v.wait_ge(rstd_done, n + 1)
                v.tensor_tensor(heads_out[b][:], heads_out[b][:], each(rstd[:, :]), ALU.mult).then_inc(normed, 1)

            v.wait_ge(q.stacks_set, 5)
            with v.Fori(0, PAIRS) as i:
                ln_vector(v, s, i)
                qkv_vector(v, s, q, i, rope, plain=False)
                for n in range(2 * HEADS):
                    max_of(i, 0, n)
                join(i, 0)
                for n in range(2 * HEADS):
                    max_of(i, 1, n)
                    if n % 4 == 3 and n >= 7:
                        combine(i, 0, n // 4 - 1)
                join(i, 1)
                combine(i, 0, PVG - 1)
                norm_a(i, 0)
                norm_b(i, 0)
                combine(i, 1, 0)
                norm_c(i, 0)
                combine(i, 1, 1)
                norm_d(i, 0)
                for grp in range(2, PVG - 1):
                    combine(i, 1, grp)
                proj.vector_add(v, i, 0)
                combine(i, 1, PVG - 1)
                norm_a(i, 1)
                norm_b(i, 1)
                norm_c(i, 1)
                norm_d(i, 1)
                proj.vector_add(v, i, 1)

        @block.gpsimd
        def _(g):
            def cut(i, b, h, slot):
                g.wait_ge(exp_done, HEADS * (2 * i + b) + h + 1)
                g.sem_inc(s.passed)
                for half in range(2):
                    at = probs[:, slot, half, :].rearrange("p (c n) -> p c n", c=NB)[:, 0:NB:2, :]
                    ins = g.affine_select(out=at, in_=at, compare_op=ALU.is_ge, fill=0.0, base=0,
                                          pattern=[[0, 2], [1, P]], channel_multiplier=-1)
                ins.then_inc(cut_done, 1)

            def split_out(i, b):
                n = 2 * i + b
                g.wait_ge(o_affine, FT * (n + 1))
                g.sem_inc(s.passed)
                g.tensor_copy(o.o_hi[:], o_full[:]).then_inc(o.o_hi_done, 1)
                g.wait_ge(o.o_hi_done, n + 1)
                g.tensor_tensor(o.o_lo[:], o_full[:], o.o_hi[:].bitcast(F32), ALU.subtract).then_inc(o.o_lo_done, 1)

            def group_rstd(i, b):
                g.wait_ge(var_eps, 2 * i + b + 1)
                g.tensor_tensor(rstd[:], var[:], c.minus_half[:, 0:HEADS], ALU.pow).then_inc(rstd_done, 1)

            g.wait_ge(w_hi_done, 1)
            g.tensor_tensor(w_lo_all[:], raw[:], w_hi_all[:].bitcast(F32), ALU.subtract).then_inc(w_lo_done, 1)
            qkv_gpsimd_prepare(g, q)
            g.wait_ge(q.stacks_set, 5)
            with g.Fori(0, PAIRS) as i:
                ln_gpsimd_rstd(g, s, i)
                ln_gpsimd_split(g, s, i, lambda half: q.h_hi[:, half, :], lambda half: q.h_lo[:, half, :])
                qkv_gpsimd(g, s, q, i, plain=False)
                for h in range(HEADS):
                    cut(i, 0, h, h % 3)
                for h in range(HEADS):
                    cut(i, 1, h, (HEADS + h) % 3)
                    if h == 5:
                        group_rstd(i, 0)
                    if h == 11:
                        split_out(i, 0)
                group_rstd(i, 1)
                split_out(i, 1)

        @block.sync
        def _(sp):
            sp.dma_start(raw[:], args.w1).then_inc(w_in, 16)
            with sp.Fori(0, PAIRS) as i:
                for b in range(2):
                    sp.wait_ge(max_rows_ready, 2 * i + b + 1)
                    for half in range(2):
                        row = 64 * half + ROWS
                        sp.dma_start(q.q_rows[row:row + 1, b, :, :].bitcast(F32),
                                     max_rows[HEADS * half:HEADS * (half + 1), :].bitcast(F32))\
                            .then_inc(max_in, 16)
            sp.wait_ge(max_in, 32 * B)


def norm_all(nc, c):
    with ExitStack() as stack:
        def sb(name, shape, dt):
            return stack.enter_context(nc.sbuf_tensor("n_" + name, shape, dt))

        def sem(name):
            return new_semaphore(nc, c, stack, "n_" + name)

        s = ln_buffers(sb, sem, c, c.mod[1], SHIFT_B, SCALE_B)
        block = stack.enter_context(nc.Block())

        @block.tensor
        def _(t_):
            with t_.Fori(0, PAIRS) as i:
                t_.wait_ge(s.ln_xn, PT_ * i + PT_)
                ln_tensor(t_, s, i)

        @block.scalar
        def _(a):
            with a.Fori(0, PAIRS) as i:
                ln_scalar(a, s, i)

        @block.gpsimd
        def _(g):
            with g.Fori(0, PAIRS) as i:
                ln_gpsimd_rstd(g, s, i)
                ln_gpsimd_split(g, s, i, lambda half: c.h_hi[:, half, bass.ds(i * NP, NP)],
                                lambda half: c.h_lo[:, half, bass.ds(i * NP, NP)])

        @block.vector
        def _(v):
            with v.Fori(0, PAIRS) as i:
                ln_vector(v, s, i)
                v.wait_ge(s.ln_lo, KD * (i + 1))


def feed_forward(nc, c, args):
    with ExitStack() as stack:
        def sb(name, shape, dt):
            return stack.enter_context(nc.sbuf_tensor("f_" + name, shape, dt))

        def sem(name):
            return new_semaphore(nc, c, stack, "f_" + name)

        m = mlp_buffers(sb, sem, FFN_TILES)
        raw = sb("raw", [P, 2, WT], F32)
        N = FFN_TILES
        block = stack.enter_context(nc.Block())

        @block.sync
        def _(sp):
            for t in range(N):
                if t >= 2:
                    sp.wait_ge(m.w_lo_done, t - 1)
                sp.dma_start(raw[:, t % 2, :], args.ffn_w[t, :, :]).then_inc(m.raw_in[t % 2], 16)

        @block.tensor
        def _(t_):
            steps = N * (TOKENS // NP)

            def up(n):
                if n < N:
                    t_.wait_ge(m.w_lo_done, n + 1)
                mlp_up(t_, c, m, n, n, n % N, n // N, n < 2)

            up(0)
            up(1)
            for n in range(steps):
                if n % N == 0 and n:
                    t_.wait_ge(m.y_added, n // N)
                mlp_down(t_, c, m, n, n, n % N, n % N == 0, n % N == N - 1)
                if n + 2 < steps:
                    up(n + 2)

        @block.scalar
        def _(a):
            def split(t):
                a.wait_ge(m.raw_in[t % 2], 16 * (t // 2 + 1))
                a.activation(m.w_hi[t][:], raw[:, t % 2, :], ACT.Copy).then_inc(m.w_hi_done, 1)

            split(0)
            split(1)
            for n in range(N):
                mlp_silu(a, c, m, n, n, n < 2)
                mlp_hi(a, m, n, n, m.act_done, n < 4)
                if n + 2 < N:
                    split(n + 2)
            with a.Fori(1, TOKENS // NP) as i:
                for j in range(N):
                    mlp_silu(a, c, m, N * i + j, j, False)
                    mlp_hi(a, m, N * i + j, j, m.act_done, False)

        @block.gpsimd
        def _(g):
            def split(t):
                g.wait_ge(m.w_hi_done, t + 1)
                g.tensor_tensor(m.w_lo[t][:], raw[:, t % 2, :], m.w_hi[t][:].bitcast(F32), ALU.subtract)\
                    .then_inc(m.w_lo_done, 1)

            split(0)
            split(1)
            for n in range(N):
                mlp_lo(g, m, n, n)
                if n + 2 < N:
                    split(n + 2)
            with g.Fori(1, TOKENS // NP) as i:
                for j in range(N):
                    mlp_lo(g, m, N * i + j, j)

        @block.vector
        def _(v):
            def store_y(tb):
                v.wait_ge(m.down_done, N * (tb + 1))
                v.tensor_copy(c.yT[:, :, bass.ds(tb * NP, NP)], c.ps[:, 6:8, :]).then_inc(m.y_added, 1)

            for n in range(N):
                mlp_act(v, c, m, n, n, n < 2, weigh=False)
            with v.Fori(1, TOKENS // NP) as i:
                for j in range(N):
                    mlp_act(v, c, m, N * i + j, j, False, weigh=False)
                    if j == 0:
                        store_y(i - 1)
            store_y(TOKENS // NP - 1)


def clear_used(nc, c):
    numbers = sorted({s.num for s in c.used})
    with nc.Block() as block:
        @block.sync
        def _(sp):
            start = numbers[0]
            for a, b in zip(numbers, numbers[1:] + [None]):
                if b != a + 1:
                    sp.sem_clear(range(start, a + 1))
                    start = b
    c.used.clear()


def program(nc, args):
    c = Parts()
    c.used = []
    with ExitStack() as stack:
        def sb(name, shape, dt):
            return stack.enter_context(nc.sbuf_tensor(name, shape, dt))

        c.ps = stack.enter_context(nc.psum_tensor("ps", [P, 8, 512], F32))
        c.psflat = c.ps[:].rearrange("p b n -> p (b n)")
        c.x = sb("x_tokens", [P, TILES, D], F32)
        c.consts = sb("consts_t", [P, C_END], F32)
        c.ident = c.consts[:, C_ID:C_ID + P]
        c.ident_bf = sb("ident_bf", [P, P], BF16)
        c.mask_bf = sb("mask_bf", [P, 2 * P], BF16)
        c.minus_half = sb("minus_half", [P, HEADS], F32)
        c.mean_of = sb("mean_of", [P, P], F32)
        c.mod = [sb(f"mod{n}", [P, 6 * KD, B], F32) for n in range(2)]
        c.neg_lam = sb("neg_lam", [P, 1], F32)
        c.gn = sb("gn_wb", [P, 8], F32)

        def table(at, width):
            return c.consts[:, at:at + BT * width].rearrange("p (t w) -> p t w", t=BT)

        c.table = table
        with ExitStack() as inner:
            c.w0 = inner.enter_context(nc.sbuf_tensor("w0_raw", [P, KD, 1024], F32))
            c.w0_hi = inner.enter_context(nc.sbuf_tensor("w0_hi", [P, KD, 1024], F32R))
            c.w0_lo = inner.enter_context(nc.sbuf_tensor("w0_lo", [P, KD, 1024], F32R))
            setup(nc, c, args)
            attention0(nc, c)
        with ExitStack() as inner:
            c.h_hi = inner.enter_context(nc.sbuf_tensor("moe_h_hi", [P, KD, TOKENS], F32R))
            c.h_lo = inner.enter_context(nc.sbuf_tensor("moe_h_lo", [P, KD, TOKENS], F32R))
            c.cw_rows = inner.enter_context(nc.sbuf_tensor("cw_rows", [2 * E, TOKENS], F32R))
            c.yT = inner.enter_context(nc.sbuf_tensor("moe_yT", [P, KD, TOKENS], F32))
            route(nc, c, args)
            experts(nc, c, args)
            add_back_phase(nc, c, c.mod[0], "moe_")
        attention1(nc, c, args)
        clear_used(nc, c)
        with ExitStack() as inner:
            c.h_hi = inner.enter_context(nc.sbuf_tensor("ffn_h_hi", [P, KD, TOKENS], F32R))
            c.h_lo = inner.enter_context(nc.sbuf_tensor("ffn_h_lo", [P, KD, TOKENS], F32R))
            c.yT = inner.enter_context(nc.sbuf_tensor("ffn_yT", [P, KD, TOKENS], F32))
            norm_all(nc, c)
            feed_forward(nc, c, args)
            add_back_phase(nc, c, c.mod[1], "ffn_")
        out_done = stack.enter_context(nc.semaphore("out_done"))
        block = stack.enter_context(nc.Block())

        @block.sync
        def _(sp):
            for b in range(0, B, 2):
                sp.dma_start(args.out.rearrange("b (t p) d -> p (b t) d", p=P)[:, BT * b:BT * b + PT_, :],
                             c.x[:, BT * b:BT * b + PT_, :]).then_inc(out_done, 16)
            sp.wait_ge(out_done, 16 * PAIRS)


def constants():
    consts = np.zeros((P, C_END), np.float32)
    consts[:, C_ID:C_ID + P] = np.eye(P)
    above = np.where(np.arange(P)[None, :] > np.arange(P)[:, None], MASKED, 0.0)
    consts[:, C_MASK:C_MASK + 2 * P] = np.concatenate([above, above], 1)
    pos = np.arange(T, dtype=np.float32)[:, None]
    inv = (1.0 / np.float32(10000.0) ** (np.arange(0, 16, 2, dtype=np.float32) / np.float32(16))).astype(np.float32)
    ang = pos * inv[None, :]
    sin = np.sin(ang).reshape(BT, P, 8)
    cos = np.cos(ang).reshape(BT, P, 8)

    def put(at, table):
        w = table.shape[2]
        consts[:, at:at + BT * w] = table.transpose(1, 0, 2).reshape(P, BT * w)

    put(C_COS0, cos)
    put(C_SIN0A, -sin[:, :, 0:4])
    put(C_SIN0B, sin[:, :, 4:8])
    put(C_COS1, np.repeat(cos, 2, axis=2))
    put(C_SIN1A, -sin)
    put(C_SIN1B, sin)
    which = np.zeros((2 * E, MOE_TILES * P), np.float32)
    expert = np.arange(MOE_TILES * P) // MOE_D
    which[expert, np.arange(MOE_TILES * P)] = 1.0
    which[E + expert, np.arange(MOE_TILES * P)] = 1.0
    return consts, which


def kernel(**inputs):
    import numpy as _np
    import concourse.bacc as _bacc
    from concourse import mybir as _mybir
    from concourse.bass_utils import run_bass_kernel_spmd as _run

    a = {n: _np.asarray(v) for n, v in inputs.items()}
    nc = _bacc.Bacc("TRN2", target_bir_lowering=False, num_devices=1)
    arrays = {}

    def give(name, array):
        array = _np.ascontiguousarray(array)
        arrays["in_" + name] = array
        return nc.dram_tensor("in_" + name, array.shape, _mybir.dt.from_np(array.dtype), kind="ExternalInput").ap()

    def halves(m):
        return m.reshape(-1, 128, m.shape[1]).transpose(1, 0, 2)

    def tiles(gate, up, down):
        n = gate.shape[0] // 128
        def turned(w):
            return w.reshape(n, 128, 2, 128).transpose(0, 3, 2, 1).reshape(n, 128, 256)
        return _np.concatenate([turned(gate), turned(up), down.reshape(n, 128, 256)], axis=2)

    consts, which = constants()
    args = Parts()
    args.x = give("x", a["L0_attn_x"].reshape(16, 128, 256).transpose(1, 0, 2))
    args.c0 = give("c0", halves(a["L0_c"].T))
    args.c1 = give("c1", halves(a["L1_c"].T))
    args.wmod0 = give("wmod0", halves(a["L0_wmod"]))
    args.wmod1 = give("wmod1", halves(a["L1_wmod"]))
    args.w0 = give("w0", halves(_np.concatenate([a["L0_attn_wq"].T, a["L0_attn_wk"].T, a["L0_attn_wv"].T,
                                                 a["L0_attn_wo"].T], axis=1)))
    w1 = halves(_np.concatenate([a["L1_attn_Wq"], a["L1_attn_Wk"], a["L1_attn_Wv"]], axis=1)).reshape(128, -1)
    args.w1 = give("w1", _np.concatenate([w1, halves(a["L1_attn_Wo"]).reshape(128, -1)], axis=1))
    args.gate_w = give("gate_w", halves(a["L0_ffn_gate_w"].T))
    args.moe_w = give("moe_w", tiles(a["L0_ffn_w_gate"].reshape(-1, 256), a["L0_ffn_w_up"].reshape(-1, 256),
                                     a["L0_ffn_w_down"].transpose(0, 2, 1).reshape(-1, 256)))
    gate_up = a["L1_ffn_w_gate_up"]
    args.ffn_w = give("ffn_w", tiles(gate_up[0:1024], gate_up[1024:2048], a["L1_ffn_w_down"].T))
    args.gn = give("gn", _np.concatenate([a["L1_attn_gn_w"].reshape(4, 128).T, a["L1_attn_gn_b"].reshape(4, 128).T],
                                         axis=1))
    lam = _np.stack([a["L1_attn_lambda_q1"], a["L1_attn_lambda_k1"], a["L1_attn_lambda_q2"], a["L1_attn_lambda_k2"]])
    args.lam = give("lam", _np.broadcast_to(lam[None], (128, 4, 16)))
    args.consts = give("consts", consts)
    args.expert_of = give("expert_of", which)
    args.out = nc.dram_tensor("out", (8, 256, 256), _mybir.dt.float32, kind="ExternalOutput").ap()
    program(nc, args)
    r = _run(nc, [arrays], core_ids=[0])
    return r.results[0]["out"]
```

```python
from contextlib import ExitStack

import numpy as np

import concourse.bass as bass
from concourse import mybir

F32 = mybir.dt.float32
F32R = mybir.dt.float32r
BF16 = mybir.dt.bfloat16
ALU = mybir.AluOpType
ACT = mybir.ActivationFunctionType
AX = mybir.AxisListType

P = 128
B, T, D = 8, 256, 256
TOKENS = B * T
TILES = TOKENS // P
BT = T // P
KD = D // P
PAIRS = B // 2
PT_ = 2 * BT
NP = 2 * T
HW = 16
ROWS = 3 * HW
HEADS = 16
E, MOE_D, TOPK = 16, 176, 6
MOE_TILES = E * MOE_D // P
INTER = 1024
FFN_TILES = INTER // P
WT = 2 * KD * P + D
LN_EPS = 1e-5
GN_EPS = 1e-5
LAMBDA_INIT = 0.2
SCALE = 0.25
MASKED = -1e30
SHIFT_A, SCALE_A, GATE_A, SHIFT_B, SCALE_B, GATE_B = range(6)

C_ID = 0
C_MASK = C_ID + P
C_COS0 = C_MASK + 2 * P
C_SIN0A = C_COS0 + BT * 8
C_SIN0B = C_SIN0A + BT * 4
C_COS1 = C_SIN0B + BT * 4
C_SIN1A = C_COS1 + BT * 16
C_SIN1B = C_SIN1A + BT * 8
C_END = C_SIN1B + BT * 8


class Parts:
    pass


def new_semaphore(nc, c, stack, name):
    made = stack.enter_context(nc.semaphore(name))
    c.used.append(made)
    return made


def flat(ap):
    return ap.rearrange("p a b -> p (a b)")


def wait_from_one(eng, sem, value):
    if not isinstance(value, int) or value > 0:
        eng.wait_ge(sem, value)


def split_heads(ap, heads, width):
    return ap.rearrange("p (h w) -> p h w", h=heads, w=width)


def ln_vector_stats(v, s, n):
    for t in range(s.nt):
        v.bn_stats(s.stats[:, t, :], flat(s.x[:, bass.ds(s.nt * n + t, 1), :])).then_inc(s.ln_stats, 1)
    v.wait_ge(s.ln_stats, s.nt * n + s.nt)
    v.sem_inc(s.passed)
    for t in range(s.nt):
        v.bn_aggr(s.moments[:, t, :], s.stats[:, t, :]).then_inc(s.ln_moments, 1)
    v.wait_ge(s.ln_moments, s.nt * n + s.nt)
    v.tensor_scalar(s.var[:], s.moments[:, :, 1], LN_EPS, None, ALU.add).then_inc(s.ln_var, 1)


def ln_vector_scale(v, s, n):
    v.wait_ge(s.ln_rstd, n + 1)
    for t in range(s.nt):
        v.tensor_scalar(s.xn[:, t, :], flat(s.x[:, bass.ds(s.nt * n + t, 1), :]), s.moments[:, t, 0:1],
                        s.rstd[:, t:t + 1], ALU.subtract, ALU.mult).then_inc(s.ln_xn, 1)


def ln_gpsimd_rstd(g, s, n):
    g.wait_ge(s.ln_var, n + 1)
    g.tensor_tensor(s.rstd[:], s.var[:], s.minus_half[:, 0:s.nt], ALU.pow).then_inc(s.ln_rstd, 1)


def ln_place(s, half, at, cols):
    if s.nt * P * KD > 512:
        return s.ps[:, s.bank + half, at:at + cols]
    return s.ps[:, s.bank, half * s.nt * P + at:half * s.nt * P + at + cols]


def ln_tensor(t_, s, n):
    t_.wait_ge(s.ln_xn, s.nt * n + s.nt)
    for half in range(KD):
        for t in range(s.nt):
            mm = t_.transpose(ln_place(s, half, t * P, P), s.xn[:, t, half * P:(half + 1) * P], s.ident)
    mm.then_inc(s.ln_turned, 1)


def ln_scalar(a, s, n):
    a.wait_ge(s.ln_turned, n + 1)
    for half in range(KD):
        for b in range(s.nt // BT):
            a.activation(s.h[:, half, b * T:(b + 1) * T], ln_place(s, half, b * T, T), ACT.Identity,
                         scale=s.mod[:, KD * s.scale + half, bass.ds(s.nt // BT * n + b, 1)],
                         bias=s.mod[:, KD * s.shift + half, bass.ds(s.nt // BT * n + b, 1)]).then_inc(s.ln_h, 1)


def ln_scalar_hi(a, s, n, h_hi):
    for half in range(KD):
        a.wait_ge(s.ln_h, KD * s.nt // BT * n + (half + 1) * s.nt // BT)
        a.activation(h_hi(half), s.h[:, half, :], ACT.Copy).then_inc(s.ln_hi, 1)


def ln_gpsimd_lo(g, s, n, h_hi, h_lo):
    for half in range(KD):
        g.wait_ge(s.ln_hi, KD * n + half + 1)
        g.tensor_tensor(h_lo(half), s.h[:, half, :], h_hi(half).bitcast(F32), ALU.subtract).then_inc(s.ln_lo, 1)


def ln_buffers(sb, sem, c, mod, shift, scale, nt, bank):
    s = Parts()
    s.x = c.x
    s.ps = c.ps
    s.ident = c.ident
    s.minus_half = c.minus_half
    s.mod = mod
    s.shift = shift
    s.scale = scale
    s.nt = nt
    s.bank = bank
    s.stats = sb("ln_stats_t", [P, nt, 6], F32)
    s.moments = sb("ln_moments_t", [P, nt, 2], F32)
    s.var = sb("ln_var_t", [P, nt], F32)
    s.rstd = sb("ln_rstd_t", [P, nt], F32)
    s.xn = sb("ln_xn_t", [P, nt, D], F32)
    s.h = sb("ln_h_t", [P, KD, nt * P], F32)
    s.ln_stats = sem("ln_stats")
    s.ln_moments = sem("ln_moments")
    s.ln_var = sem("ln_var")
    s.ln_rstd = sem("ln_rstd")
    s.ln_xn = sem("ln_xn")
    s.ln_turned = sem("ln_turned")
    s.ln_h = sem("ln_h")
    s.ln_hi = sem("ln_hi")
    s.ln_lo = sem("ln_lo")
    s.passed = sem("passed")
    return s


def qkv_buffers(sb, sem, n_q, n_k, n_v, v_width):
    q = Parts()
    q.n_q = n_q
    q.n_k = n_k
    q.n_v = n_v
    q.v_width = v_width
    q.n_qk = n_q + n_k
    q.h_hi = sb("h_hi", [P, KD, T], F32R)
    q.h_lo = sb("h_lo", [P, KD, T], F32R)
    q.cosine = sb("rope_cos_part", [P, q.n_qk * HW], F32)
    q.sine = sb("rope_sin_part", [P, q.n_qk * HW], F32)
    q.roped = sb("roped", [P, 2, q.n_qk * HW], F32)
    q.q_stack = [sb(f"q_stack{j}", [P, n_q * 64], F32) for j in range(2)]
    q.k_stack = [sb(f"k_stack{j}", [P, n_k * 64], F32) for j in range(2)]
    q.q_rows = sb("q_rows", [P, 2, n_q // 2, T], F32R)
    q.k_pad = [sb(f"k_pad{j}", [P, 2, n_k // 2, T], F32R) for j in range(2)]
    q.v = sb("v_ones", [P, 2, BT, n_v, v_width + 1], F32)
    q.qkv_done = sem("qkv_done")
    q.v_copied = sem("v_copied")
    q.plain_copied = sem("plain_copied")
    q.rope_parts = sem("rope_parts")
    q.roped_ready = sem("roped_ready")
    q.stack_hi = sem("stack_hi")
    q.stack_lo = sem("stack_lo")
    q.rows_turned = sem("rows_turned")
    q.q_rows_ready = sem("q_rows_ready")
    q.k_rows_ready = sem("k_rows_ready")
    q.stacks_set = sem("stacks_set")
    q.q_rounds, q.k_rounds = n_q // 8, n_k // 8
    q.rounds = q.q_rounds + q.k_rounds
    return q


STACKS_SET = 7


def stack_view(stack, heads):
    return stack[:, :].rearrange("p (h s w) -> p h s w", h=heads, s=4, w=HW)


def qkv_gpsimd_prepare(g, q):
    for j in range(2):
        g.memset(q.q_stack[j][:], 0.0).then_inc(q.stacks_set, 1)
        g.memset(q.k_stack[j][:], -1.0).then_inc(q.stacks_set, 1)
    g.memset(q.v[:], 1.0).then_inc(q.stacks_set, 1)


def qkv_vector_prepare(v, q):
    for j in range(2):
        other = 64 * (1 - j)
        v.memset(q.k_pad[j][other:other + 64, :, :, :].bitcast(F32), 0.0).then_inc(q.stacks_set, 1)


def tile_banks(t):
    return 6 - 2 * t


def qkv_project(t_, c, s, q, w_hi, w_lo, n, t):
    t_.wait_ge(s.ln_lo, KD * n + KD)
    b0 = tile_banks(t)
    tok = slice(t * P, (t + 1) * P)
    terms = [(h, w, k) for k in range(KD) for h, w in ((q.h_hi, w_hi), (q.h_hi, w_lo), (q.h_lo, w_hi))]
    for e, (h, w, k) in enumerate(terms):
        for bank, lo, hi in ((b0, 0, 512), (b0 + 1, 512, 768)):
            mm = t_.matmul(c.ps[:, bank, 0:hi - lo], h[:, k, tok], w[:, k, lo:hi],
                           start=(e == 0), stop=(e == len(terms) - 1))
    mm.then_inc(q.qkv_done, 1)


def qkv_turn(t_, c, q, n, t, rounds):
    t_.wait_ge(q.stack_lo, 2 * (BT * n + t + 1))
    for r in rounds:
        if r >= 2:
            if r - 2 < q.q_rounds:
                t_.wait_ge(q.q_rows_ready, q.q_rounds * (BT * n + t) + r - 1)
            else:
                t_.wait_ge(q.k_rows_ready, 2 * (q.k_rounds * (BT * n + t) + r - 1 - q.q_rounds))
        src, at = (q.q_stack, r) if r < q.q_rounds else (q.k_stack, r - q.q_rounds)
        for j in range(4):
            mm = t_.transpose(c.ps[:, tile_banks(t) + r % 2, j * P:(j + 1) * P],
                              src[t][:, (4 * at + j) * P:(4 * at + j + 1) * P], c.ident)
        mm.then_inc(q.rows_turned, 1)


def qkv_scalar_copies(a, c, q, n, t, par, plain, pv_done):
    b0 = tile_banks(t)
    a.wait_ge(q.qkv_done, BT * n + t + 1)
    if t == 0:
        wait_from_one(a, pv_done, HEADS * (n - 1))
    v_from = q.n_qk * HW - 512
    a.activation(q.v[:, par, t, :, 0:q.v_width],
                 split_heads(c.ps[:, b0 + 1, v_from:v_from + q.n_v * q.v_width], q.n_v, q.v_width),
                 ACT.Copy).then_inc(q.v_copied, 1)
    if plain:
        wait_from_one(a, q.stack_lo, 2 * (BT * (n - 1) + t + 1))
        a.activation(split_heads(q.roped[:, t, :], q.n_qk, HW)[:, :, 8:16],
                     split_heads(c.ps[:, b0, :], q.n_qk, HW)[:, :, 8:16], ACT.Copy).then_inc(q.plain_copied, 1)


def qkv_scalar_hi(a, q, n, t, plain):
    a.wait_ge(q.roped_ready, BT * n + t + 1)
    if plain:
        a.wait_ge(q.plain_copied, BT * n + t + 1)
    wait_from_one(a, q.rows_turned, q.rounds * (BT * (n - 1) + t + 1))
    roped = split_heads(q.roped[:, t, :], q.n_qk, HW)
    qs = stack_view(q.q_stack[t], q.n_q).bitcast(F32R)
    ks = stack_view(q.k_stack[t], q.n_k).bitcast(F32R)
    a.activation(qs[:, :, 0:3:2, :], roped[:, 0:q.n_q, :].unsqueeze(2).to_broadcast([P, q.n_q, 2, HW]), ACT.Copy)\
        .then_inc(q.stack_hi, 1)
    a.activation(ks[:, :, 0:2, :], roped[:, q.n_q:q.n_qk, :].unsqueeze(2).to_broadcast([P, q.n_k, 2, HW]), ACT.Copy)\
        .then_inc(q.stack_hi, 1)


def qkv_gpsimd_lo(g, q, n, t):
    g.wait_ge(q.stack_hi, 2 * (BT * n + t + 1))
    roped = split_heads(q.roped[:, t, :], q.n_qk, HW)
    qs, ks = stack_view(q.q_stack[t], q.n_q), stack_view(q.k_stack[t], q.n_k)
    g.tensor_tensor(qs[:, :, 1, :].bitcast(F32R), roped[:, 0:q.n_q, :], qs[:, :, 0, :], ALU.subtract)\
        .then_inc(q.stack_lo, 1)
    g.tensor_tensor(ks[:, :, 2, :].bitcast(F32R), roped[:, q.n_q:q.n_qk, :], ks[:, :, 0, :], ALU.subtract)\
        .then_inc(q.stack_lo, 1)


def qkv_scalar_rows(a, c, q, n, t, par, rounds):
    for r in rounds:
        if r < q.q_rounds:
            a.wait_ge(q.rows_turned, q.rounds * (BT * n + t) + r + 1)
            a.activation(q.q_rows[:, par, 4 * r:4 * r + 4, t * P:(t + 1) * P],
                         c.ps[:, tile_banks(t) + r % 2, :].rearrange("p (j n) -> p j n", j=4), ACT.Copy)\
                .then_inc(q.q_rows_ready, 1)


def qkv_vector_rows(v, c, q, n, t, par):
    for r in range(q.k_rounds):
        at = q.q_rounds + r
        v.wait_ge(q.rows_turned, q.rounds * (BT * n + t) + at + 1)
        for j in range(2):
            rows = slice(64 * j, 64 * j + 64)
            v.tensor_copy(q.k_pad[j][rows, par, 4 * r:4 * r + 4, t * P:(t + 1) * P],
                          c.ps[rows, tile_banks(t) + at % 2, :].rearrange("p (j n) -> p j n", j=4))\
                .then_inc(q.k_rows_ready, 1)


def qkv_vector_rotate(v, c, q, n, t, rope, plain):
    b0 = tile_banks(t)
    v.wait_ge(q.plain_copied if plain else q.v_copied, BT * n + t + 1)
    x = split_heads(c.psflat[:, b0 * 512:b0 * 512 + q.n_qk * HW], q.n_qk, HW)
    cp = split_heads(q.cosine[:, :], q.n_qk, HW)
    sp = split_heads(q.sine[:, :], q.n_qk, HW)
    out = split_heads(q.roped[:, t, :], q.n_qk, HW)
    w, half = rope.width, rope.width // 2
    cos = rope.cos[:, t, :].unsqueeze(1).to_broadcast([P, q.n_qk, w])
    sin_a = rope.sin_a[:, t, :].unsqueeze(1).to_broadcast([P, q.n_qk, half])
    sin_b = rope.sin_b[:, t, :].unsqueeze(1).to_broadcast([P, q.n_qk, half])
    v.tensor_tensor(cp[:, :, 0:w], x[:, :, 0:w], cos, ALU.mult).then_inc(q.rope_parts, 1)
    v.tensor_tensor(rope.first(sp), rope.second(x), sin_a, ALU.mult).then_inc(q.rope_parts, 1)
    v.tensor_tensor(rope.second(sp), rope.first(x), sin_b, ALU.mult).then_inc(q.rope_parts, 1)
    v.wait_ge(q.rope_parts, 3 * (BT * n + t + 1))
    wait_from_one(v, q.stack_lo, 2 * (BT * (n - 1) + t + 1))
    v.tensor_tensor(out[:, :, 0:w], cp[:, :, 0:w], sp[:, :, 0:w], ALU.add).then_inc(q.roped_ready, 1)


def setup(nc, c, args):
    with ExitStack() as stack:
        def sb(name, shape, dt):
            return stack.enter_context(nc.sbuf_tensor(name, shape, dt))

        def sem(name):
            return new_semaphore(nc, c, stack, name)

        cond = [sb(f"cond{n}", [P, KD, B], F32) for n in range(2)]
        cond_silu = [sb(f"cond_silu{n}", [P, KD, B], F32) for n in range(2)]
        wmod = [sb(f"wmod{n}", [P, KD, 6 * D], F32) for n in range(2)]
        gate_sign = sb("gate_sign", [P, 2, 2 * KD * B], F32)
        gate_size = sb("gate_size", [P, 2, 2 * KD * B], F32)
        lam_in = sb("lam_in", [P, 4, HW], F32)
        lam_prod = sb("lam_prod", [P, 2, HW], F32)
        lam_sum = sb("lam_sum", [P, 2], F32)
        lam_exp = sb("lam_exp", [P, 2], F32)

        consts_in, x_in, cond_in, wmod_in, attn_in, lam_loaded, gn_in = (
            sem(n) for n in ("consts_in", "x_in", "cond_in", "wmod_in", "attn_in", "lam_loaded", "gn_in"))
        silu_done, mod_done, mod_read, sign_done, size_done, gates_done = (
            sem(n) for n in ("silu_done", "mod_done", "mod_read", "sign_done", "size_done", "gates_done"))
        lam_mul, lam_added, lam_exped, lam_done = (sem(n) for n in ("lam_mul", "lam_added", "lam_exped", "lam_done"))
        whi_done, wlo_done, fills = (sem(n) for n in ("whi_done", "wlo_done", "fills"))
        block = stack.enter_context(nc.Block())

        @block.sync
        def _(sp):
            sp.dma_start(cond[0][:], args.c0).then_inc(cond_in, 16)
            sp.dma_start(cond[1][:], args.c1).then_inc(cond_in, 16)
            for n, w in enumerate((args.wmod0, args.wmod1)):
                sp.dma_start(wmod[n][:], w).then_inc(wmod_in, 16)
            sp.dma_start(c.consts[:], args.consts).then_inc(consts_in, 16)
            sp.dma_start(c.x[:], args.x).then_inc(x_in, 16)
            sp.wait_ge(consts_in, 16)
            sp.wait_ge(x_in, 16)

        @block.scalar
        def _(a):
            a.dma_start(c.w0[:], args.w0).then_inc(attn_in, 16)
            a.dma_start(lam_in[:], args.lam).then_inc(lam_loaded, 16)
            a.dma_start(c.gn[:], args.gn).then_inc(gn_in, 16)
            a.wait_ge(cond_in, 32)
            for n in range(2):
                a.activation(flat(cond_silu[n][:]), flat(cond[n][:]), ACT.Silu).then_inc(silu_done, 1)
            a.wait_ge(lam_added, 1)
            a.activation(lam_exp[:], lam_sum[:], ACT.Exp).then_inc(lam_exped, 1)
            a.wait_ge(attn_in, 16)
            a.activation(flat(c.w0_hi[:]), flat(c.w0[:]), ACT.Copy).then_inc(whi_done, 1)

        @block.gpsimd
        def _(g):
            g.memset(c.minus_half[:], -0.5).then_inc(fills, 1)
            g.memset(c.mean_of[:], 1.0 / (T * 2 * HW)).then_inc(fills, 1)
            g.wait_ge(consts_in, 16)
            g.tensor_copy(c.ident_bf[:], c.consts[:, C_ID:C_ID + P]).then_inc(fills, 1)
            g.tensor_copy(c.mask_bf[:], c.consts[:, C_MASK:C_MASK + 2 * P]).then_inc(fills, 1)
            g.wait_ge(whi_done, 1)
            g.tensor_tensor(flat(c.w0_lo[:]), flat(c.w0[:]), flat(c.w0_hi[:]).bitcast(F32), ALU.subtract)\
                .then_inc(wlo_done, 1)

        @block.tensor
        def _(t_):
            for n in range(2):
                t_.wait_ge(silu_done, n + 1)
                t_.wait_ge(wmod_in, 32)
                for col in range(6 * KD):
                    for k in range(KD):
                        mm = t_.matmul(c.ps[:, n, col * B:(col + 1) * B], wmod[n][:, k, col * P:(col + 1) * P],
                                       cond_silu[n][:, k, :], start=(k == 0), stop=(k == KD - 1))
                mm.then_inc(mod_done, 1)

        @block.vector
        def _(v):
            v.wait_ge(lam_loaded, 16)
            v.tensor_tensor(lam_prod[:], lam_in[:, 0:4:2, :], lam_in[:, 1:4:2, :], ALU.mult).then_inc(lam_mul, 1)
            v.wait_ge(lam_mul, 1)
            v.tensor_reduce(lam_sum[:], lam_prod[:], AX.X, ALU.add).then_inc(lam_added, 1)
            for n in range(2):
                mod = flat(c.mod[n][:])
                v.wait_ge(mod_done, n + 1)
                v.tensor_copy(mod, c.ps[:, n, 0:6 * KD * B]).then_inc(mod_read, 1)
                v.wait_ge(mod_read, 3 * n + 1)
                for part in (SCALE_A, SCALE_B):
                    at = c.mod[n][:, KD * part:KD * part + KD, :]
                    v.tensor_scalar(at, at, 1.0, None, ALU.add).then_inc(mod_read, 1)
                for j, part in enumerate((GATE_A, GATE_B)):
                    g = flat(c.mod[n][:, KD * part:KD * part + KD, :])
                    at = slice(j * KD * B, (j + 1) * KD * B)
                    v.tensor_scalar(gate_sign[:, n, at], g, 0.0, 2.0, ALU.is_ge, ALU.mult).then_inc(sign_done, 1)
                    v.tensor_scalar(gate_size[:, n, at], g, -1.0, None, ALU.mult).then_inc(sign_done, 1)
                v.wait_ge(sign_done, 4 * n + 4)
                for j, part in enumerate((GATE_A, GATE_B)):
                    g = flat(c.mod[n][:, KD * part:KD * part + KD, :])
                    at = slice(j * KD * B, (j + 1) * KD * B)
                    v.scalar_tensor_tensor(gate_size[:, n, at], gate_size[:, n, at], 0.25, g, ALU.max, ALU.max)\
                        .then_inc(size_done, 1)
                v.wait_ge(size_done, 2 * n + 2)
                for j, part in enumerate((GATE_A, GATE_B)):
                    g = flat(c.mod[n][:, KD * part:KD * part + KD, :])
                    at = slice(j * KD * B, (j + 1) * KD * B)
                    v.scalar_tensor_tensor(g, gate_sign[:, n, at], -1.0, gate_size[:, n, at], ALU.add, ALU.mult)\
                        .then_inc(gates_done, 1)
            v.wait_ge(lam_exped, 1)
            v.scalar_tensor_tensor(c.neg_lam[:], lam_exp[:, 1:2], -LAMBDA_INIT, lam_exp[:, 0:1],
                                   ALU.add, ALU.subtract).then_inc(lam_done, 1)
            v.wait_ge(gn_in, 16)
            v.tensor_scalar(c.gn[:], c.gn[:], 1.0 - LAMBDA_INIT, None, ALU.mult).then_inc(lam_done, 1)


def pipeline(eng, step):
    step(-1, 1, True, False, False, True)
    step(0, 0, True, True, False, True)
    step(1, 1, True, True, True, True)
    with eng.Fori(0, (B - 4) // 2) as i:
        step(2 * i + 2, 0, True, True, True, True)
        step(2 * i + 3, 1, True, True, True, True)
    step(B - 2, 0, True, True, True, False)
    step(B - 1, 1, False, True, True, False)
    step(B, 0, False, False, True, False)


def output_buffers(sb, sem, f_tiles, wo_hi, wo_lo, mod):
    o = Parts()
    o.f_tiles = f_tiles
    o.wo_hi = wo_hi
    o.wo_lo = wo_lo
    o.mod = mod
    o.o_hi = sb("o_hi", [P, f_tiles, T], F32R)
    o.o_lo = sb("o_lo", [P, f_tiles, T], F32R)
    o.y = sb("y", [P, KD, T], F32)
    o.o_hi_done = sem("o_hi_done")
    o.o_lo_done = sem("o_lo_done")
    o.y_done = sem("y_done")
    o.y_gated = sem("y_gated")
    o.y_turned = sem("y_turned")
    o.x_added = sem("x_added")
    return o


def output_tensor(t_, c, o, n):
    t_.wait_ge(o.o_lo_done, n + 1)
    for dh in range(KD):
        terms = [(w, x, f) for f in range(o.f_tiles)
                 for w, x in ((o.wo_hi, o.o_hi), (o.wo_hi, o.o_lo), (o.wo_lo, o.o_hi))]
        for m, (w, x, f) in enumerate(terms):
            mm = t_.matmul(c.ps[:, 7, dh * T:(dh + 1) * T], w[:, f, dh * P:(dh + 1) * P], x[:, f, :],
                           start=(m == 0), stop=(m == len(terms) - 1))
    mm.then_inc(o.y_done, 1)


def output_scalar_gate(a, c, o, n):
    a.wait_ge(o.y_done, n + 1)
    for dh in range(KD):
        a.activation(o.y[:, dh, :], c.ps[:, 7, dh * T:(dh + 1) * T], ACT.Copy,
                     scale=o.mod[:, KD * GATE_A + dh, bass.ds(n, 1)]).then_inc(o.y_gated, 1)


def output_tensor_back(t_, c, o, n):
    t_.wait_ge(o.y_gated, KD * (n + 1))
    for t in range(BT):
        for dh in range(KD):
            mm = t_.transpose(c.ps[:, 6, t * D + dh * P:t * D + (dh + 1) * P],
                              o.y[:, dh, t * P:(t + 1) * P], c.ident)
    mm.then_inc(o.y_turned, 1)


def output_vector_add(v, c, o, n):
    v.wait_ge(o.y_turned, n + 1)
    x = flat(c.x[:, bass.ds(BT * n, BT), :])
    v.tensor_tensor(x, x, c.ps[:, 6, :], ALU.add).then_inc(o.x_added, 1)


def send_maxima(sp, q, m, n, par):
    pairs = q.n_q // 2
    sp.wait_ge(m.max_rows_ready, n + 1)
    for half in range(2):
        row = 64 * half + ROWS
        sp.dma_start(q.q_rows[row:row + 1, par, :, :].bitcast(F32),
                     m.max_rows[pairs * half:pairs * (half + 1), :].bitcast(F32)).then_inc(m.max_in, 16)


def max_out(a, c, q, m, n):
    a.wait_ge(m.max_turned, n + 1)
    wait_from_one(a, m.max_in, 32 * n)
    a.activation(m.max_rows[:, :], c.ps[0:q.n_q, 4, 0:T], ACT.Copy).then_inc(m.max_rows_ready, 1)


def attention0(nc, c):
    with ExitStack() as stack:
        def sb(name, shape, dt):
            return stack.enter_context(nc.sbuf_tensor("a0_" + name, shape, dt))

        def sem(name):
            return new_semaphore(nc, c, stack, "a0_" + name)

        s = ln_buffers(sb, sem, c, c.mod[0], SHIFT_A, SCALE_A, BT, 7)
        q = qkv_buffers(sb, sem, HEADS, HEADS, HEADS, HW)
        w_hi, w_lo = c.w0_hi[:, :, 0:768], c.w0_lo[:, :, 0:768]
        o = output_buffers(sb, sem, KD, c.w0_hi[:, :, 768:1024], c.w0_lo[:, :, 768:1024], c.mod[0])
        m = Parts()
        m.max_rows = sb("max_rows", [HEADS, T], F32R)
        m.max_turned, m.max_rows_ready, m.max_in = (sem(n) for n in ("max_turned", "max_rows_ready", "max_in"))
        maxima = sb("maxima", [P, BT, HEADS], F32)
        probs = sb("probs", [P, 4, BT * T], F32)
        denom = sb("denom", [P, BT, HEADS], F32)
        heads_out = sb("heads_out", [P, BT, D], F32)
        scores_done, max_done = sem("scores_done"), sem("max_done")
        keyed_done, exp_done, pv_done, denom_done, out_scaled, out_turned = (
            sem(n) for n in ("keyed_done", "exp_done", "pv_done", "denom_done", "out_scaled", "out_turned"))
        rope = Parts()
        rope.width = 8
        rope.first = lambda a: a[:, :, 0:4]
        rope.second = lambda a: a[:, :, 4:8]
        rope.cos = c.table(C_COS0, 8)
        rope.sin_a = c.table(C_SIN0A, 4)
        rope.sin_b = c.table(C_SIN0B, 4)
        ps = c.ps
        ones_col = HW + 1
        pv_view = ps[:, 2:4, 0:HEADS * ones_col].rearrange("p q (h w) -> p q h w", h=HEADS, w=ones_col)
        TURNS = {1: (0, (0, 1)), 2: (0, (2, 3)), 4: (1, (0, 1)), 5: (1, (2, 3))}
        ROW_SLOTS = {6 + j: (2 * j, 2 * j + 1) for j in range(8)}
        OUT_TURN, OUT_PROJECT, OUT_BACK, NORM_TURN, MAX_TURN = 7, 9, 11, 12, 14
        block = stack.enter_context(nc.Block())

        @block.tensor
        def _(t_):
            def row_scores(n, par, h):
                if h >= 2:
                    t_.wait_ge(max_done, HEADS * n + h - 1)
                for qt in range(BT):
                    mm = t_.matmul(ps[:, 4 + h % 2, qt * T:(qt + 1) * T],
                                   q.q_rows[:, par, h // 2, qt * P:(qt + 1) * P],
                                   q.k_pad[h % 2][:, par, h // 2, :], start=(qt == 0), stop=(qt == BT - 1),
                                   skip_group_check=True)
                mm.then_inc(scores_done, 1)

            def turn_maxima(n):
                t_.wait_ge(max_done, HEADS * (n + 1))
                for qt in range(BT):
                    mm = t_.transpose(ps[0:HEADS, 4, qt * P:(qt + 1) * P], maxima[:, qt, :], c.ident)
                mm.then_inc(m.max_turned, 1)

            def key_scores(n, par, h):
                if h == 0:
                    t_.wait_ge(m.max_in, 32 * (n + 1))
                wait_from_one(t_, exp_done, HEADS * n + h - 1)
                for kt in range(BT):
                    mm = t_.matmul(ps[:, h % 2, kt * T:(kt + 1) * T],
                                   q.k_pad[h % 2][:, par, h // 2, kt * P:(kt + 1) * P],
                                   q.q_rows[:, par, h // 2, :], start=(kt == 0), stop=(kt == BT - 1),
                                   skip_group_check=True)
                mm.then_inc(keyed_done, 1)

            def weigh(n, par, h):
                t_.wait_ge(exp_done, HEADS * n + h + 1)
                if h == 0:
                    wait_from_one(t_, out_scaled, n)
                for qt in range(BT):
                    for kt in range(BT):
                        mm = t_.matmul(ps[:, 2 + qt, h * ones_col:(h + 1) * ones_col],
                                       probs[:, h % 4, kt * T + qt * P:kt * T + (qt + 1) * P],
                                       q.v[:, par, kt, h, :], start=(kt == 0), stop=(kt == BT - 1))
                mm.then_inc(pv_done, 1)

            def turn_out(n):
                t_.wait_ge(out_scaled, n + 1)
                for f in range(KD):
                    for qt in range(BT):
                        mm = t_.transpose(ps[:, 6, f * T + qt * P:f * T + (qt + 1) * P],
                                          heads_out[:, qt, f * P:(f + 1) * P], c.ident)
                mm.then_inc(out_turned, 1)

            def step(n, par, front, core, tail, norm):
                for t in range(BT):
                    if tail:
                        weigh(n - 1, 1 - par, HEADS - 2 + t)
                    if front:
                        if t == 0:
                            wait_from_one(t_, o.x_added, n - 1)
                        else:
                            wait_from_one(t_, m.max_rows_ready, n + 1)
                        qkv_project(t_, c, s, q, w_hi, w_lo, n + 1, t)
                for h in range(HEADS):
                    if core:
                        key_scores(n, par, h)
                        if h >= 2:
                            weigh(n, par, h - 2)
                    if front and h in TURNS:
                        t, rounds = TURNS[h]
                        qkv_turn(t_, c, q, n + 1, t, rounds)
                    if front and h == min(ROW_SLOTS):
                        t_.wait_ge(q.q_rows_ready, q.q_rounds * BT * (n + 2))
                        t_.wait_ge(q.k_rows_ready, 2 * q.k_rounds * BT * (n + 2))
                    if front and h in ROW_SLOTS:
                        for u in ROW_SLOTS[h]:
                            row_scores(n + 1, 1 - par, u)
                    if tail and h == OUT_TURN:
                        turn_out(n - 1)
                    if tail and h == OUT_PROJECT:
                        output_tensor(t_, c, o, n - 1)
                    if tail and h == OUT_BACK:
                        output_tensor_back(t_, c, o, n - 1)
                    if norm and h == NORM_TURN:
                        if tail:
                            t_.wait_ge(o.y_gated, KD * n)
                        ln_tensor(t_, s, n + 2)
                    if front and h == MAX_TURN:
                        turn_maxima(n + 1)

            t_.wait_ge(q.stacks_set, STACKS_SET)
            ln_tensor(t_, s, 0)
            pipeline(t_, step)

        @block.scalar
        def _(a):
            def exps(n, h):
                a.wait_ge(keyed_done, HEADS * n + h + 1)
                wait_from_one(a, pv_done, HEADS * n + h - 3)
                a.activation(probs[:, h % 4, :], ps[:, h % 2, :], ACT.Exp, scale=SCALE).then_inc(exp_done, 1)

            def out_hi(n):
                a.wait_ge(out_turned, n + 1)
                a.activation(o.o_hi[:], ps[:, 6, :].rearrange("p (f n) -> p f n", f=KD), ACT.Copy)\
                    .then_inc(o.o_hi_done, 1)

            def norm_to_hi(m_):
                ln_scalar(a, s, m_)
                wait_from_one(a, q.qkv_done, BT * m_)
                ln_scalar_hi(a, s, m_, lambda half: q.h_hi[:, half, :])

            def step(n, par, front, core, tail, norm):
                if front:
                    qkv_scalar_copies(a, c, q, n + 1, 0, 1 - par, True, pv_done)
                    qkv_scalar_hi(a, q, n + 1, 0, True)
                    qkv_scalar_copies(a, c, q, n + 1, 1, 1 - par, True, pv_done)
                for h in range(HEADS):
                    if core:
                        exps(n, h)
                    if front and h in TURNS:
                        t, rounds = TURNS[h]
                        qkv_scalar_rows(a, c, q, n + 1, t, 1 - par, rounds)
                    if front and h == 1:
                        qkv_scalar_hi(a, q, n + 1, 1, True)
                    if tail and h == OUT_TURN:
                        out_hi(n - 1)
                    if tail and h == OUT_PROJECT:
                        output_scalar_gate(a, c, o, n - 1)
                    if norm and h == NORM_TURN:
                        norm_to_hi(n + 2)
                    if front and h == MAX_TURN:
                        max_out(a, c, q, m, n + 1)

            a.wait_ge(q.stacks_set, STACKS_SET)
            norm_to_hi(0)
            pipeline(a, step)

        @block.vector
        def _(v):
            def max_of(n, h):
                v.wait_ge(scores_done, HEADS * n + h + 1)
                col = HEADS // 2 * (h % 2) + h // 2
                v.tensor_reduce(maxima[:, :, col:col + 1],
                                ps[:, 4 + h % 2, :].rearrange("p (q k) -> p q k", q=BT), AX.X, ALU.max)\
                    .then_inc(max_done, 1)

            def scale_out(n):
                v.wait_ge(pv_done, HEADS * (n + 1))
                v.reciprocal(denom[:], pv_view[:, :, :, HW]).then_inc(denom_done, 1)
                v.wait_ge(denom_done, n + 1)
                wait_from_one(v, out_turned, n)
                v.tensor_tensor(heads_out[:].rearrange("p q (h w) -> p q h w", h=HEADS, w=HW),
                                pv_view[:, :, :, 0:HW],
                                denom[:].unsqueeze(3).to_broadcast([P, BT, HEADS, HW]), ALU.mult)\
                    .then_inc(out_scaled, 1)

            def out_lo(n):
                v.wait_ge(o.o_hi_done, n + 1)
                v.tensor_tensor(o.o_lo[:], ps[:, 6, :].rearrange("p (f n) -> p f n", f=KD),
                                o.o_hi[:].bitcast(F32), ALU.subtract).then_inc(o.o_lo_done, 1)

            def step(n, par, front, core, tail, norm):
                if front:
                    qkv_vector_rotate(v, c, q, n + 1, 0, rope, True)
                if tail:
                    scale_out(n - 1)
                if front:
                    qkv_vector_rotate(v, c, q, n + 1, 1, rope, True)
                if norm:
                    ln_vector_stats(v, s, n + 2)
                if front:
                    qkv_vector_rows(v, c, q, n + 1, 0, 1 - par)
                if norm:
                    ln_vector_scale(v, s, n + 2)
                if front:
                    qkv_vector_rows(v, c, q, n + 1, 1, 1 - par)
                for h in range(HEADS):
                    if front and h in ROW_SLOTS:
                        for u in ROW_SLOTS[h]:
                            max_of(n + 1, u)
                    if tail and h == OUT_TURN:
                        out_lo(n - 1)
                    if tail and h == OUT_BACK:
                        output_vector_add(v, c, o, n - 1)

            qkv_vector_prepare(v, q)
            v.wait_ge(q.stacks_set, STACKS_SET)
            ln_vector_stats(v, s, 0)
            ln_vector_scale(v, s, 0)
            pipeline(v, step)

        @block.gpsimd
        def _(g):
            def step(n, par, front, core, tail, norm):
                if front:
                    qkv_gpsimd_lo(g, q, n + 1, 0)
                    qkv_gpsimd_lo(g, q, n + 1, 1)
                if norm:
                    ln_gpsimd_rstd(g, s, n + 2)
                    ln_gpsimd_lo(g, s, n + 2, lambda half: q.h_hi[:, half, :], lambda half: q.h_lo[:, half, :])

            qkv_gpsimd_prepare(g, q)
            g.wait_ge(q.stacks_set, STACKS_SET)
            ln_gpsimd_rstd(g, s, 0)
            ln_gpsimd_lo(g, s, 0, lambda half: q.h_hi[:, half, :], lambda half: q.h_lo[:, half, :])
            pipeline(g, step)

        @block.sync
        def _(sp):
            for n in range(B):
                send_maxima(sp, q, m, n, n % 2)
            sp.wait_ge(m.max_in, 32 * B)


def mlp_buffers(sb, sem, slots):
    m = Parts()
    m.w_hi = [sb(f"w_hi{j}", [P, WT], F32R) for j in range(slots)]
    m.w_lo = [sb(f"w_lo{j}", [P, WT], F32R) for j in range(slots)]
    m.silu = sb("silu", [P, 2, NP], F32)
    m.act = sb("act", [P, 2, NP], F32)
    m.act_hi = sb("act_hi", [P, 4, NP], F32R)
    m.act_lo = sb("act_lo", [P, 4, NP], F32R)
    m.up_done = sem("up_done")
    m.silu_done = sem("silu_done")
    m.act_done = sem("act_done")
    m.weighted = sem("weighted")
    m.act_hi_done = sem("act_hi_done")
    m.act_lo_done = sem("act_lo_done")
    m.down_done = sem("down_done")
    m.y_added = sem("y_added")
    m.w_hi_done = sem("w_hi_done")
    m.w_lo_done = sem("w_lo_done")
    m.raw_in = [sem(f"raw_in{j}") for j in range(2)]
    return m


def mlp_up(t_, c, m, n, j, slot, tb, first, expert_of=None, cw_rows=None):
    if not first:
        t_.wait_ge(m.act_done, n - 1)
        if expert_of is not None:
            t_.wait_ge(m.weighted, n - 1)
    tok = slice(tb * NP, (tb + 1) * NP)
    for bank, at in ((0, 0), (2, KD * P)):
        terms = [(w, h, k) for k in range(KD)
                 for w, h in ((m.w_hi[slot], c.h_hi), (m.w_hi[slot], c.h_lo), (m.w_lo[slot], c.h_hi))]
        for e, (w, h, k) in enumerate(terms):
            mm = t_.matmul(c.ps[:, bank + j % 2, :], w[:, at + k * P:at + (k + 1) * P], h[:, k, tok],
                           start=(e == 0), stop=(e == len(terms) - 1))
    if expert_of is not None:
        mm = t_.matmul(c.ps[:, 4 + j % 2, :], expert_of[:, :], cw_rows[:, tok], start=True, stop=True)
    mm.then_inc(m.up_done, 1)


def mlp_down(t_, c, m, n, j, slot, first, last):
    t_.wait_ge(m.act_lo_done, n + 1)
    at = 2 * KD * P
    for dh in range(KD):
        terms = ((m.w_hi[slot], m.act_hi), (m.w_hi[slot], m.act_lo), (m.w_lo[slot], m.act_hi))
        for e, (w, a) in enumerate(terms):
            mm = t_.matmul(c.ps[:, 6 + dh, :], w[:, at + dh * P:at + (dh + 1) * P], a[:, j % 4, :],
                           start=(first and e == 0), stop=(last and e == 2))
    mm.then_inc(m.down_done, 1)


def mlp_silu(a, c, m, n, j, first):
    a.wait_ge(m.up_done, n + 1)
    if not first:
        a.wait_ge(m.act_done, n - 1)
    a.activation(m.silu[:, j % 2, :], c.ps[:, j % 2, :], ACT.Silu).then_inc(m.silu_done, 1)


def mlp_hi(a, m, n, j, ready, first):
    a.wait_ge(ready, n + 1)
    if not first:
        a.wait_ge(m.down_done, n - 3)
    a.activation(m.act_hi[:, j % 4, :], m.act[:, j % 2, :], ACT.Copy).then_inc(m.act_hi_done, 1)


def mlp_lo(g, m, n, j):
    g.wait_ge(m.act_hi_done, n + 1)
    g.tensor_tensor(m.act_lo[:, j % 4, :], m.act[:, j % 2, :], m.act_hi[:, j % 4, :].bitcast(F32), ALU.subtract)\
        .then_inc(m.act_lo_done, 1)


def mlp_act(v, c, m, n, j, first, weigh):
    v.wait_ge(m.silu_done, n + 1)
    if not first:
        v.wait_ge(m.act_lo_done, n - 1)
    v.tensor_tensor(m.act[:, j % 2, :], m.silu[:, j % 2, :], c.ps[:, 2 + j % 2, :], ALU.mult).then_inc(m.act_done, 1)
    if weigh:
        v.wait_ge(m.act_done, n + 1)
        v.tensor_tensor(m.act[:, j % 2, :], m.act[:, j % 2, :], c.ps[:, 4 + j % 2, :], ALU.mult)\
            .then_inc(m.weighted, 1)


def add_back_phase(nc, c, mod, name):
    with ExitStack() as stack:
        def sem(n):
            return new_semaphore(nc, c, stack, name + n)

        gated, turned, added = sem("gated"), sem("turned"), sem("added")
        block = stack.enter_context(nc.Block())

        @block.scalar
        def _(a):
            with a.Fori(0, B) as b:
                for dh in range(KD):
                    y = c.yT[:, dh, bass.ds(b * T, T)]
                    a.activation(y, y, ACT.Copy, scale=mod[:, KD * GATE_B + dh, bass.ds(b, 1)]).then_inc(gated, 1)

        @block.tensor
        def _(t_):
            for b in range(B):
                t_.wait_ge(gated, KD * (b + 1))
                if b >= 4:
                    t_.wait_ge(added, b - 3)
                for q in range(BT):
                    for dh in range(KD):
                        at = b * T + q * P
                        mm = t_.transpose(c.ps[:, b % 4, q * D + dh * P:q * D + (dh + 1) * P],
                                          c.yT[:, dh, at:at + P], c.ident)
                mm.then_inc(turned, 1)

        @block.vector
        def _(v):
            for b in range(B):
                v.wait_ge(turned, b + 1)
                x = flat(c.x[:, BT * b:BT * b + BT, :])
                v.tensor_tensor(x, x, c.ps[:, b % 4, :], ALU.add).then_inc(added, 1)


def route(nc, c, args):
    with ExitStack() as stack:
        def sb(name, shape, dt):
            return stack.enter_context(nc.sbuf_tensor("r_" + name, shape, dt))

        def sem(name):
            return new_semaphore(nc, c, stack, "r_" + name)

        s = ln_buffers(sb, sem, c, c.mod[0], SHIFT_B, SCALE_B, PT_, 0)
        gate_w = sb("gate_w", [P, KD, E], F32)
        e_raw = sb("e_raw", [P, PT_, E], F32)
        top = sb("top", [P, PT_, 8], F32)
        neg_top = sb("neg_top", [P, PT_], F32)
        picked = sb("picked", [P, PT_, E], F32)
        total = sb("total", [P, PT_], F32)
        inv_total = sb("inv_total", [P, PT_], F32)
        share = sb("share", [P, PT_, E], F32)
        kept = sb("kept", [P, PT_, E], F32)
        cw = sb("cw", [P, PT_, 2 * E], F32)
        names = ("gate_in", "logits_done", "top_logit", "neg_done", "exped", "totaled", "inverted", "shared", "topped",
                 "cut", "matched", "masked", "cw_full", "cw_hi", "cw_lo", "cw_turned", "cw_out")
        (gate_in, logits_done, top_logit, neg_done, exped, totaled, inverted, shared, topped, cut, matched, masked,
         cw_full, cw_hi, cw_lo, cw_turned, cw_out) = (sem(n) for n in names)
        block = stack.enter_context(nc.Block())

        @block.sync
        def _(sp):
            sp.dma_start(gate_w[:], args.gate_w).then_inc(gate_in, 16)

        @block.tensor
        def _(t_):
            t_.wait_ge(gate_in, 16)
            with t_.Fori(0, PAIRS) as i:
                ln_tensor(t_, s, i)
                t_.wait_ge(s.ln_h, 2 * KD * (i + 1))
                for t in range(PT_):
                    for k in range(KD):
                        mm = t_.matmul(c.ps[:, 2, t * E:(t + 1) * E], s.h[:, k, t * P:(t + 1) * P], gate_w[:, k, :],
                                       start=(k == 0), stop=(k == KD - 1))
                mm.then_inc(logits_done, 1)
                t_.wait_ge(cw_lo, i + 1)
                for t in range(PT_):
                    mm = t_.transpose(c.ps[0:2 * E, 3, t * P:(t + 1) * P], cw[:, t, :], c.ident)
                mm.then_inc(cw_turned, 1)

        @block.scalar
        def _(a):
            with a.Fori(0, PAIRS) as i:
                ln_scalar(a, s, i)
                ln_scalar_hi(a, s, i, lambda half: c.h_hi[:, half, bass.ds(i * NP, NP)])
                a.wait_ge(neg_done, i + 1)
                for t in range(PT_):
                    a.activation(e_raw[:, t, :], c.ps[:, 2, t * E:(t + 1) * E], ACT.Exp,
                                 bias=neg_top[:, t:t + 1]).then_inc(exped, 1)
                a.wait_ge(cw_turned, i + 1)
                a.activation(c.cw_rows[:, bass.ds(i * NP, NP)], c.ps[0:2 * E, 3, :], ACT.Copy).then_inc(cw_out, 1)

        @block.gpsimd
        def _(g):
            with g.Fori(0, PAIRS) as i:
                ln_gpsimd_rstd(g, s, i)
                ln_gpsimd_lo(g, s, i, lambda half: c.h_hi[:, half, bass.ds(i * NP, NP)],
                             lambda half: c.h_lo[:, half, bass.ds(i * NP, NP)])

        @block.vector
        def _(v):
            with v.Fori(0, PAIRS) as i:
                ln_vector_stats(v, s, i)
                ln_vector_scale(v, s, i)
                v.wait_ge(logits_done, i + 1)
                v.tensor_reduce(neg_top[:], c.ps[:, 2, 0:PT_ * E].rearrange("p (t e) -> p t e", e=E), AX.X, ALU.max)\
                    .then_inc(top_logit, 1)
                v.wait_ge(top_logit, i + 1)
                v.tensor_scalar(neg_top[:], neg_top[:], -1.0, None, ALU.mult).then_inc(neg_done, 1)
                v.wait_ge(exped, PT_ * (i + 1))
                v.tensor_reduce(total[:], e_raw[:], AX.X, ALU.add).then_inc(totaled, 1)
                v.wait_ge(totaled, i + 1)
                v.reciprocal(inv_total[:], total[:]).then_inc(inverted, 1)
                v.wait_ge(inverted, i + 1)
                v.tensor_tensor(share[:], e_raw[:], inv_total[:].unsqueeze(2).to_broadcast([P, PT_, E]), ALU.mult)\
                    .then_inc(shared, 1)
                v.wait_ge(shared, i + 1)
                v.sem_inc(s.passed)
                for t in range(PT_):
                    v.max(top[:, t, :], share[:, t, :]).then_inc(topped, 1)
                v.wait_ge(topped, PT_ * (i + 1))
                v.memset(top[:, :, TOPK:8], -2.0).then_inc(cut, 1)
                v.wait_ge(cut, i + 1)
                v.sem_inc(s.passed)
                for t in range(PT_):
                    v.match_replace(picked[:, t, :], top[:, t, :], share[:, t, :], -1.0).then_inc(matched, 1)
                v.wait_ge(matched, PT_ * (i + 1))
                v.tensor_scalar(kept[:], picked[:], 0.0, None, ALU.is_lt).then_inc(masked, 1)
                v.wait_ge(masked, i + 1)
                v.tensor_tensor(kept[:], kept[:], share[:], ALU.mult).then_inc(cw_full, 1)
                v.wait_ge(cw_full, i + 1)
                v.tensor_copy(cw[:, :, 0:E].bitcast(F32R), kept[:]).then_inc(cw_hi, 1)
                v.wait_ge(cw_hi, i + 1)
                v.tensor_tensor(cw[:, :, E:2 * E].bitcast(F32R), kept[:], cw[:, :, 0:E], ALU.subtract)\
                    .then_inc(cw_lo, 1)


def experts(nc, c, args):
    TB = TOKENS // NP
    STEPS = 2 * TB
    CHUNKS = MOE_TILES // 2
    LOOP = CHUNKS // 2
    with ExitStack() as stack:
        def sb(name, shape, dt):
            return stack.enter_context(nc.sbuf_tensor("m_" + name, shape, dt))

        def sem(name):
            return new_semaphore(nc, c, stack, "m_" + name)

        m = mlp_buffers(sb, sem, 4)
        raw = sb("raw", [P, 4, WT], F32)
        which = [sb(f"which{j}", [2 * E, P], F32R) for j in range(4)]
        which_raw = sb("which_raw", [2 * E, MOE_TILES * P], F32)
        which_in, which_done, y_cleared = sem("which_in"), sem("which_done"), sem("y_cleared")
        block = stack.enter_context(nc.Block())

        def slot_of(j):
            return 2 * (j // STEPS % 2) + j % 2

        @block.sync
        def _(sp):
            def load(chunk, par):
                sp.dma_start(raw[:, 2 * par:2 * par + 2, :],
                             args.moe_w[bass.ds(2 * chunk, 2), :, :].rearrange("t p w -> p t w"))\
                    .then_inc(m.raw_in[par], 16)

            sp.dma_start(which_raw[:], args.expert_of).then_inc(which_in, 16)
            load(0, 0)
            load(1, 1)
            with sp.Fori(0, LOOP - 1) as i:
                for par in range(2):
                    sp.wait_ge(m.w_lo_done, 2 * (2 * i + par + 1))
                    load(2 * i + par + 2, par)
            sp.wait_ge(m.w_lo_done, 2 * (2 * LOOP - 1))
            load(2 * LOOP, 0)

        @block.tensor
        def _(t_):
            def step_up(i, j, first=False):
                n = 2 * STEPS * i + j
                jj = j % (2 * STEPS)
                if jj % STEPS < 2:
                    tile = 4 * i + 2 * (j // STEPS) + jj % 2
                    t_.wait_ge(m.w_lo_done, tile + 1)
                    t_.wait_ge(which_done, tile + 1)
                mlp_up(t_, c, m, n, j, slot_of(jj), jj % STEPS // 2, first, which[slot_of(jj)], c.cw_rows)

            step_up(0, 0, first=True)
            step_up(0, 1, first=True)
            t_.wait_ge(y_cleared, 1)
            t_.sem_inc(m.y_added, 1)
            with t_.Fori(0, LOOP) as i:
                for j in range(2 * STEPS):
                    n = 2 * STEPS * i + j
                    if j % 2 == 0:
                        t_.wait_ge(m.y_added, STEPS * i + j // 2 + 1)
                    mlp_down(t_, c, m, n, j, slot_of(j), j % 2 == 0, j % 2 == 1)
                    step_up(i, j + 2)
            for j in range(STEPS):
                if j % 2 == 0:
                    t_.wait_ge(m.y_added, STEPS * LOOP + j // 2 + 1)
                mlp_down(t_, c, m, 2 * STEPS * LOOP + j, j, slot_of(j), j % 2 == 0, j % 2 == 1)
                if j + 2 < STEPS:
                    step_up(LOOP, j + 2)

        @block.scalar
        def _(a):
            def split(k, par, first):
                chunk = 2 * k + par
                a.wait_ge(m.raw_in[par], 16 * (k + 1))
                if not first:
                    a.wait_ge(m.down_done, STEPS * (chunk - 1))
                for t in range(2):
                    a.activation(m.w_hi[2 * par + t][:], raw[:, 2 * par + t, :], ACT.Copy).then_inc(m.w_hi_done, 1)
                for t in range(2):
                    col = (2 * chunk + t) * P
                    a.activation(which[2 * par + t][:, :], which_raw[:, bass.ds(col, P)], ACT.Copy)\
                        .then_inc(which_done, 1)

            def step(i, j, first0=False, first1=False):
                n = 2 * STEPS * i + j
                mlp_silu(a, c, m, n, j, first0)
                mlp_hi(a, m, n, j, m.weighted, first1)

            a.wait_ge(which_in, 16)
            split(0, 0, True)
            split(0, 1, True)
            for j in range(4):
                step(0, j, first0=j < 2, first1=True)
            for j in range(4, 2 * STEPS):
                step(0, j)
                if j == STEPS + 3:
                    split(1, 0, False)
            with a.Fori(1, LOOP) as i:
                for j in range(2 * STEPS):
                    step(i, j)
                    if j == 3:
                        split(i, 1, False)
                    if j == STEPS + 3:
                        split(i + 1, 0, False)
            for j in range(STEPS):
                step(LOOP, j)

        @block.gpsimd
        def _(g):
            def split(k, par):
                chunk = 2 * k + par
                for t in range(2):
                    g.wait_ge(m.w_hi_done, 2 * chunk + t + 1)
                    g.tensor_tensor(m.w_lo[2 * par + t][:], raw[:, 2 * par + t, :],
                                    m.w_hi[2 * par + t][:].bitcast(F32), ALU.subtract).then_inc(m.w_lo_done, 1)

            split(0, 0)
            split(0, 1)
            for j in range(2 * STEPS):
                mlp_lo(g, m, j, j)
                if j == STEPS + 3:
                    split(1, 0)
            with g.Fori(1, LOOP) as i:
                for j in range(2 * STEPS):
                    mlp_lo(g, m, 2 * STEPS * i + j, j)
                    if j == 3:
                        split(i, 1)
                    if j == STEPS + 3:
                        split(i + 1, 0)
            for j in range(STEPS):
                mlp_lo(g, m, 2 * STEPS * LOOP + j, j)

        @block.vector
        def _(v):
            def add_y(n, tb):
                v.wait_ge(m.down_done, n + 1)
                y = c.yT[:, :, tb * NP:(tb + 1) * NP]
                v.tensor_tensor(y, y, c.ps[:, 6:8, :], ALU.add).then_inc(m.y_added, 1)

            def step(i, j, first=False, first_y=False):
                n = 2 * STEPS * i + j
                mlp_act(v, c, m, n, j, first, weigh=True)
                if j % 2 == 0 and not first_y:
                    add_y(n - 1, (j // 2 - 1) % TB)

            v.memset(c.yT[:], 0.0).then_inc(y_cleared, 1)
            v.wait_ge(y_cleared, 1)
            for j in range(2 * STEPS):
                step(0, j, first=j < 2, first_y=j == 0)
            with v.Fori(1, LOOP) as i:
                for j in range(2 * STEPS):
                    step(i, j)
            for j in range(STEPS):
                step(LOOP, j)
            add_y(2 * STEPS * LOOP + STEPS - 1, TB - 1)


def attention1(nc, c, args):
    with ExitStack() as stack:
        def sb(name, shape, dt):
            return stack.enter_context(nc.sbuf_tensor("a1_" + name, shape, dt))

        def sem(name):
            return new_semaphore(nc, c, stack, "a1_" + name)

        KV = 4
        VW = 2 * HW
        FT = HEADS * VW // P
        VC = VW + 1
        NB = 3
        UNITS = 2 * HEADS
        s = ln_buffers(sb, sem, c, c.mod[1], SHIFT_A, SCALE_A, BT, 7)
        q = qkv_buffers(sb, sem, 2 * HEADS, 2 * KV, KV, VW)
        raw = sb("w_raw", [P, KD * 768 + FT * D], F32)
        w_hi_all = sb("w_hi", [P, KD * 768 + FT * D], F32R)
        w_lo_all = sb("w_lo", [P, KD * 768 + FT * D], F32R)

        def qkv_w(w):
            return w[:, 0:KD * 768].rearrange("p (k n) -> p k n", k=KD)

        def wo_w(w):
            return w[:, KD * 768:].rearrange("p (f n) -> p f n", f=FT)

        o = output_buffers(sb, sem, FT, wo_w(w_hi_all), wo_w(w_lo_all), c.mod[1])
        m = Parts()
        m.max_rows = sb("max_rows", [UNITS, T], F32R)
        m.max_turned, m.max_rows_ready, m.max_in = (sem(n) for n in ("max_turned", "max_rows_ready", "max_in"))
        block_max = sb("block_max", [P, UNITS, NB], F32)
        maxima = sb("maxima", [P, BT, UNITS], F32)
        probs = sb("probs", [P, 8, NB * P], F32)
        denom = sb("denom", [P, 2, BT * 2 * 2], F32)
        parts = sb("parts", [P, 2, BT * 2, 2, VW], F32)
        heads_out = [sb(f"heads_out{b}", [P, BT, HEADS, VW], F32) for b in range(2)]
        squares = sb("squares", [P, BT, HEADS, VW], F32)
        sums = sb("sums", [P, HEADS], F32)
        sq_sums = sb("sq_sums", [P, HEADS], F32)
        var = sb("var", [P, HEADS], F32)
        rstd = sb("rstd", [P, HEADS], F32)
        o_full = sb("o_full", [P, FT, T], F32)
        w_in, w_hi_done, w_lo_done = sem("w_in"), sem("w_hi_done"), sem("w_lo_done")
        scores_done, max_done, max_joined = (sem(n) for n in ("scores_done", "max_done", "max_joined"))
        keyed_done, exp_done, cut_done, pv_done, denom_done, parted, out_ready = (
            sem(n) for n in ("keyed_done", "exp_done", "cut_done", "pv_done", "denom_done", "parted", "out_ready"))
        summed, mean_done, centred, squared, sq_summed, var_done, var_eps, rstd_done, normed, out_turned, o_affine = (
            sem(n) for n in ("summed", "mean_done", "centred", "squared", "sq_summed", "var_done", "var_eps",
                             "rstd_done", "normed", "out_turned", "o_affine"))
        rope = Parts()
        rope.width = 16
        rope.first = lambda a: a[:, :, 0:16:2]
        rope.second = lambda a: a[:, :, 1:16:2]
        rope.cos = c.table(C_COS1, 16)
        rope.sin_a = c.table(C_SIN1A, 8)
        rope.sin_b = c.table(C_SIN1B, 8)
        ps = c.ps
        PVG = HEADS // 2
        TURNS = {1: (0, (0, 1)), 2: (0, (2, 3)), 3: (0, (4,)), 4: (1, (0, 1)), 5: (1, (2, 3)), 6: (1, (4,))}
        ROW_SLOTS = {7 + j: tuple(range(4 * j, 4 * j + 4)) for j in range(8)}
        MEAN, VARIANCE, NORM_TURN, OUT_TURN, OUT_PROJECT, OUT_BACK, MAX_TURN = 5, 8, 9, 11, 14, 15, 15
        block = stack.enter_context(nc.Block())

        def pv_bank(grp):
            return ps[:, 2 + grp % 2, 0:BT * 4 * VC].rearrange("p (m w) -> p m w", w=VC)

        @block.tensor
        def _(t_):
            def row_scores(n, par, u):
                h, half, bank = u // 2, u % 2, 4 + u % 2
                if u >= 2:
                    t_.wait_ge(max_done, UNITS * n + u - 1)
                qr, kr = q.q_rows[:, par, h, :], q.k_pad[half][:, par, h // KV, :]
                t_.matmul(ps[:, bank, 0:T], qr[:, P:T], kr[:, 0:T], start=True, stop=False, skip_group_check=True)
                t_.matmul(ps[:, bank, T:T + P], qr[:, 0:P], kr[:, 0:P], start=False, stop=False,
                          skip_group_check=True)
                t_.matmul(ps[:, bank, P:P + T], c.ident_bf[:, :], c.mask_bf[:, :], start=False, stop=True,
                          skip_group_check=True).then_inc(scores_done, 1)

            def turn_maxima(n):
                t_.wait_ge(max_joined, 2 * (n + 1))
                for qt in range(BT):
                    mm = t_.transpose(ps[0:UNITS, 4, qt * P:(qt + 1) * P], maxima[:, qt, :], c.ident)
                mm.then_inc(m.max_turned, 1)

            def key_scores(n, par, u):
                h, half, bank = u // 2, u % 2, u % 2
                if u == 0:
                    t_.wait_ge(m.max_in, 32 * (n + 1))
                wait_from_one(t_, exp_done, UNITS * n + u - 1)
                qr, kr = q.q_rows[:, par, h, :], q.k_pad[half][:, par, h // KV, :]
                t_.matmul(ps[:, bank, 0:T], kr[:, 0:P], qr[:, 0:T], start=True, stop=False, skip_group_check=True)
                t_.matmul(ps[:, bank, T:T + P], kr[:, P:T], qr[:, P:T], start=False, stop=True,
                          skip_group_check=True).then_inc(keyed_done, 1)

            def weigh(n, par, h):
                grp = h // 2
                if h % 2 == 0:
                    wait_from_one(t_, parted, 2 * (PVG * n + grp - 1))
                out = pv_bank(grp)
                for half in range(2):
                    u = 2 * h + half
                    t_.wait_ge(cut_done, UNITS * n + u + 1)
                    for qt in range(BT):
                        at = (h % 2) * BT * 2 + qt * 2 + half
                        for kt in range(qt + 1):
                            blk = (0, 1)[qt] if kt == 0 else 2
                            mm = t_.matmul(out[:, at, :], probs[:, u % 8, blk * P:(blk + 1) * P],
                                           q.v[:, par, kt, h // KV, :], start=(kt == 0), stop=(kt == qt))
                mm.then_inc(pv_done, 1)

            def group_mean(bank, of, ready, done, n):
                t_.wait_ge(ready, n + 1)
                t_.matmul(ps[:, bank, 0:HEADS], c.mean_of[:, :], of[:, :], start=True, stop=True).then_inc(done, 1)

            def turn_out(n, par):
                t_.wait_ge(normed, n + 1)
                for f in range(FT):
                    for qt in range(BT):
                        at = (f % 2) * T + qt * P
                        mm = t_.transpose(ps[:, 6 + f // 2, at:at + P],
                                          heads_out[par][:, qt, 4 * f:4 * f + 4, :].rearrange("p h w -> p (h w)"),
                                          c.ident)
                mm.then_inc(out_turned, 1)

            def step(n, par, front, core, tail, norm):
                for t in range(BT):
                    if tail:
                        weigh(n - 1, 1 - par, HEADS - 2 + t)
                    if front:
                        if t == 0:
                            wait_from_one(t_, o.x_added, n - 1)
                        else:
                            wait_from_one(t_, m.max_rows_ready, n + 1)
                        qkv_project(t_, c, s, q, qkv_w(w_hi_all), qkv_w(w_lo_all), n + 1, t)
                for h in range(HEADS):
                    if core:
                        key_scores(n, par, 2 * h)
                        key_scores(n, par, 2 * h + 1)
                        if h >= 2:
                            weigh(n, par, h - 2)
                    if front and h in TURNS:
                        t, rounds = TURNS[h]
                        qkv_turn(t_, c, q, n + 1, t, rounds)
                    if tail and h == MEAN:
                        if front:
                            t_.wait_ge(q.k_rows_ready, 2 * (BT * (n + 1) + 1))
                        group_mean(6, sums, summed, mean_done, n - 1)
                    if tail and h == VARIANCE:
                        group_mean(7, sq_sums, sq_summed, var_done, n - 1)
                    if norm and h == NORM_TURN:
                        if tail:
                            t_.wait_ge(var_eps, n)
                        ln_tensor(t_, s, n + 2)
                    if tail and h == OUT_TURN:
                        if norm:
                            t_.wait_ge(s.ln_h, KD * (n + 3))
                        turn_out(n - 1, 1 - par)
                    if tail and h == OUT_PROJECT:
                        output_tensor(t_, c, o, n - 1)
                    if tail and h == OUT_BACK:
                        output_tensor_back(t_, c, o, n - 1)
                    if front and h == min(ROW_SLOTS):
                        t_.wait_ge(q.q_rows_ready, q.q_rounds * BT * (n + 2))
                        t_.wait_ge(q.k_rows_ready, 2 * q.k_rounds * BT * (n + 2))
                    if front and h in ROW_SLOTS:
                        for u in ROW_SLOTS[h]:
                            row_scores(n + 1, 1 - par, u)
                    if front and h == MAX_TURN:
                        turn_maxima(n + 1)

            t_.wait_ge(q.stacks_set, STACKS_SET)
            t_.wait_ge(w_lo_done, 1)
            ln_tensor(t_, s, 0)
            pipeline(t_, step)

        @block.scalar
        def _(a):
            def exps(n, u):
                a.wait_ge(keyed_done, UNITS * n + u + 1)
                wait_from_one(a, pv_done, HEADS * n + u // 2 - 3)
                a.activation(probs[:, u % 8, :], ps[:, u % 2, 0:NB * P], ACT.Exp, scale=SCALE).then_inc(exp_done, 1)

            def square(n, par):
                a.wait_ge(centred, n + 1)
                a.activation(squares[:].rearrange("p q h w -> p (q h w)"),
                             heads_out[par][:].rearrange("p q h w -> p (q h w)"), ACT.Square).then_inc(squared, 1)

            def affine(n):
                a.wait_ge(out_turned, n + 1)
                for f in range(FT):
                    a.activation(o_full[:, f, :], ps[:, 6 + f // 2, (f % 2) * T:(f % 2 + 1) * T], ACT.Identity,
                                 scale=c.gn[:, f:f + 1], bias=c.gn[:, FT + f:FT + f + 1]).then_inc(o_affine, 1)

            def out_hi(n):
                a.wait_ge(o_affine, FT * (n + 1))
                a.activation(o.o_hi[:], o_full[:], ACT.Copy).then_inc(o.o_hi_done, 1)

            def norm_to_hi(m_):
                ln_scalar(a, s, m_)
                wait_from_one(a, q.qkv_done, BT * m_)
                ln_scalar_hi(a, s, m_, lambda half: q.h_hi[:, half, :])

            def step(n, par, front, core, tail, norm):
                if front:
                    qkv_scalar_copies(a, c, q, n + 1, 0, 1 - par, False, pv_done)
                    qkv_scalar_hi(a, q, n + 1, 0, False)
                    qkv_scalar_copies(a, c, q, n + 1, 1, 1 - par, False, pv_done)
                for h in range(HEADS):
                    if tail and h == OUT_BACK:
                        output_scalar_gate(a, c, o, n - 1)
                    if core:
                        exps(n, 2 * h)
                        exps(n, 2 * h + 1)
                    if front and h in TURNS:
                        t, rounds = TURNS[h]
                        qkv_scalar_rows(a, c, q, n + 1, t, 1 - par, rounds)
                    if front and h == 1:
                        qkv_scalar_hi(a, q, n + 1, 1, False)
                    if tail and h == MEAN + 1:
                        square(n - 1, 1 - par)
                    if norm and h == NORM_TURN:
                        norm_to_hi(n + 2)
                    if tail and h == OUT_TURN:
                        affine(n - 1)
                        out_hi(n - 1)
                    if front and h == MAX_TURN:
                        max_out(a, c, q, m, n + 1)

            a.wait_ge(w_in, 16)
            a.activation(w_hi_all[:], raw[:], ACT.Copy).then_inc(w_hi_done, 1)
            a.wait_ge(q.stacks_set, STACKS_SET)
            norm_to_hi(0)
            pipeline(a, step)

        @block.vector
        def _(v):
            def max_of(n, u):
                v.wait_ge(scores_done, UNITS * n + u + 1)
                col = HEADS * (u % 2) + u // 2
                v.tensor_reduce(block_max[:, col, :], ps[:, 4 + u % 2, 0:NB * P].rearrange("p (c k) -> p c k", c=NB),
                                AX.X, ALU.max).then_inc(max_done, 1)

            def join(n):
                v.wait_ge(max_done, UNITS * (n + 1))
                wait_from_one(v, m.max_turned, n)
                v.tensor_tensor(maxima[:, 1, :], block_max[:, :, 0], block_max[:, :, 1], ALU.max)\
                    .then_inc(max_joined, 1)
                v.tensor_copy(maxima[:, 0, :], block_max[:, :, 2]).then_inc(max_joined, 1)

            def combine(n, par, grp):
                at_n = PVG * n + grp
                v.wait_ge(pv_done, 2 * (at_n + 1))
                src = pv_bank(grp)
                v.reciprocal(denom[:, grp % 2, :], src[:, :, VW]).then_inc(denom_done, 1)
                v.wait_ge(denom_done, at_n + 1)
                v.tensor_tensor(parts[:, grp % 2, :, :, :].rearrange("p a b w -> p (a b) w"), src[:, :, 0:VW],
                                denom[:, grp % 2, :].unsqueeze(2).to_broadcast([P, 4 * BT, VW]), ALU.mult)\
                    .then_inc(parted, 2)
                v.wait_ge(parted, 2 * (at_n + 1))
                for hh in range(2):
                    at = parts[:, grp % 2, BT * hh:BT * hh + BT, :, :]
                    v.scalar_tensor_tensor(heads_out[par][:, :, 2 * grp + hh, :], at[:, :, 1, :], c.neg_lam[:, 0:1],
                                           at[:, :, 0, :], ALU.mult, ALU.add).then_inc(out_ready, 1)

            def per_head(ap):
                return ap[:].rearrange("p q h w -> p h q w")

            def norm_a(n, par):
                v.wait_ge(out_ready, HEADS * (n + 1))
                v.tensor_reduce(sums[:], per_head(heads_out[par]), AX.XY, ALU.add).then_inc(summed, 1)

            def norm_b(n, par):
                v.wait_ge(mean_done, n + 1)
                v.tensor_tensor(heads_out[par][:], heads_out[par][:],
                                ps[:, 6, 0:HEADS].unsqueeze(1).unsqueeze(3).to_broadcast([P, BT, HEADS, VW]),
                                ALU.subtract).then_inc(centred, 1)

            def norm_c(n):
                v.wait_ge(squared, n + 1)
                v.tensor_reduce(sq_sums[:], per_head(squares), AX.XY, ALU.add).then_inc(sq_summed, 1)

            def norm_d(n):
                v.wait_ge(var_done, n + 1)
                v.tensor_scalar(var[:], ps[:, 7, 0:HEADS], GN_EPS, None, ALU.add).then_inc(var_eps, 1)

            def step(n, par, front, core, tail, norm):
                if tail:
                    combine(n - 1, 1 - par, PVG - 1)
                    norm_a(n - 1, 1 - par)
                if front:
                    qkv_vector_rotate(v, c, q, n + 1, 0, rope, False)
                    qkv_vector_rotate(v, c, q, n + 1, 1, rope, False)
                if norm:
                    ln_vector_stats(v, s, n + 2)
                for h in range(3, HEADS):
                    if front and h == 3:
                        qkv_vector_rows(v, c, q, n + 1, 0, 1 - par)
                    if front and h == 6:
                        qkv_vector_rows(v, c, q, n + 1, 1, 1 - par)
                    if tail and h == MEAN:
                        norm_b(n - 1, 1 - par)
                    if norm and h == 6:
                        ln_vector_scale(v, s, n + 2)
                    if tail and h == VARIANCE - 1:
                        norm_c(n - 1)
                    if tail and h == VARIANCE:
                        norm_d(n - 1)
                    if front and h in ROW_SLOTS:
                        for u in ROW_SLOTS[h]:
                            max_of(n + 1, u)
                    if front and h == MAX_TURN:
                        join(n + 1)
                    if core and h % 2 == 1:
                        combine(n, par, (h - 3) // 2)
                    if tail and h == OUT_BACK:
                        output_vector_add(v, c, o, n - 1)

            qkv_vector_prepare(v, q)
            v.wait_ge(q.stacks_set, STACKS_SET)
            ln_vector_stats(v, s, 0)
            ln_vector_scale(v, s, 0)
            pipeline(v, step)

        @block.gpsimd
        def _(g):
            def cut(n, u):
                g.wait_ge(exp_done, UNITS * n + u + 1)
                g.sem_inc(s.passed)
                at = probs[:, u % 8, :].rearrange("p (c n) -> p c n", c=NB)[:, 0:NB:2, :]
                g.affine_select(out=at, in_=at, compare_op=ALU.is_ge, fill=0.0, base=0,
                                pattern=[[0, 2], [1, P]], channel_multiplier=-1).then_inc(cut_done, 1)

            def group_rstd(n):
                g.wait_ge(var_eps, n + 1)
                g.tensor_tensor(rstd[:], var[:], c.minus_half[:, 0:HEADS], ALU.pow).then_inc(rstd_done, 1)

            def normalise(n, par):
                g.wait_ge(rstd_done, n + 1)
                g.tensor_tensor(heads_out[par][:], heads_out[par][:],
                                rstd[:].unsqueeze(1).unsqueeze(3).to_broadcast([P, BT, HEADS, VW]), ALU.mult)\
                    .then_inc(normed, 1)

            def out_lo(n):
                g.wait_ge(o.o_hi_done, n + 1)
                g.tensor_tensor(o.o_lo[:], o_full[:], o.o_hi[:].bitcast(F32), ALU.subtract).then_inc(o.o_lo_done, 1)

            def norm_lo(m_):
                ln_gpsimd_lo(g, s, m_, lambda half: q.h_hi[:, half, :], lambda half: q.h_lo[:, half, :])

            def step(n, par, front, core, tail, norm):
                if front:
                    qkv_gpsimd_lo(g, q, n + 1, 0)
                for h in range(HEADS):
                    if core:
                        cut(n, 2 * h)
                        cut(n, 2 * h + 1)
                    if front and h == 1:
                        qkv_gpsimd_lo(g, q, n + 1, 1)
                    if norm and h == 2:
                        ln_gpsimd_rstd(g, s, n + 2)
                    if tail and h == VARIANCE:
                        group_rstd(n - 1)
                    if tail and h == VARIANCE + 1:
                        normalise(n - 1, 1 - par)
                    if norm and h == NORM_TURN + 1:
                        norm_lo(n + 2)
                    if tail and h == OUT_TURN + 1:
                        out_lo(n - 1)

            g.wait_ge(w_hi_done, 1)
            g.tensor_tensor(w_lo_all[:], raw[:], w_hi_all[:].bitcast(F32), ALU.subtract).then_inc(w_lo_done, 1)
            qkv_gpsimd_prepare(g, q)
            g.wait_ge(q.stacks_set, STACKS_SET)
            ln_gpsimd_rstd(g, s, 0)
            norm_lo(0)
            pipeline(g, step)

        @block.sync
        def _(sp):
            sp.dma_start(raw[:], args.w1).then_inc(w_in, 16)
            for n in range(B):
                send_maxima(sp, q, m, n, n % 2)
            sp.wait_ge(m.max_in, 32 * B)


def norm_all(nc, c):
    with ExitStack() as stack:
        def sb(name, shape, dt):
            return stack.enter_context(nc.sbuf_tensor("n_" + name, shape, dt))

        def sem(name):
            return new_semaphore(nc, c, stack, "n_" + name)

        s = ln_buffers(sb, sem, c, c.mod[1], SHIFT_B, SCALE_B, PT_, 0)
        block = stack.enter_context(nc.Block())

        @block.tensor
        def _(t_):
            with t_.Fori(0, PAIRS) as i:
                ln_tensor(t_, s, i)

        @block.scalar
        def _(a):
            with a.Fori(0, PAIRS) as i:
                ln_scalar(a, s, i)
                ln_scalar_hi(a, s, i, lambda half: c.h_hi[:, half, bass.ds(i * NP, NP)])

        @block.gpsimd
        def _(g):
            with g.Fori(0, PAIRS) as i:
                ln_gpsimd_rstd(g, s, i)
                ln_gpsimd_lo(g, s, i, lambda half: c.h_hi[:, half, bass.ds(i * NP, NP)],
                             lambda half: c.h_lo[:, half, bass.ds(i * NP, NP)])

        @block.vector
        def _(v):
            with v.Fori(0, PAIRS) as i:
                ln_vector_stats(v, s, i)
                ln_vector_scale(v, s, i)


def feed_forward(nc, c, args):
    with ExitStack() as stack:
        def sb(name, shape, dt):
            return stack.enter_context(nc.sbuf_tensor("f_" + name, shape, dt))

        def sem(name):
            return new_semaphore(nc, c, stack, "f_" + name)

        m = mlp_buffers(sb, sem, FFN_TILES)
        raw = sb("raw", [P, 2, WT], F32)
        N = FFN_TILES
        block = stack.enter_context(nc.Block())

        @block.sync
        def _(sp):
            for t in range(N):
                if t >= 2:
                    sp.wait_ge(m.w_lo_done, t - 1)
                sp.dma_start(raw[:, t % 2, :], args.ffn_w[t, :, :]).then_inc(m.raw_in[t % 2], 16)

        @block.tensor
        def _(t_):
            steps = N * (TOKENS // NP)

            def up(n):
                if n < N:
                    t_.wait_ge(m.w_lo_done, n + 1)
                mlp_up(t_, c, m, n, n, n % N, n // N, n < 2)

            up(0)
            up(1)
            for n in range(steps):
                if n % N == 0 and n:
                    t_.wait_ge(m.y_added, n // N)
                mlp_down(t_, c, m, n, n, n % N, n % N == 0, n % N == N - 1)
                if n + 2 < steps:
                    up(n + 2)

        @block.scalar
        def _(a):
            def split(t):
                a.wait_ge(m.raw_in[t % 2], 16 * (t // 2 + 1))
                a.activation(m.w_hi[t][:], raw[:, t % 2, :], ACT.Copy).then_inc(m.w_hi_done, 1)

            split(0)
            split(1)
            for n in range(N):
                mlp_silu(a, c, m, n, n, n < 2)
                mlp_hi(a, m, n, n, m.act_done, n < 4)
                if n + 2 < N:
                    split(n + 2)
            with a.Fori(1, TOKENS // NP) as i:
                for j in range(N):
                    mlp_silu(a, c, m, N * i + j, j, False)
                    mlp_hi(a, m, N * i + j, j, m.act_done, False)

        @block.gpsimd
        def _(g):
            def split(t):
                g.wait_ge(m.w_hi_done, t + 1)
                g.tensor_tensor(m.w_lo[t][:], raw[:, t % 2, :], m.w_hi[t][:].bitcast(F32), ALU.subtract)\
                    .then_inc(m.w_lo_done, 1)

            split(0)
            split(1)
            for n in range(N):
                mlp_lo(g, m, n, n)
                if n + 2 < N:
                    split(n + 2)
            with g.Fori(1, TOKENS // NP) as i:
                for j in range(N):
                    mlp_lo(g, m, N * i + j, j)

        @block.vector
        def _(v):
            def store_y(tb):
                v.wait_ge(m.down_done, N * (tb + 1))
                v.tensor_copy(c.yT[:, :, bass.ds(tb * NP, NP)], c.ps[:, 6:8, :]).then_inc(m.y_added, 1)

            for n in range(N):
                mlp_act(v, c, m, n, n, n < 2, weigh=False)
            with v.Fori(1, TOKENS // NP) as i:
                for j in range(N):
                    mlp_act(v, c, m, N * i + j, j, False, weigh=False)
                    if j == 0:
                        store_y(i - 1)
            store_y(TOKENS // NP - 1)


def clear_used(nc, c):
    numbers = sorted({s.num for s in c.used})
    with nc.Block() as block:
        @block.sync
        def _(sp):
            start = numbers[0]
            for a, b in zip(numbers, numbers[1:] + [None]):
                if b != a + 1:
                    sp.sem_clear(range(start, a + 1))
                    start = b
    c.used.clear()


def program(nc, args):
    c = Parts()
    c.used = []
    with ExitStack() as stack:
        def sb(name, shape, dt):
            return stack.enter_context(nc.sbuf_tensor(name, shape, dt))

        c.ps = stack.enter_context(nc.psum_tensor("ps", [P, 8, 512], F32))
        c.psflat = c.ps[:].rearrange("p b n -> p (b n)")
        c.x = sb("x_tokens", [P, TILES, D], F32)
        c.consts = sb("consts_t", [P, C_END], F32)
        c.ident = c.consts[:, C_ID:C_ID + P]
        c.ident_bf = sb("ident_bf", [P, P], BF16)
        c.mask_bf = sb("mask_bf", [P, 2 * P], BF16)
        c.minus_half = sb("minus_half", [P, HEADS], F32)
        c.mean_of = sb("mean_of", [P, P], F32)
        c.mod = [sb(f"mod{n}", [P, 6 * KD, B], F32) for n in range(2)]
        c.neg_lam = sb("neg_lam", [P, 1], F32)
        c.gn = sb("gn_wb", [P, 8], F32)

        def table(at, width):
            return c.consts[:, at:at + BT * width].rearrange("p (t w) -> p t w", t=BT)

        c.table = table
        with ExitStack() as inner:
            c.w0 = inner.enter_context(nc.sbuf_tensor("w0_raw", [P, KD, 1024], F32))
            c.w0_hi = inner.enter_context(nc.sbuf_tensor("w0_hi", [P, KD, 1024], F32R))
            c.w0_lo = inner.enter_context(nc.sbuf_tensor("w0_lo", [P, KD, 1024], F32R))
            setup(nc, c, args)
            attention0(nc, c)
        with ExitStack() as inner:
            c.h_hi = inner.enter_context(nc.sbuf_tensor("moe_h_hi", [P, KD, TOKENS], F32R))
            c.h_lo = inner.enter_context(nc.sbuf_tensor("moe_h_lo", [P, KD, TOKENS], F32R))
            c.cw_rows = inner.enter_context(nc.sbuf_tensor("cw_rows", [2 * E, TOKENS], F32R))
            c.yT = inner.enter_context(nc.sbuf_tensor("moe_yT", [P, KD, TOKENS], F32))
            route(nc, c, args)
            experts(nc, c, args)
            add_back_phase(nc, c, c.mod[0], "moe_")
        attention1(nc, c, args)
        clear_used(nc, c)
        with ExitStack() as inner:
            c.h_hi = inner.enter_context(nc.sbuf_tensor("ffn_h_hi", [P, KD, TOKENS], F32R))
            c.h_lo = inner.enter_context(nc.sbuf_tensor("ffn_h_lo", [P, KD, TOKENS], F32R))
            c.yT = inner.enter_context(nc.sbuf_tensor("ffn_yT", [P, KD, TOKENS], F32))
            norm_all(nc, c)
            feed_forward(nc, c, args)
            add_back_phase(nc, c, c.mod[1], "ffn_")
        out_done = stack.enter_context(nc.semaphore("out_done"))
        block = stack.enter_context(nc.Block())

        @block.sync
        def _(sp):
            for b in range(0, B, 2):
                sp.dma_start(args.out.rearrange("b (t p) d -> p (b t) d", p=P)[:, BT * b:BT * b + PT_, :],
                             c.x[:, BT * b:BT * b + PT_, :]).then_inc(out_done, 16)
            sp.wait_ge(out_done, 16 * PAIRS)


def constants():
    consts = np.zeros((P, C_END), np.float32)
    consts[:, C_ID:C_ID + P] = np.eye(P)
    above = np.where(np.arange(P)[None, :] > np.arange(P)[:, None], MASKED, 0.0)
    consts[:, C_MASK:C_MASK + 2 * P] = np.concatenate([above, above], 1)
    pos = np.arange(T, dtype=np.float32)[:, None]
    inv = (1.0 / np.float32(10000.0) ** (np.arange(0, 16, 2, dtype=np.float32) / np.float32(16))).astype(np.float32)
    ang = pos * inv[None, :]
    sin = np.sin(ang).reshape(BT, P, 8)
    cos = np.cos(ang).reshape(BT, P, 8)

    def put(at, table):
        w = table.shape[2]
        consts[:, at:at + BT * w] = table.transpose(1, 0, 2).reshape(P, BT * w)

    put(C_COS0, cos)
    put(C_SIN0A, -sin[:, :, 0:4])
    put(C_SIN0B, sin[:, :, 4:8])
    put(C_COS1, np.repeat(cos, 2, axis=2))
    put(C_SIN1A, -sin)
    put(C_SIN1B, sin)
    which = np.zeros((2 * E, MOE_TILES * P), np.float32)
    expert = np.arange(MOE_TILES * P) // MOE_D
    which[expert, np.arange(MOE_TILES * P)] = 1.0
    which[E + expert, np.arange(MOE_TILES * P)] = 1.0
    return consts, which


def kernel(**inputs):
    import numpy as _np
    import concourse.bacc as _bacc
    from concourse import mybir as _mybir
    from concourse.bass_utils import run_bass_kernel_spmd as _run

    a = {n: _np.asarray(v) for n, v in inputs.items()}
    nc = _bacc.Bacc("TRN2", target_bir_lowering=False, num_devices=1)
    arrays = {}

    def give(name, array):
        array = _np.ascontiguousarray(array)
        arrays["in_" + name] = array
        return nc.dram_tensor("in_" + name, array.shape, _mybir.dt.from_np(array.dtype), kind="ExternalInput").ap()

    def halves(m):
        return m.reshape(-1, 128, m.shape[1]).transpose(1, 0, 2)

    def tiles(gate, up, down):
        n = gate.shape[0] // 128
        def turned(w):
            return w.reshape(n, 128, 2, 128).transpose(0, 3, 2, 1).reshape(n, 128, 256)
        return _np.concatenate([turned(gate), turned(up), down.reshape(n, 128, 256)], axis=2)

    consts, which = constants()
    args = Parts()
    args.x = give("x", a["L0_attn_x"].reshape(16, 128, 256).transpose(1, 0, 2))
    args.c0 = give("c0", halves(a["L0_c"].T))
    args.c1 = give("c1", halves(a["L1_c"].T))
    args.wmod0 = give("wmod0", halves(a["L0_wmod"]))
    args.wmod1 = give("wmod1", halves(a["L1_wmod"]))
    args.w0 = give("w0", halves(_np.concatenate([a["L0_attn_wq"].T, a["L0_attn_wk"].T, a["L0_attn_wv"].T,
                                                 a["L0_attn_wo"].T], axis=1)))
    w1 = halves(_np.concatenate([a["L1_attn_Wq"], a["L1_attn_Wk"], a["L1_attn_Wv"]], axis=1)).reshape(128, -1)
    args.w1 = give("w1", _np.concatenate([w1, halves(a["L1_attn_Wo"]).reshape(128, -1)], axis=1))
    args.gate_w = give("gate_w", halves(a["L0_ffn_gate_w"].T))
    args.moe_w = give("moe_w", tiles(a["L0_ffn_w_gate"].reshape(-1, 256), a["L0_ffn_w_up"].reshape(-1, 256),
                                     a["L0_ffn_w_down"].transpose(0, 2, 1).reshape(-1, 256)))
    gate_up = a["L1_ffn_w_gate_up"]
    args.ffn_w = give("ffn_w", tiles(gate_up[0:1024], gate_up[1024:2048], a["L1_ffn_w_down"].T))
    args.gn = give("gn", _np.concatenate([a["L1_attn_gn_w"].reshape(4, 128).T, a["L1_attn_gn_b"].reshape(4, 128).T],
                                         axis=1))
    lam = _np.stack([a["L1_attn_lambda_q1"], a["L1_attn_lambda_k1"], a["L1_attn_lambda_q2"], a["L1_attn_lambda_k2"]])
    args.lam = give("lam", _np.broadcast_to(lam[None], (128, 4, 16)))
    args.consts = give("consts", consts)
    args.expert_of = give("expert_of", which)
    args.out = nc.dram_tensor("out", (8, 256, 256), _mybir.dt.float32, kind="ExternalOutput").ap()
    program(nc, args)
    r = _run(nc, [arrays], core_ids=[0])
    return r.results[0]["out"]
```

```python
from contextlib import ExitStack

import numpy as np

import concourse.bass as bass
from concourse import mybir

F32 = mybir.dt.float32
F32R = mybir.dt.float32r
BF16 = mybir.dt.bfloat16
ALU = mybir.AluOpType
ACT = mybir.ActivationFunctionType
AX = mybir.AxisListType

P = 128
B, T, D = 8, 256, 256
TOKENS = B * T
TILES = TOKENS // P
BT = T // P
KD = D // P
PAIRS = B // 2
PT_ = 2 * BT
NP = 2 * T
HW = 16
ROWS = 3 * HW
HEADS = 16
E, MOE_D, TOPK = 16, 176, 6
MOE_TILES = E * MOE_D // P
INTER = 1024
FFN_TILES = INTER // P
WT = 2 * KD * P + D
LN_EPS = 1e-5
GN_EPS = 1e-5
LAMBDA_INIT = 0.2
SCALE = 0.25
MASKED = -1e30
SHIFT_A, SCALE_A, GATE_A, SHIFT_B, SCALE_B, GATE_B = range(6)

C_ID = 0
C_MASK = C_ID + P
C_COS0 = C_MASK + 2 * P
C_SIN0A = C_COS0 + BT * 8
C_SIN0B = C_SIN0A + BT * 4
C_COS1 = C_SIN0B + BT * 4
C_SIN1A = C_COS1 + BT * 16
C_SIN1B = C_SIN1A + BT * 8
C_MEAN = C_SIN1B + BT * 8
C_END = C_MEAN + P


class Parts:
    pass


def new_semaphore(nc, c, stack, name):
    made = stack.enter_context(nc.semaphore(name))
    c.used.append(made)
    return made


def flat(ap):
    return ap.rearrange("p a b -> p (a b)")


def wait_from_one(eng, sem, value):
    if not isinstance(value, int) or value > 0:
        eng.wait_ge(sem, value)


def split_heads(ap, heads, width):
    return ap.rearrange("p (h w) -> p h w", h=heads, w=width)


def ln_slot(s, n):
    return n % 2 if s.slots == 2 else 0


def ln_vector_stats(v, s, n):
    at = ln_slot(s, n)
    for t in range(s.nt):
        v.bn_stats(s.stats[:, t, :], flat(s.x[:, bass.ds(s.nt * n + t, 1), :])).then_inc(s.ln_stats, 1)
    v.wait_ge(s.ln_stats, s.nt * n + s.nt)
    v.sem_inc(s.passed)
    for t in range(s.nt):
        v.bn_aggr(s.moments[:, at, t, :], s.stats[:, t, :]).then_inc(s.ln_moments, 1)
    v.wait_ge(s.ln_moments, s.nt * n + s.nt)
    v.tensor_scalar(s.var[:, at, :], s.moments[:, at, :, 1], LN_EPS, None, ALU.add).then_inc(s.ln_var, 1)


def ln_vector_scale(v, s, n):
    at = ln_slot(s, n)
    v.wait_ge(s.ln_rstd, n + 1)
    if s.slots == 2:
        wait_from_one(v, s.ln_turned, n - 1)
    for t in range(s.nt):
        v.tensor_scalar(s.xn[:, at, t, :], flat(s.x[:, bass.ds(s.nt * n + t, 1), :]), s.moments[:, at, t, 0:1],
                        s.rstd[:, at, t:t + 1], ALU.subtract, ALU.mult).then_inc(s.ln_xn, 1)


def ln_gpsimd_rstd(g, s, n):
    at = ln_slot(s, n)
    g.wait_ge(s.ln_var, n + 1)
    g.tensor_tensor(s.rstd[:, at, :], s.var[:, at, :], s.minus_half[:, 0:s.nt], ALU.pow).then_inc(s.ln_rstd, 1)


def ln_place(s, n, half, at, cols):
    if s.nt * P * KD > 512:
        return s.ps[:, s.bank + KD * ln_slot(s, n) + half, at:at + cols]
    return s.ps[:, s.bank, half * s.nt * P + at:half * s.nt * P + at + cols]


def ln_tensor(t_, s, n):
    t_.wait_ge(s.ln_xn, s.nt * n + s.nt)
    if s.slots == 2:
        wait_from_one(t_, s.ln_h, KD * s.nt // BT * (n - 1))
    for half in range(KD):
        for t in range(s.nt):
            mm = t_.transpose(ln_place(s, n, half, t * P, P), s.xn[:, ln_slot(s, n), t, half * P:(half + 1) * P],
                              s.ident)
    mm.then_inc(s.ln_turned, 1)


def ln_scalar(a, s, n, h_out):
    a.wait_ge(s.ln_turned, n + 1)
    for half in range(KD):
        for b in range(s.nt // BT):
            a.activation(h_out(half, b), ln_place(s, n, half, b * T, T), ACT.Identity,
                         scale=s.mod[:, KD * s.scale + half, bass.ds(s.nt // BT * n + b, 1)],
                         bias=s.mod[:, KD * s.shift + half, bass.ds(s.nt // BT * n + b, 1)]).then_inc(s.ln_h, 1)


def ln_buffers(sb, sem, c, mod, shift, scale, nt, bank, slots=1):
    s = Parts()
    s.x = c.x
    s.ps = c.ps
    s.ident = c.ident
    s.minus_half = c.minus_half
    s.mod = mod
    s.shift = shift
    s.scale = scale
    s.nt = nt
    s.bank = bank
    s.slots = slots
    s.stats = sb("ln_stats_t", [P, nt, 6], F32)
    s.moments = sb("ln_moments_t", [P, slots, nt, 2], F32)
    s.var = sb("ln_var_t", [P, slots, nt], F32)
    s.rstd = sb("ln_rstd_t", [P, slots, nt], F32)
    s.xn = sb("ln_xn_t", [P, slots, nt, D], F32)
    s.ln_stats = sem("ln_stats")
    s.ln_moments = sem("ln_moments")
    s.ln_var = sem("ln_var")
    s.ln_rstd = sem("ln_rstd")
    s.ln_xn = sem("ln_xn")
    s.ln_turned = sem("ln_turned")
    s.ln_h = sem("ln_h")
    s.passed = sem("passed")
    return s


def ln_all_buffers(sb, sem, s):
    s.h = sb("ln_h_t", [P, 2, KD, NP], F32)
    s.ln_hi, s.ln_lo = sem("ln_hi"), sem("ln_lo")


def ln_all_scalar(a, c, s, h_read=None):
    for i in range(PAIRS):
        if i >= 2:
            a.wait_ge(s.ln_lo, i - 1)
            if h_read is not None:
                a.wait_ge(h_read, i - 1)
        ln_scalar(a, s, i, lambda half, b: s.h[:, i % 2, half, b * T:(b + 1) * T])
        a.wait_ge(s.ln_h, 2 * KD * (i + 1))
        a.activation(c.h_hi[:, :, i * NP:(i + 1) * NP], s.h[:, i % 2, :, :], ACT.Copy).then_inc(s.ln_hi, 1)


def ln_all_gpsimd(g, c, s):
    ln_gpsimd_rstd(g, s, 0)
    for i in range(PAIRS):
        if i + 1 < PAIRS:
            ln_gpsimd_rstd(g, s, i + 1)
        at = slice(i * NP, (i + 1) * NP)
        g.wait_ge(s.ln_hi, i + 1)
        g.tensor_tensor(c.h_lo[:, :, at], s.h[:, i % 2, :, :], c.h_hi[:, :, at].bitcast(F32), ALU.subtract)\
            .then_inc(s.ln_lo, 1)


def ln_all_vector(v, s):
    ln_vector_stats(v, s, 0)
    for i in range(PAIRS):
        if i + 1 < PAIRS:
            ln_vector_stats(v, s, i + 1)
        ln_vector_scale(v, s, i)


def qkv_buffers(sb, sem, n_q, n_k, n_v, v_width):
    q = Parts()
    q.n_q = n_q
    q.n_k = n_k
    q.n_v = n_v
    q.v_width = v_width
    q.n_qk = n_q + n_k
    q.h = sb("h", [P, KD, T], F32)
    q.cosine = sb("rope_cos_part", [P, q.n_qk * HW], F32)
    q.sine = sb("rope_sin_part", [P, q.n_qk * HW], F32)
    q.roped = sb("roped", [P, 2, q.n_qk * HW], F32)
    q.q_stack = [sb(f"q_stack{j}", [P, n_q * 64], F32) for j in range(2)]
    q.k_stack = [sb(f"k_stack{j}", [P, n_k * 64], F32) for j in range(2)]
    q.q_rows = sb("q_rows", [P, 2, n_q // 2, T], F32R)
    q.k_pad = [sb(f"k_pad{j}", [P, 2, n_k // 2, T], F32R) for j in range(2)]
    q.v_pad = 64 - v_width
    q.v = sb("v_strips", [P, 2, BT, n_v, 3 * q.v_pad + 2 * v_width], F32)
    q.qkv_done = sem("qkv_done")
    q.v_copied = sem("v_copied")
    q.plain_copied = sem("plain_copied")
    q.rope_parts = sem("rope_parts")
    q.roped_ready = sem("roped_ready")
    q.stack_hi = sem("stack_hi")
    q.stack_lo = sem("stack_lo")
    q.rows_turned = sem("rows_turned")
    q.q_rows_ready = sem("q_rows_ready")
    q.k_rows_ready = [sem(f"k_rows_ready{j}") for j in range(2)]
    q.stacks_set = sem("stacks_set")
    q.strips_set = sem("strips_set")
    q.pads_set = sem("pads_set")
    q.q_rounds, q.k_rounds = n_q // 8, n_k // 8
    q.rounds = q.q_rounds + q.k_rounds
    return q


def value_window(q, par, kt, head, j):
    at = q.v_pad - q.v_width * j
    return q.v[:, par, kt, head, at:at + P]


def stack_view(stack, heads):
    return stack[:, :].rearrange("p (h s w) -> p h s w", h=heads, s=4, w=HW)


def qkv_gpsimd_stacks(g, q):
    for j in range(2):
        g.memset(q.q_stack[j][:], 0.0).then_inc(q.stacks_set, 1)
        g.memset(q.k_stack[j][:], -1.0).then_inc(q.stacks_set, 1)


def qkv_gpsimd_strips(g, q):
    pad, w = q.v_pad, q.v_width
    for at, end, fill in ((0, pad, 0.0), (pad + w, 2 * pad + w, 0.0), (2 * pad + w, 2 * pad + 2 * w, 1.0),
                          (2 * pad + 2 * w, 3 * pad + 2 * w, 0.0)):
        g.memset(q.v[:, :, :, :, at:end], fill).then_inc(q.strips_set, 1)


def qkv_vector_pads(v, q):
    for j in range(2):
        other = 64 * (1 - j)
        v.memset(q.k_pad[j][other:other + 64, :, :, :].bitcast(F32), 0.0).then_inc(q.pads_set, 1)


def tile_banks(t):
    return 6 - 2 * t


def qkv_project(t_, c, s, q, w, n, t, halves=(0, 1)):
    t_.wait_ge(s.ln_h, KD * n + KD)
    b0 = tile_banks(t)
    tok = slice(t * P, (t + 1) * P)
    for k in halves:
        for bank, lo, hi in ((b0, 0, 512), (b0 + 1, 512, 768)):
            mm = t_.matmul(c.ps[:, bank, 0:hi - lo], q.h[:, k, tok], w[:, k, lo:hi],
                           start=(k == 0), stop=(k == KD - 1))
    if KD - 1 in halves:
        mm.then_inc(q.qkv_done, 1)


def qkv_turn(t_, c, q, n, t, rounds):
    t_.wait_ge(q.stack_lo, 2 * (BT * n + t + 1))
    for r in rounds:
        if r >= 2:
            if r - 2 < q.q_rounds:
                t_.wait_ge(q.q_rows_ready, q.q_rounds * (BT * n + t) + r - 1)
            else:
                for j in range(2):
                    t_.wait_ge(q.k_rows_ready[j], q.k_rounds * (BT * n + t) + r - 1 - q.q_rounds)
        src, at = (q.q_stack, r) if r < q.q_rounds else (q.k_stack, r - q.q_rounds)
        for j in range(4):
            mm = t_.transpose(c.ps[:, tile_banks(t) + r % 2, j * P:(j + 1) * P],
                              src[t][:, (4 * at + j) * P:(4 * at + j + 1) * P], c.ident)
        mm.then_inc(q.rows_turned, 1)


def qkv_scalar_copies(a, c, q, n, t, par, plain, pv_done):
    b0 = tile_banks(t)
    a.wait_ge(q.qkv_done, BT * n + t + 1)
    if t == 0:
        wait_from_one(a, pv_done, HEADS * (n - 1))
    v_from = q.n_qk * HW - 512
    a.activation(q.v[:, par, t, :, q.v_pad:q.v_pad + q.v_width],
                 split_heads(c.ps[:, b0 + 1, v_from:v_from + q.n_v * q.v_width], q.n_v, q.v_width),
                 ACT.Copy).then_inc(q.v_copied, 1)
    if plain:
        wait_from_one(a, q.stack_lo, 2 * (BT * (n - 1) + t + 1))
        a.activation(split_heads(q.roped[:, t, :], q.n_qk, HW)[:, :, 8:16],
                     split_heads(c.ps[:, b0, :], q.n_qk, HW)[:, :, 8:16], ACT.Copy).then_inc(q.plain_copied, 1)


def qkv_scalar_hi(a, q, n, t, plain, parts=("q", "k")):
    a.wait_ge(q.roped_ready, BT * n + t + 1)
    if plain:
        a.wait_ge(q.plain_copied, BT * n + t + 1)
    wait_from_one(a, q.rows_turned, q.rounds * (BT * (n - 1) + t + 1))
    roped = split_heads(q.roped[:, t, :], q.n_qk, HW)
    qs = stack_view(q.q_stack[t], q.n_q).bitcast(F32R)
    ks = stack_view(q.k_stack[t], q.n_k).bitcast(F32R)
    if "q" in parts:
        a.activation(qs[:, :, 0:3:2, :], roped[:, 0:q.n_q, :].unsqueeze(2).to_broadcast([P, q.n_q, 2, HW]),
                     ACT.Copy).then_inc(q.stack_hi, 1)
    if "k" in parts:
        a.activation(ks[:, :, 0:2, :], roped[:, q.n_q:q.n_qk, :].unsqueeze(2).to_broadcast([P, q.n_k, 2, HW]),
                     ACT.Copy).then_inc(q.stack_hi, 1)


def qkv_gpsimd_lo(g, q, n, t):
    g.wait_ge(q.stack_hi, 2 * (BT * n + t + 1))
    roped = split_heads(q.roped[:, t, :], q.n_qk, HW)
    qs, ks = stack_view(q.q_stack[t], q.n_q), stack_view(q.k_stack[t], q.n_k)
    g.tensor_tensor(qs[:, :, 1, :].bitcast(F32R), roped[:, 0:q.n_q, :], qs[:, :, 0, :], ALU.subtract)\
        .then_inc(q.stack_lo, 1)
    g.tensor_tensor(ks[:, :, 2, :].bitcast(F32R), roped[:, q.n_q:q.n_qk, :], ks[:, :, 0, :], ALU.subtract)\
        .then_inc(q.stack_lo, 1)


def qkv_scalar_rows(a, c, q, n, t, par, rounds):
    for r in rounds:
        if r < q.q_rounds:
            a.wait_ge(q.rows_turned, q.rounds * (BT * n + t) + r + 1)
            a.activation(q.q_rows[:, par, 4 * r:4 * r + 4, t * P:(t + 1) * P],
                         c.ps[:, tile_banks(t) + r % 2, :].rearrange("p (j n) -> p j n", j=4), ACT.Copy)\
                .then_inc(q.q_rows_ready, 1)
        else:
            at = r - q.q_rounds
            a.wait_ge(q.rows_turned, q.rounds * (BT * n + t) + r + 1)
            a.wait_ge(q.k_rows_ready[0], q.k_rounds * (BT * n + t) + at + 1)
            a.activation(q.k_pad[1][64:128, par, 4 * at:4 * at + 4, t * P:(t + 1) * P],
                         c.ps[64:128, tile_banks(t) + r % 2, :].rearrange("p (j n) -> p j n", j=4), ACT.Copy)\
                .then_inc(q.k_rows_ready[1], 1)


def qkv_vector_rows(v, c, q, n, t, par):
    for r in range(q.k_rounds):
        at = q.q_rounds + r
        v.wait_ge(q.rows_turned, q.rounds * (BT * n + t) + at + 1)
        v.tensor_copy(q.k_pad[0][0:64, par, 4 * r:4 * r + 4, t * P:(t + 1) * P],
                      c.ps[0:64, tile_banks(t) + at % 2, :].rearrange("p (j n) -> p j n", j=4))\
            .then_inc(q.k_rows_ready[0], 1)


def qkv_vector_rotate(v, c, q, n, t, rope, plain):
    b0 = tile_banks(t)
    v.wait_ge(q.plain_copied if plain else q.v_copied, BT * n + t + 1)
    x = split_heads(c.psflat[:, b0 * 512:b0 * 512 + q.n_qk * HW], q.n_qk, HW)
    cp = split_heads(q.cosine[:, :], q.n_qk, HW)
    sp = split_heads(q.sine[:, :], q.n_qk, HW)
    out = split_heads(q.roped[:, t, :], q.n_qk, HW)
    w, half = rope.width, rope.width // 2
    cos = rope.cos[:, t, :].unsqueeze(1).to_broadcast([P, q.n_qk, w])
    sin_a = rope.sin_a[:, t, :].unsqueeze(1).to_broadcast([P, q.n_qk, half])
    sin_b = rope.sin_b[:, t, :].unsqueeze(1).to_broadcast([P, q.n_qk, half])
    wait_from_one(v, q.roped_ready, BT * n + t)
    v.tensor_tensor(cp[:, :, 0:w], x[:, :, 0:w], cos, ALU.mult).then_inc(q.rope_parts, 1)
    v.tensor_tensor(rope.first(sp), rope.second(x), sin_a, ALU.mult).then_inc(q.rope_parts, 1)
    v.tensor_tensor(rope.second(sp), rope.first(x), sin_b, ALU.mult).then_inc(q.rope_parts, 1)
    v.wait_ge(q.rope_parts, 3 * (BT * n + t + 1))
    wait_from_one(v, q.stack_lo, 2 * (BT * (n - 1) + t + 1))
    v.tensor_tensor(out[:, :, 0:w], cp[:, :, 0:w], sp[:, :, 0:w], ALU.add).then_inc(q.roped_ready, 1)


def modulation_buffers(sb, sem):
    mo = Parts()
    mo.sign = sb("gate_sign", [P, 2 * KD * B], F32)
    mo.size = sb("gate_size", [P, 2 * KD * B], F32)
    mo.done, mo.read, mo.sign_done, mo.size_done, mo.gates_done = (
        sem(n) for n in ("mod_done", "mod_read", "sign_done", "size_done", "gates_done"))
    return mo


def modulation_tensor(t_, c, mo, n):
    t_.wait_ge(c.wmod_in[n], 16)
    for col in range(6 * KD):
        for k in range(KD):
            mm = t_.matmul(c.ps[:, 5, col * B:(col + 1) * B], c.wmod[n][:, k, col * P:(col + 1) * P],
                           c.cond_silu[n][:, k, :], start=(k == 0), stop=(k == KD - 1))
    mm.then_inc(mo.done, 1)


def modulation_vector(v, c, mo, n):
    v.wait_ge(mo.done, 1)
    v.tensor_copy(flat(c.mod[n][:]), c.ps[:, 5, 0:6 * KD * B]).then_inc(mo.read, 1)
    v.wait_ge(mo.read, 1)
    for part in (SCALE_A, SCALE_B):
        at = c.mod[n][:, KD * part:KD * part + KD, :]
        v.tensor_scalar(at, at, 1.0, None, ALU.add).then_inc(mo.read, 1)
    gates = [(slice(j * KD * B, (j + 1) * KD * B), flat(c.mod[n][:, KD * part:KD * part + KD, :]))
             for j, part in enumerate((GATE_A, GATE_B))]
    for at, g in gates:
        v.tensor_scalar(mo.sign[:, at], g, 0.0, 2.0, ALU.is_ge, ALU.mult).then_inc(mo.sign_done, 1)
        v.tensor_scalar(mo.size[:, at], g, -1.0, None, ALU.mult).then_inc(mo.sign_done, 1)
    v.wait_ge(mo.sign_done, 4)
    for at, g in gates:
        v.scalar_tensor_tensor(mo.size[:, at], mo.size[:, at], 0.25, g, ALU.max, ALU.max).then_inc(mo.size_done, 1)
    v.wait_ge(mo.size_done, 2)
    for at, g in gates:
        v.scalar_tensor_tensor(g, mo.sign[:, at], -1.0, mo.size[:, at], ALU.add, ALU.mult).then_inc(mo.gates_done, 1)


def setup(nc, c, args):
    with ExitStack() as stack:
        def sb(name, shape, dt):
            return stack.enter_context(nc.sbuf_tensor(name, shape, dt))

        def sem(name):
            return new_semaphore(nc, c, stack, name)

        cond = [sb(f"cond{n}", [P, KD, B], F32) for n in range(2)]
        mo = modulation_buffers(sb, sem)
        lam_in = sb("lam_in", [P, 4, HW], F32)
        lam_prod = sb("lam_prod", [P, 2, HW], F32)
        lam_sum = sb("lam_sum", [P, 2], F32)
        lam_exp = sb("lam_exp", [P, 2], F32)

        consts_in, x_in, cond_in, attn_in, lam_loaded, gn_in = (
            sem(n) for n in ("consts_in", "x_in", "cond_in", "attn_in", "lam_loaded", "gn_in"))
        silu_done = sem("silu_done")
        lam_mul, lam_added, lam_exped, lam_done = (sem(n) for n in ("lam_mul", "lam_added", "lam_exped", "lam_done"))
        fills = sem("fills")
        block = stack.enter_context(nc.Block())

        @block.sync
        def _(sp):
            sp.dma_start(cond[0][:], args.c0).then_inc(cond_in, 16)
            sp.dma_start(cond[1][:], args.c1).then_inc(cond_in, 16)
            sp.dma_start(c.wmod[0][:], args.wmod0).then_inc(c.wmod_in[0], 16)
            sp.dma_start(c.consts[:], args.consts).then_inc(consts_in, 16)
            sp.dma_start(c.x[:], args.x).then_inc(x_in, 16)
            sp.dma_start(c.wmod[1][:], args.wmod1).then_inc(c.wmod_in[1], 16)
            sp.wait_ge(consts_in, 16)
            sp.wait_ge(x_in, 16)

        @block.scalar
        def _(a):
            a.dma_start(c.w0[:], args.w0).then_inc(attn_in, 16)
            a.dma_start(lam_in[:], args.lam).then_inc(lam_loaded, 16)
            a.dma_start(c.gn[:], args.gn).then_inc(gn_in, 16)
            a.wait_ge(cond_in, 32)
            for n in range(2):
                a.activation(flat(c.cond_silu[n][:]), flat(cond[n][:]), ACT.Silu).then_inc(silu_done, 1)
            a.wait_ge(lam_added, 1)
            a.activation(lam_exp[:], lam_sum[:], ACT.Exp).then_inc(lam_exped, 1)
            a.dma_start(c.w1[:], args.w1).then_inc(c.w1_in, 16)
            a.wait_ge(attn_in, 16)

        @block.gpsimd
        def _(g):
            g.memset(c.minus_half[:], -0.5).then_inc(fills, 1)
            g.wait_ge(consts_in, 16)
            g.tensor_copy(c.ident_bf[:], c.consts[:, C_ID:C_ID + P]).then_inc(fills, 1)
            g.tensor_copy(c.mask_bf[:], c.consts[:, C_MASK:C_MASK + 2 * P]).then_inc(fills, 1)

        @block.tensor
        def _(t_):
            t_.wait_ge(silu_done, 1)
            modulation_tensor(t_, c, mo, 0)

        @block.vector
        def _(v):
            v.wait_ge(lam_loaded, 16)
            v.tensor_tensor(lam_prod[:], lam_in[:, 0:4:2, :], lam_in[:, 1:4:2, :], ALU.mult).then_inc(lam_mul, 1)
            v.wait_ge(lam_mul, 1)
            v.tensor_reduce(lam_sum[:], lam_prod[:], AX.X, ALU.add).then_inc(lam_added, 1)
            modulation_vector(v, c, mo, 0)
            v.wait_ge(lam_exped, 1)
            v.scalar_tensor_tensor(c.neg_lam[:], lam_exp[:, 1:2], -LAMBDA_INIT, lam_exp[:, 0:1],
                                   ALU.add, ALU.subtract).then_inc(lam_done, 1)
            v.wait_ge(gn_in, 16)
            v.tensor_scalar(c.gn[:], c.gn[:], 1.0 - LAMBDA_INIT, None, ALU.mult).then_inc(lam_done, 1)


def pipeline(eng, step):
    step(-1, 1, True, False, False, True)
    step(0, 0, True, True, False, True)
    step(1, 1, True, True, True, True)
    with eng.Fori(0, (B - 4) // 2) as i:
        step(2 * i + 2, 0, True, True, True, True)
        step(2 * i + 3, 1, True, True, True, True)
    step(B - 2, 0, True, True, True, False)
    step(B - 1, 1, False, True, True, False)
    step(B, 0, False, False, True, False)


def output_buffers(sb, sem, f_tiles, wo, mod):
    o = Parts()
    o.f_tiles = f_tiles
    o.wo = wo
    o.mod = mod
    o.o = sb("o", [P, f_tiles, T], F32)
    o.y = sb("y", [P, KD, T], F32)
    o.o_ready = sem("o_ready")
    o.y_done = sem("y_done")
    o.y_gated = sem("y_gated")
    o.y_turned = sem("y_turned")
    o.x_added = sem("x_added")
    return o


def output_tensor(t_, c, o, n):
    t_.wait_ge(o.o_ready, 4 * (n + 1))
    for dh in range(KD):
        for f in range(o.f_tiles):
            mm = t_.matmul(c.ps[:, 7, dh * T:(dh + 1) * T], o.wo[:, f, dh * P:(dh + 1) * P], o.o[:, f, :],
                           start=(f == 0), stop=(f == o.f_tiles - 1))
    mm.then_inc(o.y_done, 1)


def output_scalar_gate(a, c, o, n):
    a.wait_ge(o.y_done, n + 1)
    for dh in range(KD):
        a.activation(o.y[:, dh, :], c.ps[:, 7, dh * T:(dh + 1) * T], ACT.Copy,
                     scale=o.mod[:, KD * GATE_A + dh, bass.ds(n, 1)]).then_inc(o.y_gated, 1)


def output_tensor_back(t_, c, o, n):
    t_.wait_ge(o.y_gated, KD * (n + 1))
    for t in range(BT):
        for dh in range(KD):
            mm = t_.transpose(c.ps[:, 6, t * D + dh * P:t * D + (dh + 1) * P],
                              o.y[:, dh, t * P:(t + 1) * P], c.ident)
    mm.then_inc(o.y_turned, 1)


def output_vector_add(v, c, o, n):
    v.wait_ge(o.y_turned, n + 1)
    x = flat(c.x[:, bass.ds(BT * n, BT), :])
    v.tensor_tensor(x, x, c.ps[:, 6, :], ALU.add).then_inc(o.x_added, 1)


def send_maxima(sp, q, m, n, par):
    pairs = q.n_q // 2
    sp.wait_ge(m.max_rows_ready, n + 1)
    for half in range(2):
        row = 64 * half + ROWS
        sp.dma_start(q.q_rows[row:row + 1, par, :, :].bitcast(F32),
                     m.max_rows[pairs * half:pairs * (half + 1), :].bitcast(F32)).then_inc(m.max_in, 16)


def max_out(a, c, q, m, n):
    a.wait_ge(m.max_turned, n + 1)
    wait_from_one(a, m.max_in, 32 * n)
    a.activation(m.max_rows[:, :], c.ps[0:q.n_q, 4, 0:T], ACT.Copy).then_inc(m.max_rows_ready, 1)


def attention0(nc, c):
    with ExitStack() as stack:
        def sb(name, shape, dt):
            return stack.enter_context(nc.sbuf_tensor("a0_" + name, shape, dt))

        def sem(name):
            return new_semaphore(nc, c, stack, "a0_" + name)

        s = ln_buffers(sb, sem, c, c.mod[0], SHIFT_A, SCALE_A, BT, 7)
        q = qkv_buffers(sb, sem, HEADS, HEADS, HEADS, HW)
        o = output_buffers(sb, sem, KD, c.w0[:, :, 768:1024], c.mod[0])
        m = Parts()
        m.max_rows = sb("max_rows", [HEADS, T], F32R)
        m.max_turned, m.max_rows_ready, m.max_in = (sem(n) for n in ("max_turned", "max_rows_ready", "max_in"))
        maxima = sb("maxima", [P, BT, HEADS], F32)
        probs = sb("probs", [P, 4, BT * T], F32)
        log_sum = sb("log_sum", [64, 2 * T], F32)
        inverse = sb("inverse", [64, 2 * T], F32)
        scores_done, max_done = sem("scores_done"), sem("max_done")
        keyed_done, exp_done, pv_done, logged, inverted = (
            sem(n) for n in ("keyed_done", "exp_done", "pv_done", "logged", "inverted"))
        rope = Parts()
        rope.width = 8
        rope.first = lambda a: a[:, :, 0:4]
        rope.second = lambda a: a[:, :, 4:8]
        rope.cos = c.table(C_COS0, 8)
        rope.sin_a = c.table(C_SIN0A, 4)
        rope.sin_b = c.table(C_SIN0B, 4)
        ps = c.ps
        TURNS = {3: (0, (0, 1)), 4: (0, (2, 3)), 5: (1, (0, 1)), 6: (1, (2, 3))}
        ROW_SLOTS = {8 + j: (2 * j, 2 * j + 1) for j in range(8)}
        OUT_PROJECT, OUT_BACK, NORM_TURN, MAX_TURN = 7, 10, 12, 15
        FIRST_ROWS = min(ROW_SLOTS)
        block = stack.enter_context(nc.Block())

        @block.tensor
        def _(t_):
            def row_scores(n, par, h):
                if h >= 2:
                    t_.wait_ge(max_done, HEADS * n + h - 1)
                for qt in range(BT):
                    mm = t_.matmul(ps[:, 4 + h % 2, qt * T:(qt + 1) * T],
                                   q.q_rows[:, par, h // 2, qt * P:(qt + 1) * P],
                                   q.k_pad[h % 2][:, par, h // 2, :], start=(qt == 0), stop=(qt == BT - 1),
                                   skip_group_check=True)
                mm.then_inc(scores_done, 1)

            def turn_maxima(n):
                t_.wait_ge(max_done, HEADS * (n + 1))
                for qt in range(BT):
                    mm = t_.transpose(ps[0:HEADS, 4, qt * P:(qt + 1) * P], maxima[:, qt, :], c.ident)
                mm.then_inc(m.max_turned, 1)

            def key_scores(n, par, h):
                if h == 0:
                    t_.wait_ge(m.max_in, 32 * (n + 1))
                wait_from_one(t_, exp_done, HEADS * n + h - 1)
                for kt in range(BT):
                    mm = t_.matmul(ps[:, h % 2, kt * T:(kt + 1) * T],
                                   q.k_pad[h % 2][:, par, h // 2, kt * P:(kt + 1) * P],
                                   q.q_rows[:, par, h // 2, :], start=(kt == 0), stop=(kt == BT - 1),
                                   skip_group_check=True)
                mm.then_inc(keyed_done, 1)

            def weigh(n, par, h, between=()):
                t_.wait_ge(exp_done, HEADS * n + h + 1)
                if h % 8 == 0:
                    wait_from_one(t_, o.o_ready, 4 * (n - 1) + 2 * (h // 8) + 2)
                for kt in range(BT):
                    if kt == 1:
                        for u in between:
                            row_scores(n + 1, 1 - par, u)
                    mm = t_.matmul(ps[:, 2 + h // 8, h // 4 % 2 * T:(h // 4 % 2 + 1) * T],
                                   value_window(q, par, kt, h, h % 4), probs[:, h % 4, kt * T:(kt + 1) * T],
                                   start=(h % 8 == 0 and kt == 0), stop=(h % 8 == 7 and kt == BT - 1),
                                   skip_group_check=True)
                mm.then_inc(pv_done, 1)

            def step(n, par, front, core, tail, norm):
                if tail:
                    weigh(n - 1, 1 - par, HEADS - 2)
                if front:
                    wait_from_one(t_, o.x_added, n - 1)
                    qkv_project(t_, c, s, q, c.w0[:, :, 0:768], n + 1, 0, (0,))
                if tail:
                    weigh(n - 1, 1 - par, HEADS - 1)
                if front:
                    qkv_project(t_, c, s, q, c.w0[:, :, 0:768], n + 1, 0, (1,))
                    wait_from_one(t_, m.max_rows_ready, n + 1)
                    qkv_project(t_, c, s, q, c.w0[:, :, 0:768], n + 1, 1)
                for h in range(HEADS):
                    rows = list(ROW_SLOTS[h]) if front and h in ROW_SLOTS and h > FIRST_ROWS else []
                    if front and not core and h == 0:
                        t_.wait_ge(q.pads_set, 2)
                    if core and not tail and h == 2:
                        t_.wait_ge(q.strips_set, 4)
                    if core:
                        key_scores(n, par, h)
                        if h >= 2:
                            weigh(n, par, h - 2, rows[0:1])
                            rows = rows[1:]
                    if front and h == FIRST_ROWS:
                        t_.wait_ge(q.q_rows_ready, q.q_rounds * BT * (n + 2))
                        for j in range(2):
                            t_.wait_ge(q.k_rows_ready[j], q.k_rounds * BT * (n + 2))
                        rows = ROW_SLOTS[h]
                    for u in rows:
                        row_scores(n + 1, 1 - par, u)
                    if front and h in TURNS:
                        t, rounds = TURNS[h]
                        qkv_turn(t_, c, q, n + 1, t, rounds)
                    if tail and h == OUT_PROJECT:
                        output_tensor(t_, c, o, n - 1)
                    if tail and h == OUT_BACK:
                        output_tensor_back(t_, c, o, n - 1)
                    if norm and h == NORM_TURN:
                        if tail:
                            t_.wait_ge(o.y_gated, KD * n)
                        ln_tensor(t_, s, n + 2)
                    if front and h == MAX_TURN:
                        turn_maxima(n + 1)

            ln_tensor(t_, s, 0)
            pipeline(t_, step)

        @block.scalar
        def _(a):
            def exps(n, h):
                a.wait_ge(keyed_done, HEADS * n + h + 1)
                wait_from_one(a, pv_done, HEADS * n + h - 3)
                a.activation(probs[:, h % 4, :], ps[:, h % 2, :], ACT.Exp, scale=SCALE).then_inc(exp_done, 1)

            def invert_sums(n, f):
                a.wait_ge(pv_done, HEADS * n + 8 * (f + 1))
                wait_from_one(a, inverted, 2 * n + f)
                a.activation(log_sum[:], ps[64:128, 2 + f, :], ACT.Ln).then_inc(logged, 1)
                a.wait_ge(logged, 2 * n + f + 1)
                wait_from_one(a, o.o_ready, 4 * n + 2 * f)
                a.activation(inverse[:], log_sum[:], ACT.Exp, scale=-1.0).then_inc(inverted, 1)

            def norm_out(m_):
                wait_from_one(a, q.qkv_done, BT * m_)
                ln_scalar(a, s, m_, lambda half, b: q.h[:, half, :])

            def step(n, par, front, core, tail, norm):
                if front:
                    qkv_scalar_copies(a, c, q, n + 1, 0, 1 - par, True, pv_done)
                if tail:
                    invert_sums(n - 1, 1)
                if front:
                    qkv_scalar_copies(a, c, q, n + 1, 1, 1 - par, True, pv_done)
                for h in range(HEADS):
                    if core:
                        exps(n, h)
                    if front and h in TURNS:
                        t, rounds = TURNS[h]
                        qkv_scalar_rows(a, c, q, n + 1, t, 1 - par, rounds)
                    if front and h in (0, 2):
                        qkv_scalar_hi(a, q, n + 1, h // 2, True)
                    if tail and h == OUT_PROJECT:
                        output_scalar_gate(a, c, o, n - 1)
                    if core and h == 10:
                        invert_sums(n, 0)
                    if norm and h == NORM_TURN:
                        norm_out(n + 2)
                    if front and h == MAX_TURN:
                        max_out(a, c, q, m, n + 1)

            a.preload_act_table_set("natural_log_exp_and_others")
            norm_out(0)
            a.wait_ge(q.stacks_set, 4)
            pipeline(a, step)

        @block.vector
        def _(v):
            def max_of(n, h):
                v.wait_ge(scores_done, HEADS * n + h + 1)
                col = HEADS // 2 * (h % 2) + h // 2
                v.tensor_reduce(maxima[:, :, col:col + 1],
                                ps[:, 4 + h % 2, :].rearrange("p (q k) -> p q k", q=BT), AX.X, ALU.max)\
                    .then_inc(max_done, 1)

            def scale_out(n, f):
                v.wait_ge(inverted, 2 * n + f + 1)
                wait_from_one(v, o.y_done, n)
                for g in range(2):
                    v.tensor_tensor(o.o[64 * g:64 * g + 64, f, :], ps[0:64, 2 + f, g * T:(g + 1) * T],
                                    inverse[:, g * T:(g + 1) * T], ALU.mult).then_inc(o.o_ready, 1)

            def step(n, par, front, core, tail, norm):
                if front:
                    qkv_vector_rotate(v, c, q, n + 1, 0, rope, True)
                if tail:
                    scale_out(n - 1, 1)
                if front:
                    qkv_vector_rotate(v, c, q, n + 1, 1, rope, True)
                if norm:
                    ln_vector_stats(v, s, n + 2)
                if front:
                    qkv_vector_rows(v, c, q, n + 1, 0, 1 - par)
                if norm:
                    ln_vector_scale(v, s, n + 2)
                if front:
                    qkv_vector_rows(v, c, q, n + 1, 1, 1 - par)
                for h in range(HEADS):
                    if front and h in ROW_SLOTS:
                        for u in ROW_SLOTS[h]:
                            max_of(n + 1, u)
                    if core and h == 10:
                        scale_out(n, 0)
                    if tail and h == OUT_BACK:
                        output_vector_add(v, c, o, n - 1)

            ln_vector_stats(v, s, 0)
            ln_vector_scale(v, s, 0)
            qkv_vector_pads(v, q)
            pipeline(v, step)

        @block.gpsimd
        def _(g):
            def step(n, par, front, core, tail, norm):
                if front:
                    qkv_gpsimd_lo(g, q, n + 1, 0)
                    qkv_gpsimd_lo(g, q, n + 1, 1)
                if norm:
                    ln_gpsimd_rstd(g, s, n + 2)
                if front and not core:
                    qkv_gpsimd_strips(g, q)

            ln_gpsimd_rstd(g, s, 0)
            qkv_gpsimd_stacks(g, q)
            pipeline(g, step)

        @block.sync
        def _(sp):
            for n in range(B):
                send_maxima(sp, q, m, n, n % 2)
            sp.wait_ge(m.max_in, 32 * B)


def mlp_buffers(sb, sem, slots):
    m = Parts()
    m.w_hi = [sb(f"w_hi{j}", [P, WT], F32R) for j in range(slots)]
    m.w_lo = [sb(f"w_lo{j}", [P, WT], F32R) for j in range(slots)]
    m.silu = sb("silu", [P, 2, NP], F32)
    m.act = sb("act", [P, 2, NP], F32)
    m.act_hi = sb("act_hi", [P, 4, NP], F32R)
    m.act_lo = sb("act_lo", [P, 4, NP], F32R)
    m.up_done = sem("up_done")
    m.silu_done = sem("silu_done")
    m.act_done = sem("act_done")
    m.weighted = sem("weighted")
    m.act_hi_done = sem("act_hi_done")
    m.act_lo_done = sem("act_lo_done")
    m.down_done = sem("down_done")
    m.y_added = sem("y_added")
    m.w_hi_done = sem("w_hi_done")
    m.w_lo_done = sem("w_lo_done")
    return m


def mlp_up(t_, c, m, n, j, slot, tb, first, expert_of=None, cw_rows=None):
    if not first:
        t_.wait_ge(m.act_done, n - 1)
        if expert_of is not None:
            t_.wait_ge(m.weighted, n - 1)
    tok = slice(tb * NP, (tb + 1) * NP)
    for bank, at in ((0, 0), (2, KD * P)):
        terms = [(w, h, k) for k in range(KD)
                 for w, h in ((m.w_hi[slot], c.h_hi), (m.w_hi[slot], c.h_lo), (m.w_lo[slot], c.h_hi))]
        for e, (w, h, k) in enumerate(terms):
            mm = t_.matmul(c.ps[:, bank + j % 2, :], w[:, at + k * P:at + (k + 1) * P], h[:, k, tok],
                           start=(e == 0), stop=(e == len(terms) - 1))
    if expert_of is not None:
        mm = t_.matmul(c.ps[:, 4 + j % 2, :], expert_of[:, :], cw_rows[:, tok], start=True, stop=True)
    mm.then_inc(m.up_done, 1)


def mlp_down(t_, c, m, n, j, slot, first, last):
    t_.wait_ge(m.act_lo_done, n + 1)
    at = 2 * KD * P
    for dh in range(KD):
        terms = ((m.w_hi[slot], m.act_hi), (m.w_hi[slot], m.act_lo), (m.w_lo[slot], m.act_hi))
        for e, (w, a) in enumerate(terms):
            mm = t_.matmul(c.ps[:, 6 + dh, :], w[:, at + dh * P:at + (dh + 1) * P], a[:, j % 4, :],
                           start=(first and e == 0), stop=(last and e == 2))
    mm.then_inc(m.down_done, 1)


def mlp_silu(a, c, m, n, j, first):
    a.wait_ge(m.up_done, n + 1)
    if not first:
        a.wait_ge(m.act_done, n - 1)
    a.activation(m.silu[:, j % 2, :], c.ps[:, j % 2, :], ACT.Silu).then_inc(m.silu_done, 1)


def mlp_hi(a, m, n, j, ready, first):
    a.wait_ge(ready, n + 1)
    if not first:
        a.wait_ge(m.down_done, n - 3)
    a.activation(m.act_hi[:, j % 4, :], m.act[:, j % 2, :], ACT.Copy).then_inc(m.act_hi_done, 1)


def mlp_lo(g, m, n, j):
    g.wait_ge(m.act_hi_done, n + 1)
    g.tensor_tensor(m.act_lo[:, j % 4, :], m.act[:, j % 2, :], m.act_hi[:, j % 4, :].bitcast(F32), ALU.subtract)\
        .then_inc(m.act_lo_done, 1)


def mlp_act(v, c, m, n, j, first, weigh):
    v.wait_ge(m.silu_done, n + 1)
    if not first:
        v.wait_ge(m.act_lo_done, n - 1)
    v.tensor_tensor(m.act[:, j % 2, :], m.silu[:, j % 2, :], c.ps[:, 2 + j % 2, :], ALU.mult).then_inc(m.act_done, 1)
    if weigh:
        v.wait_ge(m.act_done, n + 1)
        v.tensor_tensor(m.act[:, j % 2, :], m.act[:, j % 2, :], c.ps[:, 4 + j % 2, :], ALU.mult)\
            .then_inc(m.weighted, 1)


def add_back_phase(nc, c, mod, name):
    with ExitStack() as stack:
        def sem(n):
            return new_semaphore(nc, c, stack, name + n)

        gated, turned, added = sem("gated"), sem("turned"), sem("added")
        block = stack.enter_context(nc.Block())

        @block.scalar
        def _(a):
            with a.Fori(0, B) as b:
                for dh in range(KD):
                    y = c.yT[:, dh, bass.ds(b * T, T)]
                    a.activation(y, y, ACT.Copy, scale=mod[:, KD * GATE_B + dh, bass.ds(b, 1)]).then_inc(gated, 1)

        @block.tensor
        def _(t_):
            for b in range(B):
                t_.wait_ge(gated, KD * (b + 1))
                if b >= 4:
                    t_.wait_ge(added, b - 3)
                for q in range(BT):
                    for dh in range(KD):
                        at = b * T + q * P
                        mm = t_.transpose(c.ps[:, b % 4, q * D + dh * P:q * D + (dh + 1) * P],
                                          c.yT[:, dh, at:at + P], c.ident)
                mm.then_inc(turned, 1)

        @block.vector
        def _(v):
            for b in range(B):
                v.wait_ge(turned, b + 1)
                x = flat(c.x[:, BT * b:BT * b + BT, :])
                v.tensor_tensor(x, x, c.ps[:, b % 4, :], ALU.add).then_inc(added, 1)


def route(nc, c, args):
    with ExitStack() as stack:
        def sb(name, shape, dt):
            return stack.enter_context(nc.sbuf_tensor("r_" + name, shape, dt))

        def sem(name):
            return new_semaphore(nc, c, stack, "r_" + name)

        s = ln_buffers(sb, sem, c, c.mod[0], SHIFT_B, SCALE_B, PT_, 0, slots=2)
        ln_all_buffers(sb, sem, s)
        mo = modulation_buffers(sb, sem)
        gate_w = sb("gate_w", [P, KD, E], F32)
        top_logit = sb("top_logit", [P, TILES], F32)
        centred = sb("centred", [P, TILES, E], F32)
        e_raw = sb("e_raw", [P, TILES, E], F32)
        total = sb("total", [P, TILES], F32)
        inv_total = sb("inv_total", [P, TILES], F32)
        share = sb("share", [P, TILES, E], F32)
        top = sb("top", [P, TILES, 8], F32)
        picked = sb("picked", [P, TILES, E], F32)
        kept = sb("kept", [P, TILES, E], F32)
        cw = sb("cw", [P, TILES, 2 * E], F32)
        names = ("gate_in", "logits_done", "topped_logit", "below_top", "exped", "totaled", "inverted", "shared",
                 "topped", "cut", "matched", "masked", "cw_full", "cw_hi", "cw_lo", "cw_turned", "cw_out")
        (gate_in, logits_done, topped_logit, below_top, exped, totaled, inverted, shared, topped, cut, matched,
         masked, cw_full, cw_hi, cw_lo, cw_turned, cw_out) = (sem(n) for n in names)
        logits = c.ps[:, 4, 0:TILES * E].rearrange("p (t e) -> p t e", e=E)
        block = stack.enter_context(nc.Block())

        def over_experts(ap):
            return ap[:].unsqueeze(2).to_broadcast([P, TILES, E])

        @block.sync
        def _(sp):
            sp.dma_start(gate_w[:], args.gate_w).then_inc(gate_in, 16)
            load_experts(sp, c, args, 0, 0)
            load_experts(sp, c, args, 1, 1)

        @block.tensor
        def _(t_):
            def gate(i):
                t_.wait_ge(s.ln_h, 2 * KD * (i + 1))
                for t in range(PT_ * i, PT_ * i + PT_):
                    for k in range(KD):
                        mm = t_.matmul(logits[:, t, :], s.h[:, i % 2, k, t % PT_ * P:(t % PT_ + 1) * P], gate_w[:, k, :],
                                       start=(k == 0), stop=(k == KD - 1))
                mm.then_inc(logits_done, 1)

            t_.wait_ge(gate_in, 16)
            ln_tensor(t_, s, 0)
            for i in range(PAIRS):
                if i + 1 < PAIRS:
                    ln_tensor(t_, s, i + 1)
                gate(i)
            modulation_tensor(t_, c, mo, 1)
            t_.wait_ge(cw_lo, 1)
            for t in range(TILES):
                mm = t_.transpose(c.ps[0:2 * E, t // PT_, t % PT_ * P:(t % PT_ + 1) * P], cw[:, t, :], c.ident)
                if t % PT_ == PT_ - 1:
                    mm.then_inc(cw_turned, 1)

        @block.scalar
        def _(a):
            ln_all_scalar(a, c, s, h_read=logits_done)
            a.wait_ge(below_top, 1)
            a.activation(e_raw[:], centred[:], ACT.Exp).then_inc(exped, 1)
            for i in range(PAIRS):
                a.wait_ge(cw_turned, i + 1)
                a.activation(c.cw_rows[:, i * NP:(i + 1) * NP], c.ps[0:2 * E, i, :], ACT.Copy).then_inc(cw_out, 1)

        @block.gpsimd
        def _(g):
            ln_all_gpsimd(g, c, s)

        @block.vector
        def _(v):
            ln_all_vector(v, s)
            v.wait_ge(logits_done, PAIRS)
            v.tensor_reduce(top_logit[:], logits, AX.X, ALU.max).then_inc(topped_logit, 1)
            v.wait_ge(topped_logit, 1)
            v.tensor_tensor(centred[:], logits, over_experts(top_logit), ALU.subtract).then_inc(below_top, 1)
            v.wait_ge(exped, 1)
            v.tensor_reduce(total[:], e_raw[:], AX.X, ALU.add).then_inc(totaled, 1)
            v.wait_ge(totaled, 1)
            v.reciprocal(inv_total[:], total[:]).then_inc(inverted, 1)
            v.wait_ge(inverted, 1)
            v.tensor_tensor(share[:], e_raw[:], over_experts(inv_total), ALU.mult).then_inc(shared, 1)
            v.wait_ge(shared, 1)
            for t in range(TILES):
                v.max(top[:, t, :], share[:, t, :]).then_inc(topped, 1)
            v.wait_ge(topped, TILES)
            v.memset(top[:, :, TOPK:8], -2.0).then_inc(cut, 1)
            v.wait_ge(cut, 1)
            for t in range(TILES):
                v.match_replace(picked[:, t, :], top[:, t, :], share[:, t, :], -1.0).then_inc(matched, 1)
            v.wait_ge(matched, TILES)
            v.tensor_scalar(kept[:], picked[:], 0.0, None, ALU.is_lt).then_inc(masked, 1)
            v.wait_ge(masked, 1)
            v.tensor_tensor(kept[:], kept[:], share[:], ALU.mult).then_inc(cw_full, 1)
            v.wait_ge(cw_full, 1)
            v.tensor_copy(cw[:, :, 0:E].bitcast(F32R), kept[:]).then_inc(cw_hi, 1)
            v.wait_ge(cw_hi, 1)
            v.tensor_tensor(cw[:, :, E:2 * E].bitcast(F32R), kept[:], cw[:, :, 0:E], ALU.subtract).then_inc(cw_lo, 1)
            modulation_vector(v, c, mo, 1)


def load_experts(sp, c, args, chunk, par):
    sp.dma_start(c.moe_raw[:, 2 * par:2 * par + 2, :],
                 args.moe_w[bass.ds(2 * chunk, 2), :, :].rearrange("t p w -> p t w")).then_inc(c.moe_raw_in[par], 16)


def experts(nc, c, args):
    TB = TOKENS // NP
    STEPS = 2 * TB
    CHUNKS = MOE_TILES // 2
    LOOP = CHUNKS // 2
    with ExitStack() as stack:
        def sb(name, shape, dt):
            return stack.enter_context(nc.sbuf_tensor("m_" + name, shape, dt))

        def sem(name):
            return new_semaphore(nc, c, stack, "m_" + name)

        m = mlp_buffers(sb, sem, 4)
        m.raw_in = c.moe_raw_in
        raw = c.moe_raw
        which = [sb(f"which{j}", [2 * E, P], F32R) for j in range(4)]
        which_raw = sb("which_raw", [2 * E, MOE_TILES * P], F32)
        which_in, which_done, y_cleared = sem("which_in"), sem("which_done"), sem("y_cleared")
        block = stack.enter_context(nc.Block())

        def slot_of(j):
            return 2 * (j // STEPS % 2) + j % 2

        @block.sync
        def _(sp):
            def load(chunk, par):
                load_experts(sp, c, args, chunk, par)

            sp.dma_start(which_raw[:], args.expert_of).then_inc(which_in, 16)
            with sp.Fori(0, LOOP - 1) as i:
                for par in range(2):
                    sp.wait_ge(m.w_lo_done, 2 * (2 * i + par + 1))
                    load(2 * i + par + 2, par)
            sp.wait_ge(m.w_lo_done, 2 * (2 * LOOP - 1))
            load(2 * LOOP, 0)

        @block.tensor
        def _(t_):
            def step_up(i, j, first=False):
                n = 2 * STEPS * i + j
                jj = j % (2 * STEPS)
                if jj % STEPS < 2:
                    tile = 4 * i + 2 * (j // STEPS) + jj % 2
                    t_.wait_ge(m.w_lo_done, tile + 1)
                    t_.wait_ge(which_done, tile + 1)
                mlp_up(t_, c, m, n, j, slot_of(jj), jj % STEPS // 2, first, which[slot_of(jj)], c.cw_rows)

            step_up(0, 0, first=True)
            step_up(0, 1, first=True)
            t_.wait_ge(y_cleared, 1)
            t_.sem_inc(m.y_added, 1)
            with t_.Fori(0, LOOP) as i:
                for j in range(2 * STEPS):
                    n = 2 * STEPS * i + j
                    if j % 2 == 0:
                        t_.wait_ge(m.y_added, STEPS * i + j // 2 + 1)
                    mlp_down(t_, c, m, n, j, slot_of(j), j % 2 == 0, j % 2 == 1)
                    step_up(i, j + 2)
            for j in range(STEPS):
                if j % 2 == 0:
                    t_.wait_ge(m.y_added, STEPS * LOOP + j // 2 + 1)
                mlp_down(t_, c, m, 2 * STEPS * LOOP + j, j, slot_of(j), j % 2 == 0, j % 2 == 1)
                if j + 2 < STEPS:
                    step_up(LOOP, j + 2)

        @block.scalar
        def _(a):
            def split(k, par, first):
                chunk = 2 * k + par
                a.wait_ge(m.raw_in[par], 16 * (k + 1))
                if not first:
                    a.wait_ge(m.down_done, STEPS * (chunk - 1))
                for t in range(2):
                    a.activation(m.w_hi[2 * par + t][:], raw[:, 2 * par + t, :], ACT.Copy).then_inc(m.w_hi_done, 1)
                for t in range(2):
                    col = (2 * chunk + t) * P
                    a.activation(which[2 * par + t][:, :], which_raw[:, bass.ds(col, P)], ACT.Copy)\
                        .then_inc(which_done, 1)

            def step(i, j, first0=False, first1=False):
                n = 2 * STEPS * i + j
                mlp_silu(a, c, m, n, j, first0)
                mlp_hi(a, m, n, j, m.weighted, first1)

            a.wait_ge(which_in, 16)
            split(0, 0, True)
            split(0, 1, True)
            for j in range(4):
                step(0, j, first0=j < 2, first1=True)
            for j in range(4, 2 * STEPS):
                step(0, j)
                if j == STEPS + 3:
                    split(1, 0, False)
            with a.Fori(1, LOOP) as i:
                for j in range(2 * STEPS):
                    step(i, j)
                    if j == 3:
                        split(i, 1, False)
                    if j == STEPS + 3:
                        split(i + 1, 0, False)
            for j in range(STEPS):
                step(LOOP, j)

        @block.gpsimd
        def _(g):
            def split(k, par):
                chunk = 2 * k + par
                for t in range(2):
                    g.wait_ge(m.w_hi_done, 2 * chunk + t + 1)
                    g.tensor_tensor(m.w_lo[2 * par + t][:], raw[:, 2 * par + t, :],
                                    m.w_hi[2 * par + t][:].bitcast(F32), ALU.subtract).then_inc(m.w_lo_done, 1)

            split(0, 0)
            split(0, 1)
            for j in range(2 * STEPS):
                mlp_lo(g, m, j, j)
                if j == STEPS + 3:
                    split(1, 0)
            with g.Fori(1, LOOP) as i:
                for j in range(2 * STEPS):
                    mlp_lo(g, m, 2 * STEPS * i + j, j)
                    if j == 3:
                        split(i, 1)
                    if j == STEPS + 3:
                        split(i + 1, 0)
            for j in range(STEPS):
                mlp_lo(g, m, 2 * STEPS * LOOP + j, j)

        @block.vector
        def _(v):
            def add_y(n, tb):
                v.wait_ge(m.down_done, n + 1)
                y = c.yT[:, :, tb * NP:(tb + 1) * NP]
                v.tensor_tensor(y, y, c.ps[:, 6:8, :], ALU.add).then_inc(m.y_added, 1)

            def step(i, j, first=False, first_y=False):
                n = 2 * STEPS * i + j
                mlp_act(v, c, m, n, j, first, weigh=True)
                if j % 2 == 0 and not first_y:
                    add_y(n - 1, (j // 2 - 1) % TB)

            v.memset(c.yT[:], 0.0).then_inc(y_cleared, 1)
            v.wait_ge(y_cleared, 1)
            for j in range(2 * STEPS):
                step(0, j, first=j < 2, first_y=j == 0)
            with v.Fori(1, LOOP) as i:
                for j in range(2 * STEPS):
                    step(i, j)
            for j in range(STEPS):
                step(LOOP, j)
            add_y(2 * STEPS * LOOP + STEPS - 1, TB - 1)


def attention1(nc, c):
    with ExitStack() as stack:
        def sb(name, shape, dt):
            return stack.enter_context(nc.sbuf_tensor("a1_" + name, shape, dt))

        def sem(name):
            return new_semaphore(nc, c, stack, "a1_" + name)

        KV = 4
        VW = 2 * HW
        FT = HEADS * VW // P
        NB = 3
        UNITS = 2 * HEADS
        s = ln_buffers(sb, sem, c, c.mod[1], SHIFT_A, SCALE_A, BT, 7)
        q = qkv_buffers(sb, sem, 2 * HEADS, 2 * KV, KV, VW)
        w_qkv = c.w1[:, 0:KD * 768].rearrange("p (k n) -> p k n", k=KD)
        o = output_buffers(sb, sem, FT, c.w1[:, KD * 768:].rearrange("p (f n) -> p f n", f=FT), c.mod[1])
        m = Parts()
        m.max_rows = sb("max_rows", [UNITS, T], F32R)
        m.max_turned, m.max_rows_ready, m.max_in = (sem(n) for n in ("max_turned", "max_rows_ready", "max_in"))
        block_max = sb("block_max", [P, UNITS, NB], F32)
        maxima = sb("maxima", [P, BT, UNITS], F32)
        probs = sb("probs", [P, 8, NB * P], F32)
        log_sum = sb("log_sum", [64, 2 * T], F32)
        inverse = sb("inverse", [64, 2, 2 * T], F32)
        parts = sb("parts", [P, 2, 2, T], F32)
        heads_out = [sb(f"heads_out{b}", [P, FT, T], F32) for b in range(2)]
        gn_stats = sb("gn_stats", [P, FT, 6], F32)
        row_moments = sb("row_moments", [P, FT, 2], F32)
        off_mean = sb("off_mean", [P, FT], F32)
        off_square = sb("off_square", [P, FT], F32)
        row_spread = sb("row_spread", [P, FT], F32)
        group_mean = sb("group_mean", [P, FT], F32)
        var = sb("var", [P, FT], F32)
        rstd = sb("rstd", [P, FT], F32)
        gn_scale = sb("gn_scale", [P, FT], F32)
        gn_product = sb("gn_product", [P, FT], F32)
        gn_bias = sb("gn_bias", [P, FT], F32)
        scores_done, max_done, max_joined = (sem(n) for n in ("scores_done", "max_done", "max_joined"))
        keyed_done, exp_done, cut_done, pv_done, logged, inverted, parted, out_ready = (
            sem(n) for n in ("keyed_done", "exp_done", "cut_done", "pv_done", "logged", "inverted", "parted",
                             "out_ready"))
        gn_counted, row_done, mean_done, off_done, spread_done, var_done, var_eps, rstd_done, affine_set = (
            sem(n) for n in ("gn_counted", "row_done", "mean_done", "off_done", "spread_done", "var_done", "var_eps",
                             "rstd_done", "affine_set"))
        off_scaled = sem("off_scaled")
        rope = Parts()
        rope.width = 16
        rope.first = lambda a: a[:, :, 0:16:2]
        rope.second = lambda a: a[:, :, 1:16:2]
        rope.cos = c.table(C_COS1, 16)
        rope.sin_a = c.table(C_SIN1A, 8)
        rope.sin_b = c.table(C_SIN1B, 8)
        ps = c.ps
        PVG = HEADS // 2
        TURNS = {2: (0, (0, 1)), 3: (0, (2, 3)), 4: (0, (4,)), 5: (1, (0, 1)), 6: (1, (2, 3)), 7: (1, (4,))}
        ROW_SLOTS = {8 + j: tuple(range(4 * j, 4 * j + 4)) for j in range(8)}
        MEAN, VARIANCE, NORM_TURN, OUT_PROJECT, OUT_BACK, MAX_TURN = 6, 8, 10, 12, 15, 15
        FIRST_ROWS = min(ROW_SLOTS)
        block = stack.enter_context(nc.Block())

        @block.tensor
        def _(t_):
            def row_scores(n, par, u):
                h, half, bank = u // 2, u % 2, 4 + u % 2
                if u >= 2:
                    t_.wait_ge(max_done, UNITS * n + u - 1)
                qr, kr = q.q_rows[:, par, h, :], q.k_pad[half][:, par, h // KV, :]
                t_.matmul(ps[:, bank, 0:T], qr[:, P:T], kr[:, 0:T], start=True, stop=False, skip_group_check=True)
                t_.matmul(ps[:, bank, T:T + P], qr[:, 0:P], kr[:, 0:P], start=False, stop=False,
                          skip_group_check=True)
                t_.matmul(ps[:, bank, P:P + T], c.ident_bf[:, :], c.mask_bf[:, :], start=False, stop=True,
                          skip_group_check=True).then_inc(scores_done, 1)

            def turn_maxima(n):
                t_.wait_ge(max_joined, 2 * (n + 1))
                for qt in range(BT):
                    mm = t_.transpose(ps[0:UNITS, 4, qt * P:(qt + 1) * P], maxima[:, qt, :], c.ident)
                mm.then_inc(m.max_turned, 1)

            def key_scores(n, par, u):
                h, half, bank = u // 2, u % 2, u % 2
                if u == 0:
                    t_.wait_ge(m.max_in, 32 * (n + 1))
                wait_from_one(t_, exp_done, UNITS * n + u - 1)
                qr, kr = q.q_rows[:, par, h, :], q.k_pad[half][:, par, h // KV, :]
                t_.matmul(ps[:, bank, 0:T], kr[:, 0:P], qr[:, 0:T], start=True, stop=False, skip_group_check=True)
                t_.matmul(ps[:, bank, T:T + P], kr[:, P:T], qr[:, P:T], start=False, stop=True,
                          skip_group_check=True).then_inc(keyed_done, 1)

            def weigh(n, par, h, between=()):
                grp = h // 2
                if h % 2 == 0:
                    wait_from_one(t_, parted, 2 * (PVG * n + grp - 1))
                for half in range(2):
                    if half == 1:
                        for ahead in between:
                            row_scores(n + 1, 1 - par, ahead)
                    u = 2 * h + half
                    t_.wait_ge(cut_done, UNITS * n + u + 1)
                    for kt, first, cols in ((0, 0, T), (1, P, P)):
                        at = half * T + first
                        mm = t_.matmul(ps[:, 2 + grp % 2, at:at + cols], value_window(q, par, kt, h // KV, h % 2),
                                       probs[:, u % 8, kt * T:kt * T + cols],
                                       start=(h % 2 == 0 and half == 0 and kt == 0),
                                       stop=(h % 2 == 1 and half == 1 and kt == 1), skip_group_check=True)
                mm.then_inc(pv_done, 1)

            def average(bank, of, ready, count, done):
                t_.wait_ge(ready, count)
                t_.matmul(ps[:, bank, 0:FT], c.mean_of[:, :], of, start=True, stop=True).then_inc(done, 1)

            def step(n, par, front, core, tail, norm):
                if tail:
                    weigh(n - 1, 1 - par, HEADS - 2)
                if front:
                    wait_from_one(t_, o.x_added, n - 1)
                    qkv_project(t_, c, s, q, w_qkv, n + 1, 0, (0,))
                if tail:
                    weigh(n - 1, 1 - par, HEADS - 1)
                if front:
                    qkv_project(t_, c, s, q, w_qkv, n + 1, 0, (1,))
                    wait_from_one(t_, m.max_rows_ready, n + 1)
                    qkv_project(t_, c, s, q, w_qkv, n + 1, 1)
                for h in range(HEADS):
                    rows = list(ROW_SLOTS[h]) if front and h in ROW_SLOTS and h > FIRST_ROWS else []
                    if front and not core and h == 0:
                        t_.wait_ge(q.pads_set, 2)
                    if core and not tail and h == 2:
                        t_.wait_ge(q.strips_set, 4)
                    if core:
                        key_scores(n, par, 2 * h)
                        for u in rows[0:1]:
                            row_scores(n + 1, 1 - par, u)
                        key_scores(n, par, 2 * h + 1)
                        for u in rows[1:2]:
                            row_scores(n + 1, 1 - par, u)
                        rows = rows[2:]
                        if h >= 2:
                            weigh(n, par, h - 2, rows[0:1])
                            rows = rows[1:]
                    if front and h == FIRST_ROWS:
                        t_.wait_ge(q.q_rows_ready, q.q_rounds * BT * (n + 2))
                        for j in range(2):
                            t_.wait_ge(q.k_rows_ready[j], q.k_rounds * BT * (n + 2))
                        rows = ROW_SLOTS[h]
                    for u in rows:
                        row_scores(n + 1, 1 - par, u)
                    if front and h in TURNS:
                        t, rounds = TURNS[h]
                        qkv_turn(t_, c, q, n + 1, t, rounds)
                    if tail and h == MEAN:
                        if front:
                            for j in range(2):
                                t_.wait_ge(q.k_rows_ready[j], BT * (n + 1) + 1)
                        average(6, row_moments[:, :, 0], row_done, FT * n, mean_done)
                    if tail and h == VARIANCE:
                        average(7, row_spread[:, :], spread_done, n, var_done)
                    if norm and h == NORM_TURN:
                        if tail:
                            t_.wait_ge(var_eps, n)
                        ln_tensor(t_, s, n + 2)
                    if tail and h == OUT_PROJECT:
                        if norm:
                            t_.wait_ge(s.ln_h, KD * (n + 3))
                        output_tensor(t_, c, o, n - 1)
                    if tail and h == OUT_BACK:
                        output_tensor_back(t_, c, o, n - 1)
                    if front and h == MAX_TURN:
                        turn_maxima(n + 1)

            t_.wait_ge(c.w1_in, 16)
            ln_tensor(t_, s, 0)
            pipeline(t_, step)

        @block.scalar
        def _(a):
            def exps(n, u):
                a.wait_ge(keyed_done, UNITS * n + u + 1)
                wait_from_one(a, pv_done, HEADS * n + u // 2 - 3)
                a.activation(probs[:, u % 8, :], ps[:, u % 2, 0:NB * P], ACT.Exp, scale=SCALE).then_inc(exp_done, 1)

            def affine(n, par):
                a.wait_ge(affine_set, n + 1)
                for f in range(FT):
                    a.activation(o.o[:, f, :], heads_out[par][:, f, :], ACT.Identity,
                                 scale=gn_scale[:, f:f + 1], bias=gn_bias[:, f:f + 1]).then_inc(o.o_ready, 1)

            def invert_sums(n, grp):
                at_n = PVG * n + grp
                a.wait_ge(pv_done, 2 * (at_n + 1))
                wait_from_one(a, inverted, at_n)
                a.activation(log_sum[:], ps[64:128, 2 + grp % 2, :], ACT.Ln).then_inc(logged, 1)
                a.wait_ge(logged, at_n + 1)
                wait_from_one(a, parted, 2 * (at_n - 1))
                a.activation(inverse[:, grp % 2, :], log_sum[:], ACT.Exp, scale=-1.0).then_inc(inverted, 1)

            def norm_out(m_):
                wait_from_one(a, q.qkv_done, BT * m_)
                ln_scalar(a, s, m_, lambda half, b: q.h[:, half, :])

            def step(n, par, front, core, tail, norm):
                if tail:
                    invert_sums(n - 1, PVG - 1)
                if front:
                    qkv_scalar_copies(a, c, q, n + 1, 0, 1 - par, False, pv_done)
                    qkv_scalar_copies(a, c, q, n + 1, 1, 1 - par, False, pv_done)
                for h in range(HEADS):
                    if tail and h == OUT_BACK:
                        output_scalar_gate(a, c, o, n - 1)
                    if core:
                        exps(n, 2 * h)
                    if front and h in (0, 2):
                        qkv_scalar_hi(a, q, n + 1, h // 2, False, ("q",))
                    if core:
                        exps(n, 2 * h + 1)
                        if h % 2 == 0 and h >= 4:
                            invert_sums(n, (h - 4) // 2)
                    if front and h in TURNS:
                        t, rounds = TURNS[h]
                        qkv_scalar_rows(a, c, q, n + 1, t, 1 - par, rounds)
                    if front and h in (0, 2):
                        qkv_scalar_hi(a, q, n + 1, h // 2, False, ("k",))
                    if core and h == HEADS - 1:
                        invert_sums(n, PVG - 2)
                    if norm and h == NORM_TURN:
                        norm_out(n + 2)
                    if tail and h == OUT_PROJECT - 1:
                        affine(n - 1, 1 - par)
                    if front and h == MAX_TURN:
                        max_out(a, c, q, m, n + 1)

            a.preload_act_table_set("natural_log_exp_and_others")
            norm_out(0)
            a.wait_ge(q.stacks_set, 4)
            pipeline(a, step)

        @block.vector
        def _(v):
            def max_of(n, u):
                v.wait_ge(scores_done, UNITS * n + u + 1)
                col = HEADS * (u % 2) + u // 2
                v.tensor_reduce(block_max[:, col, :], ps[:, 4 + u % 2, 0:NB * P].rearrange("p (c k) -> p c k", c=NB),
                                AX.X, ALU.max).then_inc(max_done, 1)

            def join(n):
                v.wait_ge(max_done, UNITS * (n + 1))
                wait_from_one(v, m.max_turned, n)
                v.tensor_tensor(maxima[:, 1, :], block_max[:, :, 0], block_max[:, :, 1], ALU.max)\
                    .then_inc(max_joined, 1)
                v.tensor_copy(maxima[:, 0, :], block_max[:, :, 2]).then_inc(max_joined, 1)

            def combine(n, par, grp):
                at_n = PVG * n + grp
                bank, rows = 2 + grp % 2, slice(64 * (grp % 2), 64 * (grp % 2) + 64)
                v.wait_ge(inverted, at_n + 1)
                wait_from_one(v, out_ready, FT * n + grp // 2 - 1)
                v.tensor_tensor(parts[rows, grp // 2 % 2, 0, :], ps[0:64, bank, 0:T], inverse[:, grp % 2, 0:T],
                                ALU.mult).then_inc(parted, 1)
                v.scalar_tensor_tensor(parts[rows, grp // 2 % 2, 1, :], ps[0:64, bank, T:2 * T],
                                       c.neg_lam[0:64, 0:1], inverse[:, grp % 2, T:2 * T], ALU.mult, ALU.mult)\
                    .then_inc(parted, 1)

            def norm_a(n, par):
                v.wait_ge(out_ready, FT * (n + 1))
                v.sem_inc(s.passed)
                for f in range(FT):
                    v.bn_stats(gn_stats[:, f, :], heads_out[par][:, f, :]).then_inc(gn_counted, 1)
                v.wait_ge(gn_counted, FT * (n + 1))
                v.sem_inc(s.passed)
                for f in range(FT):
                    v.bn_aggr(row_moments[:, f, :], gn_stats[:, f, :]).then_inc(row_done, 1)

            def norm_b(n):
                v.wait_ge(mean_done, n + 1)
                v.tensor_tensor(off_mean[:], row_moments[:, :, 0], ps[:, 6, 0:FT], ALU.subtract).then_inc(off_done, 1)
                v.tensor_copy(group_mean[:], ps[:, 6, 0:FT]).then_inc(off_done, 1)
                v.wait_ge(off_done, 3 * n + 2)
                v.tensor_tensor(off_square[:], off_mean[:], off_mean[:], ALU.mult).then_inc(off_done, 1)
                v.wait_ge(off_done, 3 * n + 3)
                v.tensor_tensor(row_spread[:], off_square[:], row_moments[:, :, 1], ALU.add).then_inc(spread_done, 1)

            def norm_c(n):
                v.wait_ge(var_done, n + 1)
                v.tensor_scalar(var[:], ps[:, 7, 0:FT], GN_EPS, None, ALU.add).then_inc(var_eps, 1)

            def norm_d(n):
                v.wait_ge(rstd_done, n + 1)
                v.tensor_tensor(gn_scale[:], rstd[:], c.gn[:, 0:FT], ALU.mult).then_inc(off_scaled, 1)
                v.wait_ge(off_scaled, 2 * n + 1)
                v.tensor_tensor(gn_product[:], group_mean[:], gn_scale[:], ALU.mult).then_inc(off_scaled, 1)
                v.wait_ge(off_scaled, 2 * n + 2)
                v.tensor_tensor(gn_bias[:], c.gn[:, FT:2 * FT], gn_product[:], ALU.subtract).then_inc(affine_set, 1)

            def step(n, par, front, core, tail, norm):
                if tail:
                    combine(n - 1, 1 - par, PVG - 1)
                if front:
                    qkv_vector_rotate(v, c, q, n + 1, 0, rope, False)
                    qkv_vector_rotate(v, c, q, n + 1, 1, rope, False)
                if tail:
                    norm_a(n - 1, 1 - par)
                if norm:
                    ln_vector_stats(v, s, n + 2)
                for h in range(3, HEADS):
                    if front and h == 4:
                        qkv_vector_rows(v, c, q, n + 1, 0, 1 - par)
                    if front and h == 7:
                        qkv_vector_rows(v, c, q, n + 1, 1, 1 - par)
                    if tail and h == MEAN:
                        norm_b(n - 1)
                    if norm and h == 6:
                        ln_vector_scale(v, s, n + 2)
                    if front and h in ROW_SLOTS:
                        for u in ROW_SLOTS[h]:
                            max_of(n + 1, u)
                    if tail and h == VARIANCE:
                        norm_c(n - 1)
                    if tail and h == VARIANCE + 1:
                        norm_d(n - 1)
                    if front and h == MAX_TURN:
                        join(n + 1)
                    if core and h % 2 == 1 and h >= 5:
                        combine(n, par, (h - 5) // 2)
                    if core and h == HEADS - 1:
                        combine(n, par, PVG - 2)
                    if tail and h == OUT_BACK:
                        output_vector_add(v, c, o, n - 1)

            ln_vector_stats(v, s, 0)
            ln_vector_scale(v, s, 0)
            qkv_vector_pads(v, q)
            pipeline(v, step)

        @block.gpsimd
        def _(g):
            def cut(n, u):
                g.wait_ge(exp_done, UNITS * n + u + 1)
                g.sem_inc(s.passed)
                at = probs[:, u % 8, :].rearrange("p (c n) -> p c n", c=NB)[:, 0:NB:2, :]
                g.affine_select(out=at, in_=at, compare_op=ALU.is_ge, fill=0.0, base=0,
                                pattern=[[0, 2], [1, P]], channel_multiplier=-1).then_inc(cut_done, 1)

            def group_rstd(n):
                g.wait_ge(var_eps, n + 1)
                g.tensor_tensor(rstd[:], var[:], c.minus_half[:, 0:FT], ALU.pow).then_inc(rstd_done, 1)

            def add_parts(n, par, f):
                g.wait_ge(parted, 4 * (FT * n + f + 1))
                g.tensor_tensor(heads_out[par][:, f, :], parts[:, f % 2, 0, :], parts[:, f % 2, 1, :], ALU.add)\
                    .then_inc(out_ready, 1)

            def step(n, par, front, core, tail, norm):
                if tail:
                    add_parts(n - 1, 1 - par, FT - 2)
                    add_parts(n - 1, 1 - par, FT - 1)
                for h in range(HEADS):
                    if core:
                        cut(n, 2 * h)
                        cut(n, 2 * h + 1)
                        if h in (9, 13):
                            add_parts(n, par, (h - 9) // 4)
                    if front and h in (0, 2):
                        qkv_gpsimd_lo(g, q, n + 1, h // 2)
                    if norm and h == 2:
                        ln_gpsimd_rstd(g, s, n + 2)
                    if front and not core and h == 2:
                        qkv_gpsimd_strips(g, q)
                    if tail and h == VARIANCE:
                        group_rstd(n - 1)

            ln_gpsimd_rstd(g, s, 0)
            qkv_gpsimd_stacks(g, q)
            pipeline(g, step)

        @block.sync
        def _(sp):
            for n in range(B):
                send_maxima(sp, q, m, n, n % 2)
            sp.wait_ge(m.max_in, 32 * B)


def norm_all(nc, c, args):
    with ExitStack() as stack:
        def sb(name, shape, dt):
            return stack.enter_context(nc.sbuf_tensor("n_" + name, shape, dt))

        def sem(name):
            return new_semaphore(nc, c, stack, "n_" + name)

        s = ln_buffers(sb, sem, c, c.mod[1], SHIFT_B, SCALE_B, PT_, 0, slots=2)
        ln_all_buffers(sb, sem, s)
        block = stack.enter_context(nc.Block())

        @block.sync
        def _(sp):
            for t in range(2):
                sp.dma_start(c.ffn_raw[:, t, :], args.ffn_w[t, :, :]).then_inc(c.ffn_raw_in[t], 16)

        @block.tensor
        def _(t_):
            for i in range(PAIRS):
                ln_tensor(t_, s, i)

        @block.scalar
        def _(a):
            ln_all_scalar(a, c, s)

        @block.gpsimd
        def _(g):
            ln_all_gpsimd(g, c, s)

        @block.vector
        def _(v):
            ln_all_vector(v, s)


def feed_forward(nc, c, args):
    with ExitStack() as stack:
        def sb(name, shape, dt):
            return stack.enter_context(nc.sbuf_tensor("f_" + name, shape, dt))

        def sem(name):
            return new_semaphore(nc, c, stack, "f_" + name)

        m = mlp_buffers(sb, sem, FFN_TILES)
        m.raw_in = c.ffn_raw_in
        raw = c.ffn_raw
        N = FFN_TILES
        block = stack.enter_context(nc.Block())

        @block.sync
        def _(sp):
            for t in range(2, N):
                sp.wait_ge(m.w_lo_done, t - 1)
                sp.dma_start(raw[:, t % 2, :], args.ffn_w[t, :, :]).then_inc(m.raw_in[t % 2], 16)

        @block.tensor
        def _(t_):
            steps = N * (TOKENS // NP)

            def up(n):
                if n < N:
                    t_.wait_ge(m.w_lo_done, n + 1)
                mlp_up(t_, c, m, n, n, n % N, n // N, n < 2)

            up(0)
            up(1)
            for n in range(steps):
                if n % N == 0 and n:
                    t_.wait_ge(m.y_added, n // N)
                mlp_down(t_, c, m, n, n, n % N, n % N == 0, n % N == N - 1)
                if n + 2 < steps:
                    up(n + 2)

        @block.scalar
        def _(a):
            def split(t):
                a.wait_ge(m.raw_in[t % 2], 16 * (t // 2 + 1))
                a.activation(m.w_hi[t][:], raw[:, t % 2, :], ACT.Copy).then_inc(m.w_hi_done, 1)

            split(0)
            split(1)
            for n in range(N):
                mlp_silu(a, c, m, n, n, n < 2)
                mlp_hi(a, m, n, n, m.act_done, n < 4)
                if n + 2 < N:
                    split(n + 2)
            with a.Fori(1, TOKENS // NP) as i:
                for j in range(N):
                    mlp_silu(a, c, m, N * i + j, j, False)
                    mlp_hi(a, m, N * i + j, j, m.act_done, False)

        @block.gpsimd
        def _(g):
            def split(t):
                g.wait_ge(m.w_hi_done, t + 1)
                g.tensor_tensor(m.w_lo[t][:], raw[:, t % 2, :], m.w_hi[t][:].bitcast(F32), ALU.subtract)\
                    .then_inc(m.w_lo_done, 1)

            split(0)
            split(1)
            for n in range(N):
                mlp_lo(g, m, n, n)
                if n + 2 < N:
                    split(n + 2)
            with g.Fori(1, TOKENS // NP) as i:
                for j in range(N):
                    mlp_lo(g, m, N * i + j, j)

        @block.vector
        def _(v):
            def store_y(tb):
                v.wait_ge(m.down_done, N * (tb + 1))
                v.tensor_copy(c.yT[:, :, bass.ds(tb * NP, NP)], c.ps[:, 6:8, :]).then_inc(m.y_added, 1)

            for n in range(N):
                mlp_act(v, c, m, n, n, n < 2, weigh=False)
            with v.Fori(1, TOKENS // NP) as i:
                for j in range(N):
                    mlp_act(v, c, m, N * i + j, j, False, weigh=False)
                    if j == 0:
                        store_y(i - 1)
            store_y(TOKENS // NP - 1)


def clear_used(nc, c):
    numbers = sorted({s.num for s in c.used})
    with nc.Block() as block:
        @block.sync
        def _(sp):
            start = numbers[0]
            for a, b in zip(numbers, numbers[1:] + [None]):
                if b != a + 1:
                    sp.sem_clear(range(start, a + 1))
                    start = b
    c.used.clear()


def program(nc, args):
    c = Parts()
    c.used = []
    with ExitStack() as stack:
        def sb(name, shape, dt):
            return stack.enter_context(nc.sbuf_tensor(name, shape, dt))

        c.ps = stack.enter_context(nc.psum_tensor("ps", [P, 8, 512], F32))
        c.psflat = c.ps[:].rearrange("p b n -> p (b n)")
        c.x = sb("x_tokens", [P, TILES, D], F32)
        c.consts = sb("consts_t", [P, C_END], F32)
        c.ident = c.consts[:, C_ID:C_ID + P]
        c.ident_bf = sb("ident_bf", [P, P], BF16)
        c.mask_bf = sb("mask_bf", [P, 2 * P], BF16)
        c.minus_half = sb("minus_half", [P, HEADS], F32)
        c.mean_of = c.consts[:, C_MEAN:C_MEAN + P]
        c.mod = [sb(f"mod{n}", [P, 6 * KD, B], F32) for n in range(2)]
        c.neg_lam = sb("neg_lam", [P, 1], F32)
        c.gn = sb("gn_wb", [P, 8], F32)

        def table(at, width):
            return c.consts[:, at:at + BT * width].rearrange("p (t w) -> p t w", t=BT)

        c.table = table
        c.w1 = sb("w1_t", [P, KD * 768 + 4 * D], F32)
        c.w1_in = stack.enter_context(nc.semaphore("w1_in"))
        c.wmod_in = [stack.enter_context(nc.semaphore(f"wmod_in{n}")) for n in range(2)]
        c.cond_silu = [sb(f"cond_silu{n}", [P, KD, B], F32) for n in range(2)]
        c.wmod = [sb(f"wmod{n}", [P, KD, 6 * D], F32) for n in range(2)]
        with ExitStack() as inner:
            c.w0 = inner.enter_context(nc.sbuf_tensor("w0_t", [P, KD, 1024], F32))
            setup(nc, c, args)
            attention0(nc, c)
        with ExitStack() as inner:
            c.h_hi = inner.enter_context(nc.sbuf_tensor("moe_h_hi", [P, KD, TOKENS], F32R))
            c.h_lo = inner.enter_context(nc.sbuf_tensor("moe_h_lo", [P, KD, TOKENS], F32R))
            c.cw_rows = inner.enter_context(nc.sbuf_tensor("cw_rows", [2 * E, TOKENS], F32R))
            c.yT = inner.enter_context(nc.sbuf_tensor("moe_yT", [P, KD, TOKENS], F32))
            c.moe_raw = inner.enter_context(nc.sbuf_tensor("moe_raw", [P, 4, WT], F32))
            c.moe_raw_in = [new_semaphore(nc, c, stack, f"moe_raw_in{j}") for j in range(2)]
            route(nc, c, args)
            experts(nc, c, args)
            add_back_phase(nc, c, c.mod[0], "moe_")
        clear_used(nc, c)
        c.ffn_raw = sb("ffn_raw", [P, 2, WT], F32)
        c.ffn_raw_in = [new_semaphore(nc, c, stack, f"ffn_raw_in{j}") for j in range(2)]
        attention1(nc, c)
        clear_used(nc, c)
        with ExitStack() as inner:
            c.h_hi = inner.enter_context(nc.sbuf_tensor("ffn_h_hi", [P, KD, TOKENS], F32R))
            c.h_lo = inner.enter_context(nc.sbuf_tensor("ffn_h_lo", [P, KD, TOKENS], F32R))
            c.yT = inner.enter_context(nc.sbuf_tensor("ffn_yT", [P, KD, TOKENS], F32))
            norm_all(nc, c, args)
            feed_forward(nc, c, args)
            add_back_phase(nc, c, c.mod[1], "ffn_")
        out_done = stack.enter_context(nc.semaphore("out_done"))
        block = stack.enter_context(nc.Block())

        @block.sync
        def _(sp):
            for b in range(0, B, 2):
                sp.dma_start(args.out.rearrange("b (t p) d -> p (b t) d", p=P)[:, BT * b:BT * b + PT_, :],
                             c.x[:, BT * b:BT * b + PT_, :]).then_inc(out_done, 16)
            sp.wait_ge(out_done, 16 * PAIRS)


def constants():
    consts = np.zeros((P, C_END), np.float32)
    consts[:, C_ID:C_ID + P] = np.eye(P)
    above = np.where(np.arange(P)[None, :] > np.arange(P)[:, None], MASKED, 0.0)
    consts[:, C_MASK:C_MASK + 2 * P] = np.concatenate([above, above], 1)
    pos = np.arange(T, dtype=np.float32)[:, None]
    inv = (1.0 / np.float32(10000.0) ** (np.arange(0, 16, 2, dtype=np.float32) / np.float32(16))).astype(np.float32)
    ang = pos * inv[None, :]
    sin = np.sin(ang).reshape(BT, P, 8)
    cos = np.cos(ang).reshape(BT, P, 8)

    def put(at, table):
        w = table.shape[2]
        consts[:, at:at + BT * w] = table.transpose(1, 0, 2).reshape(P, BT * w)

    put(C_COS0, cos)
    put(C_SIN0A, -sin[:, :, 0:4])
    put(C_SIN0B, sin[:, :, 4:8])
    put(C_COS1, np.repeat(cos, 2, axis=2))
    put(C_SIN1A, -sin)
    put(C_SIN1B, sin)
    consts[:, C_MEAN:C_MEAN + P] = np.kron(np.eye(4), np.full((32, 32), 1 / 32))
    which = np.zeros((2 * E, MOE_TILES * P), np.float32)
    expert = np.arange(MOE_TILES * P) // MOE_D
    which[expert, np.arange(MOE_TILES * P)] = 1.0
    which[E + expert, np.arange(MOE_TILES * P)] = 1.0
    return consts, which


def kernel(**inputs):
    import numpy as _np
    import concourse.bacc as _bacc
    from concourse import mybir as _mybir
    from concourse.bass_utils import run_bass_kernel_spmd as _run

    a = {n: _np.asarray(v) for n, v in inputs.items()}
    nc = _bacc.Bacc("TRN2", target_bir_lowering=False, num_devices=1)
    arrays = {}

    def give(name, array):
        array = _np.ascontiguousarray(array)
        arrays["in_" + name] = array
        return nc.dram_tensor("in_" + name, array.shape, _mybir.dt.from_np(array.dtype), kind="ExternalInput").ap()

    def halves(m):
        return m.reshape(-1, 128, m.shape[1]).transpose(1, 0, 2)

    def tiles(gate, up, down):
        n = gate.shape[0] // 128
        def turned(w):
            return w.reshape(n, 128, 2, 128).transpose(0, 3, 2, 1).reshape(n, 128, 256)
        return _np.concatenate([turned(gate), turned(up), down.reshape(n, 128, 256)], axis=2)

    consts, which = constants()
    args = Parts()
    args.x = give("x", a["L0_attn_x"].reshape(16, 128, 256).transpose(1, 0, 2))
    args.c0 = give("c0", halves(a["L0_c"].T))
    args.c1 = give("c1", halves(a["L1_c"].T))
    args.wmod0 = give("wmod0", halves(a["L0_wmod"]))
    args.wmod1 = give("wmod1", halves(a["L1_wmod"]))
    args.w0 = give("w0", halves(_np.concatenate([a["L0_attn_wq"].T, a["L0_attn_wk"].T, a["L0_attn_wv"].T,
                                                 a["L0_attn_wo"].T], axis=1)))
    w1 = halves(_np.concatenate([a["L1_attn_Wq"], a["L1_attn_Wk"], a["L1_attn_Wv"]], axis=1)).reshape(128, -1)
    args.w1 = give("w1", _np.concatenate([w1, halves(a["L1_attn_Wo"]).reshape(128, -1)], axis=1))
    args.gate_w = give("gate_w", halves(a["L0_ffn_gate_w"].T))
    args.moe_w = give("moe_w", tiles(a["L0_ffn_w_gate"].reshape(-1, 256), a["L0_ffn_w_up"].reshape(-1, 256),
                                     a["L0_ffn_w_down"].transpose(0, 2, 1).reshape(-1, 256)))
    gate_up = a["L1_ffn_w_gate_up"]
    args.ffn_w = give("ffn_w", tiles(gate_up[0:1024], gate_up[1024:2048], a["L1_ffn_w_down"].T))
    args.gn = give("gn", _np.concatenate([a["L1_attn_gn_w"].reshape(4, 128).T, a["L1_attn_gn_b"].reshape(4, 128).T],
                                         axis=1))
    lam = _np.stack([a["L1_attn_lambda_q1"], a["L1_attn_lambda_k1"], a["L1_attn_lambda_q2"], a["L1_attn_lambda_k2"]])
    args.lam = give("lam", _np.broadcast_to(lam[None], (128, 4, 16)))
    args.consts = give("consts", consts)
    args.expert_of = give("expert_of", which)
    args.out = nc.dram_tensor("out", (8, 256, 256), _mybir.dt.float32, kind="ExternalOutput").ap()
    program(nc, args)
    r = _run(nc, [arrays], core_ids=[0])
    return r.results[0]["out"]
```
